# Optimizing a Trainium2 kernel written in Bass

```python
import numpy as np
import jax
import jax.numpy as jnp

def _softmax(x, axis=-1):
    return jax.nn.softmax(x, axis=axis)

def _gelu(x):
    return jax.nn.gelu(x, approximate=True)

def _silu(x):
    return jax.nn.silu(x)

def _sigmoid(x):
    return jax.nn.sigmoid(x)

def _layernorm(x, axis=-1, eps=1e-05):
    m = jnp.mean(x, axis=axis, keepdims=True)
    v = jnp.var(x, axis=axis, keepdims=True)
    return (x - m) / jnp.sqrt(v + eps)

def _scatter_add(tgt, idx, src, axis=0):
    return tgt.at[idx].add(src)

def _segment_sum(src, seg, n):
    return jax.ops.segment_sum(src, seg, n)
kernel_name = 'mk_macaron_d2_jaxref_r8_b19262'

def setup_inputs(seed: int=0):
    np.random.seed(seed)
    _w = jnp.asarray

    def _L0_attn_setup():
        import jax, jax.numpy as jnp
        import numpy as np
        H = 256
        Q_RANK = 32
        SCALE = float(np.sqrt(Q_RANK))
        key = jax.random.key(seed)
        k_x, k_s, k_a, k_o, k_b = jax.random.split(key, 5)
        B, L = (4, 512)
        x = jax.random.normal(k_x, (B, L, H), dtype=jnp.float32)
        Ws = jax.random.normal(k_s, (H, Q_RANK), dtype=jnp.float32) / np.sqrt(H)
        Wa = jax.random.normal(k_a, (H, Q_RANK), dtype=jnp.float32) / np.sqrt(H)
        Wo = jax.random.normal(k_o, (H, H), dtype=jnp.float32) / np.sqrt(H)
        bo = jax.random.normal(k_b, (H,), dtype=jnp.float32) * 0.01
        return {'x': x, 'Ws': Ws, 'Wa': Wa, 'Wo': Wo, 'bo': bo}
    _L0_attn_in = _L0_attn_setup()

    def _L0_ffn_setup():
        import jax, jax.numpy as jnp
        import numpy as np
        B, S, H = (1, 256, 256)
        E, K, I = (16, 4, 176)
        IS = 352
        CAP = 128
        key = jax.random.key(seed)
        ks = jax.random.split(key, 8)
        sc = 0.02
        return {'hidden_states': jax.random.normal(ks[0], (B, S, H), jnp.float32), 'gate_w': jax.random.normal(ks[1], (E, H), jnp.float32) * sc, 'w_gate': jax.random.normal(ks[2], (E, H, I), jnp.float32) * sc, 'w_up': jax.random.normal(ks[3], (E, H, I), jnp.float32) * sc, 'w_down': jax.random.normal(ks[4], (E, I, H), jnp.float32) * sc, 'sw_gate': jax.random.normal(ks[5], (H, IS), jnp.float32) * sc, 'sw_up': jax.random.normal(ks[6], (H, IS), jnp.float32) * sc, 'sw_down': jax.random.normal(ks[7], (IS, H), jnp.float32) * sc}
    _L0_ffn_in = _L0_ffn_setup()

    def _L1_attn_setup():
        import jax, jax.numpy as jnp
        import numpy as np
        DIM = 256
        NUM_HEADS = 16
        HEAD_DIM = 128
        T_LEN = 256
        W_MAX = 1.0

        def _init_linear(key, out_f, in_f):
            std = 0.5 * in_f ** (-0.5)
            bound = 3.0 ** 0.5 * std
            return jax.random.uniform(key, (out_f, in_f), jnp.float32, -bound, bound)

        def _rope_tables(T, dh, dtype):
            af = (1.0 / 1024.0) ** jnp.linspace(0.0, 1.0, dh // 4, dtype=jnp.float32)
            af = jnp.concatenate([af, jnp.zeros(dh // 4, jnp.float32)])
            theta = jnp.arange(T, dtype=jnp.float32)[:, None] * af[None, :]
            return (jnp.cos(theta), jnp.sin(theta))

        def _apply_rope(x_BTHD, cos, sin):
            x = x_BTHD.astype(jnp.float32)
            x1, x2 = jnp.split(x, 2, axis=-1)
            c = cos[None, :, None, :]
            s = sin[None, :, None, :]
            y1 = x1 * c + x2 * s
            y2 = -x1 * s + x2 * c
            return jnp.concatenate([y1, y2], axis=-1).astype(x_BTHD.dtype)
        key = jax.random.key(seed)
        kx, kq, kk, kv, ko = jax.random.split(key, 5)
        hdim = NUM_HEADS * HEAD_DIM
        return {'x': jax.random.normal(kx, (1, T_LEN, DIM), jnp.float32), 'Wq': _init_linear(kq, hdim, DIM), 'Wk': _init_linear(kk, hdim, DIM), 'Wv': _init_linear(kv, hdim, DIM), 'Wo': _init_linear(ko, DIM, hdim)}
    _L1_attn_in = _L1_attn_setup()

    def _L1_ffn_setup():
        import jax, jax.numpy as jnp
        import numpy as np
        HIDDEN = 256
        INTER = 704
        B, S = (2, 256)

        def _ternary(key, shape):
            return jax.random.randint(key, shape, -1, 2).astype(jnp.float32)
        key = jax.random.key(seed)
        ks = jax.random.split(key, 7)
        x = jax.random.normal(ks[0], (B, S, HIDDEN), dtype=jnp.float32)
        gate_w = _ternary(ks[1], (INTER, HIDDEN))
        up_w = _ternary(ks[2], (INTER, HIDDEN))
        down_w = _ternary(ks[3], (HIDDEN, INTER))
        gate_s = jax.random.uniform(ks[4], (INTER,), minval=0.01, maxval=0.1, dtype=jnp.float32)
        up_s = jax.random.uniform(ks[5], (INTER,), minval=0.01, maxval=0.1, dtype=jnp.float32)
        down_s = jax.random.uniform(ks[6], (HIDDEN,), minval=0.01, maxval=0.1, dtype=jnp.float32)
        return {'x': x, 'gate_w': gate_w, 'up_w': up_w, 'down_w': down_w, 'gate_s': gate_s, 'up_s': up_s, 'down_s': down_s}
    _L1_ffn_in = _L1_ffn_setup()
    _d = {'L0_attn_x': _L0_attn_in['x'], 'L0_attn_Ws': _L0_attn_in['Ws'], 'L0_attn_Wa': _L0_attn_in['Wa'], 'L0_attn_Wo': _L0_attn_in['Wo'], 'L0_attn_bo': _L0_attn_in['bo'], 'L0_ffn_gate_w': _L0_ffn_in['gate_w'], 'L0_ffn_w_gate': _L0_ffn_in['w_gate'], 'L0_ffn_w_up': _L0_ffn_in['w_up'], 'L0_ffn_w_down': _L0_ffn_in['w_down'], 'L0_ffn_sw_gate': _L0_ffn_in['sw_gate'], 'L0_ffn_sw_up': _L0_ffn_in['sw_up'], 'L0_ffn_sw_down': _L0_ffn_in['sw_down'], 'L1_attn_Wq': _L1_attn_in['Wq'], 'L1_attn_Wk': _L1_attn_in['Wk'], 'L1_attn_Wv': _L1_attn_in['Wv'], 'L1_attn_Wo': _L1_attn_in['Wo'], 'L1_ffn_gate_w': _L1_ffn_in['gate_w'], 'L1_ffn_up_w': _L1_ffn_in['up_w'], 'L1_ffn_down_w': _L1_ffn_in['down_w'], 'L1_ffn_gate_s': _L1_ffn_in['gate_s'], 'L1_ffn_up_s': _L1_ffn_in['up_s'], 'L1_ffn_down_s': _L1_ffn_in['down_s']}
    _x0 = _d['L0_attn_x']
    _d['L0_attn_x'] = jax.random.normal(jax.random.fold_in(jax.random.key(seed), 1), (1, 2048, 256), dtype=_x0.dtype)
    del _x0
    return _d

def reference(L0_attn_x, L0_attn_Ws, L0_attn_Wa, L0_attn_Wo, L0_attn_bo, L0_ffn_gate_w, L0_ffn_w_gate, L0_ffn_w_up, L0_ffn_w_down, L0_ffn_sw_gate, L0_ffn_sw_up, L0_ffn_sw_down, L1_attn_Wq, L1_attn_Wk, L1_attn_Wv, L1_attn_Wo, L1_ffn_gate_w, L1_ffn_up_w, L1_ffn_down_w, L1_ffn_gate_s, L1_ffn_up_s, L1_ffn_down_s):

    def _L0_attn_ref(x, Ws, Wa, Wo, bo):
        import jax, jax.numpy as jnp
        import numpy as np
        H = 256
        Q_RANK = 32
        SCALE = float(np.sqrt(Q_RANK))
        B, L, _ = x.shape
        state = jnp.einsum('blh,hr->blr', x, Ws)
        action = jnp.einsum('blh,hr->blr', x, Wa)
        q_values = jnp.einsum('bir,bjr->bij', state, action) / SCALE
        causal = jnp.tril(jnp.ones((L, L), dtype=bool))
        q_values = jnp.where(causal, q_values, -jnp.inf)
        weights = jax.nn.softmax(q_values, axis=-1)
        out = jnp.einsum('bij,bjh->bih', weights, x)
        return jnp.einsum('bih,ho->bio', out, Wo.T) + bo

    def _L0_ffn_ref(hidden_states, gate_w, w_gate, w_up, w_down, sw_gate, sw_up, sw_down):
        import jax, jax.numpy as jnp
        import numpy as np
        B, S, H = (1, 256, 256)
        E, K, I = (16, 4, 176)
        IS = 352
        CAP = 128
        b, s, h = hidden_states.shape
        x = hidden_states.reshape(-1, h)
        T = x.shape[0]
        scores = jax.nn.softmax(x @ gate_w.T, axis=-1)
        topk_w, topk_i = jax.lax.top_k(scores, K)
        topk_w = topk_w / (topk_w.sum(-1, keepdims=True) + 1e-20)
        flat_i = topk_i.reshape(-1)
        flat_w = topk_w.reshape(-1)
        order = jnp.argsort(flat_i)
        se = flat_i[order]
        counts = jax.ops.segment_sum(jnp.ones_like(flat_i), flat_i, num_segments=E)
        starts = jnp.cumsum(counts) - counts
        rank = jnp.arange(T * K) - starts[se]
        tok = order // K
        slot = jnp.where(rank < CAP, rank, CAP)
        buf = jnp.full((E, CAP + 1), T, dtype=jnp.int32).at[se, slot].set(tok)[:, :CAP]
        wbuf = jnp.zeros((E, CAP + 1), x.dtype).at[se, slot].set(flat_w[order])[:, :CAP]
        xpad = jnp.concatenate([x, jnp.zeros((1, h), x.dtype)], axis=0)
        xg = xpad[buf]
        gact = jax.nn.silu(jnp.einsum('ech,ehi->eci', xg, w_gate))
        mid = gact * jnp.einsum('ech,ehi->eci', xg, w_up)
        eout = jnp.einsum('eci,eih->ech', mid, w_down) * wbuf[..., None]
        y = jnp.zeros((T + 1, h), x.dtype).at[buf.reshape(-1)].add(eout.reshape(-1, h))[:T]
        shared = jax.nn.silu(x @ sw_gate) * (x @ sw_up) @ sw_down
        return (y + shared).reshape(b, s, h)

    def _L1_attn_ref(x, Wq, Wk, Wv, Wo):
        import jax, jax.numpy as jnp
        import numpy as np
        DIM = 256
        NUM_HEADS = 16
        HEAD_DIM = 128
        T_LEN = 256
        W_MAX = 1.0

        def _init_linear(key, out_f, in_f):
            std = 0.5 * in_f ** (-0.5)
            bound = 3.0 ** 0.5 * std
            return jax.random.uniform(key, (out_f, in_f), jnp.float32, -bound, bound)

        def _rope_tables(T, dh, dtype):
            af = (1.0 / 1024.0) ** jnp.linspace(0.0, 1.0, dh // 4, dtype=jnp.float32)
            af = jnp.concatenate([af, jnp.zeros(dh // 4, jnp.float32)])
            theta = jnp.arange(T, dtype=jnp.float32)[:, None] * af[None, :]
            return (jnp.cos(theta), jnp.sin(theta))

        def _apply_rope(x_BTHD, cos, sin):
            x = x_BTHD.astype(jnp.float32)
            x1, x2 = jnp.split(x, 2, axis=-1)
            c = cos[None, :, None, :]
            s = sin[None, :, None, :]
            y1 = x1 * c + x2 * s
            y2 = -x1 * s + x2 * c
            return jnp.concatenate([y1, y2], axis=-1).astype(x_BTHD.dtype)
        B, T, _ = x.shape
        H, Dh = (NUM_HEADS, HEAD_DIM)
        scale = Dh ** 0.5 / W_MAX ** 2 / Dh
        q = (x @ Wq.T).reshape(B, T, H, Dh)
        k = (x @ Wk.T).reshape(B, T, H, Dh)
        v = (x @ Wv.T).reshape(B, T, H, Dh)
        cos, sin = _rope_tables(T, Dh, x.dtype)
        q = _apply_rope(q, cos, sin)
        k = _apply_rope(k, cos, sin)
        scores = jnp.einsum('bthd,bshd->bhts', q, k) * scale
        causal = jnp.tril(jnp.ones((T, T), bool))
        scores = jnp.where(causal[None, None], scores, -jnp.inf)
        attn = jax.nn.softmax(scores, axis=-1)
        y = jnp.einsum('bhts,bshd->bthd', attn, v).reshape(B, T, H * Dh)
        return y / 3.0 @ Wo.T

    def _L1_ffn_ref(x, gate_w, up_w, down_w, gate_s, up_s, down_s):
        import jax, jax.numpy as jnp
        import numpy as np
        HIDDEN = 256
        INTER = 704
        B, S = (2, 256)

        def _ternary(key, shape):
            return jax.random.randint(key, shape, -1, 2).astype(jnp.float32)
        b, s, h = x.shape
        xf = x.reshape(b * s, h)
        g = jnp.einsum('th,ih->ti', xf, gate_w) * gate_s
        u = jnp.einsum('th,ih->ti', xf, up_w) * up_s
        hdn = jax.nn.silu(g) * u
        out = jnp.einsum('ti,hi->th', hdn, down_w) * down_s
        return out.reshape(b, s, -1)
    x = L0_attn_x
    x = x + 0.5 * _L0_ffn_ref(_layernorm(x, axis=-1), L0_ffn_gate_w, L0_ffn_w_gate, L0_ffn_w_up, L0_ffn_w_down, L0_ffn_sw_gate, L0_ffn_sw_up, L0_ffn_sw_down)
    x = x + _L0_attn_ref(_layernorm(x, axis=-1), L0_attn_Ws, L0_attn_Wa, L0_attn_Wo, L0_attn_bo)
    x = x + 0.5 * _L0_ffn_ref(_layernorm(x, axis=-1), L0_ffn_gate_w, L0_ffn_w_gate, L0_ffn_w_up, L0_ffn_w_down, L0_ffn_sw_gate, L0_ffn_sw_up, L0_ffn_sw_down)
    x = x + 0.5 * _L1_ffn_ref(_layernorm(x, axis=-1), L1_ffn_gate_w, L1_ffn_up_w, L1_ffn_down_w, L1_ffn_gate_s, L1_ffn_up_s, L1_ffn_down_s)
    x = x + _L1_attn_ref(_layernorm(x, axis=-1), L1_attn_Wq, L1_attn_Wk, L1_attn_Wv, L1_attn_Wo)
    x = x + 0.5 * _L1_ffn_ref(_layernorm(x, axis=-1), L1_ffn_gate_w, L1_ffn_up_w, L1_ffn_down_w, L1_ffn_gate_s, L1_ffn_up_s, L1_ffn_down_s)
    return x

_drawn_inputs = setup_inputs


def setup_inputs(seed=0):
    import zlib

    import numpy as np

    out = dict(_drawn_inputs(seed))
    spreads = {}
    factors = {'L0_attn_bo': 5.252,
     'L0_ffn_gate_w': 8.0,
     'L0_ffn_w_gate': 8.0,
     'L0_ffn_w_up': 8.0,
     'L0_ffn_w_down': 8.0,
     'L1_attn_Wq': 8.0,
     'L1_attn_Wk': 8.0,
     'L1_attn_Wv': 7.71,
     'L1_attn_Wo': 7.697}
    for name, (base, spread) in spreads.items():
        noise = np.random.default_rng([zlib.crc32(name.encode()), seed]).standard_normal(out[name].shape)
        drawn = base * np.exp(spread * noise) if base else spread * noise
        out[name] = jnp.asarray(drawn.astype(out[name].dtype))
    for name, factor in factors.items():
        out[name] = (out[name] * factor).astype(out[name].dtype)
    return out
```

```python
from contextlib import ExitStack

import numpy as np

import concourse.bass as bass
from concourse import mybir
from concourse.alu_op_type import AluOpType as ALU

F32 = mybir.dt.float32
F32R = mybir.dt.float32r
BF16 = mybir.dt.bfloat16
I32 = mybir.dt.int32
U32 = mybir.dt.uint32
ACT = mybir.ActivationFunctionType
AX = mybir.AxisListType

P = 128
H = 256
HK = H // P
T = 2048
NT = T // P
CH = 512
NCH = T // CH
BANK = 512
EPS = 1e-5

NE, TOPK, CAP = 16, 4, 128
I0 = 176
I0P = 256
IS = 352
ISM = 3
TRASH = T

R0 = 32
NH, DH = 16, 128
I1 = 704
I1M = 6
CREDIT = 1024
NEG = -1e30


class Flow:

    def __init__(self, sem, step):
        self.sem, self.step, self.before, self.per = sem, step, {}, {}
        self.total = 0


class Tick:

    def __init__(self, section, flow, k):
        self.section, self.flow, self.k = section, flow, k


class Section:

    def __init__(self, times):
        self.times, self.items, self.named = times, {}, {}


class Queues:

    ENGINES = ("pe", "act", "dve", "pool", "sp")

    def __init__(self, nc, stack):
        self.nc, self.stack = nc, stack
        self.own = {e: self.flow(f"done_{e}", 1) for e in self.ENGINES}
        self.waited = self.flow("waited", 1)
        self.sections, self.section = [], None

    def flow(self, name, step):
        return Flow(self.stack.enter_context(self.nc.semaphore(name)), step)

    def credit(self, flow):
        flow.total += CREDIT
        return Flow(flow.sem, CREDIT)

    def begin(self, times=1):
        self.section = Section(times)
        self.sections.append(self.section)
        self.seen = {}

    def op(self, engine, fn, flow=None, tick=True, name=None):
        if not tick:
            self.section.items.setdefault(engine, []).append((fn, None))
            return None
        flow = flow or self.own[engine]
        k = flow.per.get(self.section, 0) + flow.step
        flow.per[self.section] = k
        self.section.items.setdefault(engine, []).append((fn, flow))
        t = Tick(self.section, flow, k)
        if name is not None:
            self.section.named[name] = t
        return t

    def last(self, engine):
        flow = self.own[engine]
        return Tick(self.section, flow, flow.per.get(self.section, 0))

    def wait(self, engine, *ticks):
        for t in ticks:
            if t is None:
                continue
            key = (engine, t.flow)
            old = self.seen.get(key)
            if old is not None and old[0] is t.section and old[1] >= t.k:
                continue
            self.seen[key] = (t.section, t.k)
            self.section.items.setdefault(engine, []).append((t, None))

    def wait_before(self, engine, name):
        self.section.items.setdefault(engine, []).append((name, -1))

    def release(self, name, tick):
        self.section.named[name] = tick

    def acquire(self, engine, name):
        if name in self.section.named:
            self.wait(engine, self.section.named[name])
        elif self.section.times > 1:
            self.wait_before(engine, name)
        elif len(self.sections) > 1 and name in self.sections[-2].named:
            self.wait(engine, self.sections[-2].named[name])

    def meet(self):
        for e in self.ENGINES:
            self.wait(e, *(self.last(other) for other in ("pe", "act", "dve", "pool") if self.own[other].per.get(self.section)))

    def wait_turn(self, engine, tick, turn):
        self.section.items.setdefault(engine, []).append((tick, turn))

    def chain(self, engine, fn, **kw):
        self.wait(engine, self.last(engine))
        return self.op(engine, fn, **kw)

    def emit(self):
        nc = self.nc
        for s in self.sections:
            for f in {t for e in s.items.values() for _, t in e if isinstance(t, Flow)}:
                f.before[s] = f.total
                f.total += s.times * f.per[s]

        def run(engine, name):
            for s in self.sections:
                items = s.items.get(name)
                if not items:
                    continue

                def body(i):
                    for what, extra in items:
                        if isinstance(what, Tick):
                            f = what.flow
                            turn = extra if extra is not None else i if what.section is s else what.section.times - 1
                            engine.wait_ge(f.sem, turn * f.per[what.section] + f.before[what.section] + what.k)
                        elif extra == -1:
                            t = s.named[what]
                            f = t.flow
                            engine.wait_ge(f.sem, i * f.per[s] + f.before[s] + t.k - f.per[s])
                        else:
                            ins = what(engine, i)
                            if extra is not None:
                                ins.then_inc(extra.sem, extra.step)
                        if not callable(what) and name == "sp" and s.times > 1:
                            engine.sem_inc(self.waited.sem, 1)

                if s.times == 1:
                    body(0)
                else:
                    with engine.Fori(0, s.times) as i:
                        body(i)

        with nc.Block() as block:
            block.tensor(lambda eng: run(eng, "pe"))
            block.scalar(lambda eng: run(eng, "act"))
            block.vector(lambda eng: run(eng, "dve"))
            block.gpsimd(lambda eng: run(eng, "pool"))
            block.sync(lambda eng: run(eng, "sp"))
        self.sections = []


def cols(ap, start, n):
    return ap[:, bass.ds(start, n)]


def as_f32(ap):
    return ap.bitcast(F32)


class Core:

    def __init__(self, nc, stack, q, src):
        self.nc, self.q, self.src, self.phase = nc, q, src, 0
        sb = lambda name, shape, dt: stack.enter_context(nc.sbuf_tensor("sb_" + name, shape, dt))
        self.x = sb("x", [P, NT, H], F32)
        self.xt_hi = sb("xt_hi", [P, HK, T], F32R)
        self.xt_lo = sb("xt_lo", [P, HK, T], F32R)
        self.ident = sb("ident", [P, P], F32)
        self.ident_b = sb("ident_b", [P, P], BF16)
        self.mask_b = sb("mask_b", [P, P], BF16)
        self.loads = [q.flow(f"load_{n}", 16) for n in range(24)]
        self.gather_out = [q.flow(f"gather_{n}", 16) for n in range(NE)]
        self.add_out = [q.flow(f"add_{n}", 16) for n in range(2)]
        self.xn_rows = nc.dram_tensor("xn_rows", (T + CAP, H), F32).ap()
        self.y_rows = nc.dram_tensor("y_rows", (T + CAP, H), F32).ap()


    def rooms(self, stack):
        self.phase += 1
        tag = f"phase{self.phase}_"
        return (lambda name, shape, dt=F32: stack.enter_context(self.nc.sbuf_tensor(tag + name, shape, dt)),
                lambda name, shape, dt=F32: stack.enter_context(self.nc.psum_tensor(tag + name, shape, dt)))


def load(core, n, out, src):
    return core.q.op("sp", lambda e, i: e.dma_start(out, src), flow=core.loads[n])


def split(q, hi_engine, lo_engine, hi, lo, value, ready, scale=None):
    q.wait(hi_engine, ready)
    if hi_engine == "act":
        t = q.op("act", lambda e, i: e.activation(hi, value, ACT.Copy, scale=1.0 if scale is None else scale))
    elif scale is None:
        t = q.op(hi_engine, lambda e, i: e.tensor_copy(hi, value))
    else:
        t = q.op(hi_engine, lambda e, i: e.tensor_scalar(hi, value, scale, None, ALU.mult))
    q.wait(lo_engine, ready, t)
    if scale is None:
        return q.op(lo_engine, lambda e, i: e.tensor_tensor(lo, value, as_f32(hi), ALU.subtract))
    return q.op(lo_engine, lambda e, i: e.scalar_tensor_tensor(lo, value, scale, as_f32(hi), ALU.mult, ALU.subtract))


def products(q, out, left_hi, left_lo, rights, first=True, last=True):
    n = len(rights)
    for c, (r_hi, r_lo) in enumerate(rights):
        for p, (a, b) in enumerate(((left_hi[c], r_hi), (left_hi[c], r_lo), (left_lo[c], r_hi))):
            s, e = first and c == 0 and p == 0, last and c == n - 1 and p == 2
            t = q.op("pe", (lambda a, b, s, e: lambda eng, i: eng.matmul(
                out(i) if callable(out) else out, a, b(i) if callable(b) else b, start=s, stop=e))(a, b, s, e),
                tick=c == n - 1 and p == 2)
    return t


def start_phase(core):
    q, c, src = core.q, core, core.src
    q.begin()
    done = [load(core, 0, c.x[:], src["x"].rearrange("(t p) h -> p t h", p=P)),
            load(core, 1, c.ident[:], src["ident"]),
            load(core, 2, c.ident_b[:], src["ident_b"]),
            load(core, 3, c.mask_b[:], src["mask_b"])]
    q.wait("sp", *done)
    for engine, flow in q.own.items():
        q.op(engine, lambda e, i: e.nop(), flow=q.credit(flow))
    q.emit()


def layernorm_phase(core, add_y=False, keep_rows=False):
    q, nc = core.q, core.nc
    with ExitStack() as stack:
        sb, psum = core.rooms(stack)
        ps = psum("ps", [P, 4, BANK])
        xn = sb("ln_xn", [P, NT, H])
        stats = sb("ln_stats", [P, NT, 6])
        mv = sb("ln_mv", [P, NT, 2])
        var, root, rstd, tmp = (sb(f"ln_{n}", [P, NT]) for n in ("var", "root", "rstd", "tmp"))
        q.begin()
        if add_y:
            yb = sb("ln_y", [P, NT, H])
            rows = core.y_rows[0:T, :].rearrange("(t p) h -> p t h", p=P)
            for c in range(4):
                here = yb[:, 4 * c:4 * c + 4, :], core.x[:, 4 * c:4 * c + 4, :]
                t = load(core, c, here[0], rows[:, 4 * c:4 * c + 4, :])
                q.wait("dve", t)
                t = q.op("dve", lambda e, i, h=here: e.tensor_tensor(h[1], h[1], h[0], ALU.add))
            q.wait("dve", t)
        for t in range(NT):
            last = q.op("dve", lambda e, i, t=t: e.bn_stats(stats[:, t, :], core.x[:, t, :]))
        q.wait("dve", last)
        for t in range(NT):
            q.op("dve", lambda e, i, t=t: e.bn_aggr(mv[:, t, :], stats[:, t, :]))
        ready = q.chain("dve", lambda e, i: e.tensor_scalar(var[:], mv[:, :, 1], EPS, None, ALU.add))
        q.wait("act", ready)
        ready = q.op("act", lambda e, i: e.activation(root[:], var[:], ACT.Sqrt))
        q.wait("dve", ready)
        q.op("dve", lambda e, i: e.reciprocal(rstd[:], root[:]))
        q.chain("dve", lambda e, i: e.tensor_tensor(tmp[:], rstd[:], rstd[:], ALU.mult))
        q.chain("dve", lambda e, i: e.tensor_tensor(tmp[:], tmp[:], var[:], ALU.mult))
        q.chain("dve", lambda e, i: e.tensor_scalar(tmp[:], tmp[:], -0.5, 1.5, ALU.mult, ALU.add))
        q.chain("dve", lambda e, i: e.tensor_tensor(rstd[:], rstd[:], tmp[:], ALU.mult))
        q.wait("dve", q.last("dve"))
        normed = [q.op("dve", lambda e, i, t=t: e.tensor_scalar(
            xn[:, t, :], core.x[:, t, :], mv[:, t, 0:1], rstd[:, t:t + 1], ALU.subtract, ALU.mult)) for t in range(NT)]
        freed = []
        for c in range(NCH):
            for k in range(HK):
                b = (HK * c + k) % 4
                if len(freed) >= 4:
                    q.wait("pe", freed[-4])
                q.wait("pe", normed[4 * c + 3])
                for j in range(4):
                    done = q.op("pe", lambda e, i, c=c, k=k, b=b, j=j: e.transpose(
                        ps[:, b, j * P:(j + 1) * P], xn[:, 4 * c + j, k * P:(k + 1) * P], core.ident[:]), tick=j == 3)
                where = slice(c * CH, (c + 1) * CH)
                freed.append(split(q, "act", "dve", core.xt_hi[:, k, where], core.xt_lo[:, k, where], ps[:, b, :], done))
        if keep_rows:
            for c in range(4):
                q.wait("sp", normed[4 * c + 3])
                t = load(core, 4 + c, core.xn_rows[0:T, :].rearrange("(t p) h -> p t h", p=P)[:, 4 * c:4 * c + 4, :],
                         xn[:, 4 * c:4 * c + 4, :])
                q.wait("sp", t)
        q.emit()


def ffn_phase(core, up_src, down_src, width, scales=None, extra=None):
    q, nc, merged = core.q, core.nc, scales is not None
    pairs = width // P if merged else -(-width // P)
    pieces = pairs + merged
    n_up = (2 * pairs + merged) * P
    with ExitStack() as stack:
        sb, psum = core.rooms(stack)
        ps = psum("ps", [P, 8, BANK])
        up_hi, up_lo = (sb(n, [P, HK, n_up], F32R) for n in ("up_hi", "up_lo"))
        dn_hi, dn_lo = (sb(n, [P, pieces, H], F32R) for n in ("dn_hi", "dn_lo"))
        raw_up, raw_dn = sb("raw_up", [P, HK, n_up]), sb("raw_dn", [P, pieces, H])
        h_hi, h_lo = (sb(n, [P, pieces, CH], F32R) for n in ("h_hi", "h_lo"))
        gate, act = sb("gate", [P, 2, CH]), sb("act", [P, 2, CH])
        q.begin()
        if extra:
            extra(stack)
        ready = []
        for k in range(HK):
            t = load(core, k, raw_up[:, k, :], up_src[:, k, :])
            ready.append(split(q, "act", "dve", up_hi[:, k, :], up_lo[:, k, :], raw_up[:, k, :], t))
        t = load(core, 2, raw_dn[:], down_src)
        ready.append(split(q, "act", "pool", dn_hi[:], dn_lo[:], raw_dn[:], t))
        if merged:
            gs, us, ds = sb("gs", [P, pieces]), sb("us", [P, pieces]), sb("ds", [P, H])
            s_t = [load(core, 3, gs[:], scales[0]), load(core, 4, us[:], scales[1]),
                   load(core, 5, ds[:], scales[2].partition_broadcast(P))]
            q.wait("dve", *s_t)
            q.wait("act", *s_t)
            ready.append(q.op("dve", lambda e, i: e.tensor_scalar(ds[:], ds[:], 0.5, None, ALU.mult)))
            ready.append(q.chain("pool", lambda e, i: e.memset(as_f32(h_hi[64:P, pieces - 1, :]), 0.0)))
            ready.append(q.op("pool", lambda e, i: e.memset(as_f32(h_lo[64:P, pieces - 1, :]), 0.0)))
            tmp = sb("tmp", [P, 2, H])

        q.wait("pe", *ready)
        q.wait("dve", *ready)
        q.begin(NCH)
        xt = lambda src, k: (lambda i: src[:, k, bass.ds(i * CH, CH)])
        rights = [(xt(core.xt_hi, k), xt(core.xt_lo, k)) for k in range(HK)]
        split_h = []
        acted = []
        for m in range(pieces):
            half = merged and m == pieces - 1
            rows = slice(0, 64) if half else slice(0, P)
            banks = (m % 2, 2 + m % 2)
            if m >= 2:
                q.wait("pe", acted[m - 2])
            else:
                q.wait_before("pe", ("act", pieces - 1))
            for n, bank in enumerate(banks[:1] if half else banks):
                at = (2 * m + n) * P
                done = products(q, ps[:, bank, :], [up_hi[:, k, at:at + P] for k in range(HK)],
                                [up_lo[:, k, at:at + P] for k in range(HK)], rights)
            g = ps[rows, banks[0], :]
            u = ps[64:P, banks[0], :] if half else ps[:, banks[1], :]
            q.wait("act", done)
            if m >= 2:
                q.wait("act", acted[m - 2])
            else:
                q.wait_before("act", ("act", pieces - 1))
            g_t = q.op("act", lambda e, i, g=g, m=m, rows=rows: e.activation(
                gate[rows, m % 2, :], g, ACT.Silu, scale=gs[rows, m:m + 1] if merged else 1.0))
            q.wait("dve", g_t)
            if m >= 2:
                q.wait("dve", split_h[m - 2])
            else:
                q.wait_before("dve", ("split", pieces - 1))
            urow = slice(64, P) if half else slice(0, P)
            acted.append(q.op("dve", lambda e, i, u=u, m=m, rows=rows, urow=urow: e.scalar_tensor_tensor(
                act[rows, m % 2, :], u, us[urow, m:m + 1] if merged else 1.0, gate[rows, m % 2, :], ALU.mult, ALU.mult),
                name=("act", m)))
            q.wait("pool", q.last("pool")) if m else q.wait_before("pool", ("split", pieces - 1))
            q.wait_before("act", ("down", pieces - 1))
            q.wait_before("pool", ("down", pieces - 1))
            s = split(q, "act", "pool", h_hi[rows, m, :], h_lo[rows, m, :], act[rows, m % 2, :], acted[-1])
            q.section.named[("split", m)] = s
            split_h.append(s)
        q.wait_before("pe", "added")
        for m in range(pieces):
            q.wait("pe", split_h[m])
            for j in range(4):
                t = products(q, ps[:, 4 + j, 0:H], [h_hi[:, m, j * P:(j + 1) * P]], [h_lo[:, m, j * P:(j + 1) * P]],
                             [(dn_hi[:, m, :], dn_lo[:, m, :])], first=m == 0, last=m == pieces - 1)
            q.section.named[("down", m)] = t
        for j in range(4):
            q.wait("dve", t)
            row = lambda i, j=j: core.x[:, bass.ds(i * 4 + j, 1), :].rearrange("p a h -> p (a h)")
            if merged:
                q.wait("dve", q.last("dve"))
                q.op("dve", lambda e, i, j=j: e.tensor_tensor(tmp[:, j % 2, :], ps[:, 4 + j, 0:H], ds[:], ALU.mult))
                q.chain("dve", lambda e, i, j=j, row=row: e.tensor_tensor(row(i), row(i), tmp[:, j % 2, :], ALU.add), name="added")
            else:
                q.op("dve", lambda e, i, j=j, row=row: e.scalar_tensor_tensor(
                    row(i), ps[:, 4 + j, 0:H], 0.5, row(i), ALU.mult, ALU.add), name="added")
        q.emit()


class Attention:

    def __init__(self, core, stack):
        self.core, self.q = core, core.q
        sb, psum = core.rooms(stack)
        self.sb = sb
        self.scores = psum("scores", [P, 4 * BANK])
        self.turned = psum("turned", [P, 2, BANK])
        self.y = psum("y", [P, BANK])
        self.misc = psum("misc", [P, BANK])
        self.p = sb("p", [P, T])
        self.pt_hi, self.pt_lo = ([sb(f"pt_{n}{b}", [P, NT - 2 * (b == 0), 2 * P], F32R) for b in range(2)] for n in ("hi", "lo"))
        self.peaks, self.bias = sb("peaks", [P, 2, 4]), sb("bias", [P, 2])
        self.sums, self.total = sb("sums", [P, 2, 2]), sb("total", [P, 2])
        self.inv = sb("inv", [P, 2, NT])
        self.batch = 0

    def qk(self, t, c, pairs, ready):
        q = self.q
        diag = c == t // 4
        n = max(256, (t % 4 + 1) * P) if diag else BANK
        out = self.scores[:, c * BANK:c * BANK + n]
        q.wait("pe", *ready)
        q.acquire("pe", ("scores", c))
        products_ = pairs(n)
        for k, (a, b) in enumerate(products_):
            done = q.op("pe", lambda e, i, a=a, b=b, k=k: e.matmul(
                out, a, b, start=k == 0, stop=k == len(products_) - 1),
                tick=k == len(products_) - 1)
        if diag:
            at = t * P
            done = q.op("pe", lambda e, i: e.matmul(self.scores[:, at:at + P], self.core.ident_b[:], self.core.mask_b[:],
                                                    start=False, stop=True, skip_group_check=True))
        width = (t % 4 + 1) * P if diag else BANK
        q.wait("dve", done)
        q.op("dve", lambda e, i: e.tensor_reduce(self.peaks[:, t % 2, c:c + 1],
                                                 self.scores[:, c * BANK:c * BANK + width], AX.X, ALU.max))

    def exps(self, t, slot):
        q, chunks = self.q, t // 4 + 1
        q.wait("dve", q.last("dve"))
        q.acquire("dve", ("bias", t % 2))
        biased = q.op("dve", lambda e, i: e.tensor_reduce(self.bias[:, t % 2:t % 2 + 1], self.peaks[:, t % 2, 0:chunks],
                                                          AX.X, ALU.max, negate=True))
        q.wait("act", biased)
        parts = [(0, min(2, chunks))] + ([(2, chunks)] if chunks > 2 else [])
        q.acquire("act", ("sums", t % 2))
        for n, (a, b) in enumerate(parts):
            lo, hi = a * BANK, min(b * BANK, (t + 1) * P)
            for c in range(a, b):
                q.acquire("act", ("p", c))
            done = q.op("act", lambda e, i, n=n, lo=lo, hi=hi: e.activation(
                self.p[:, lo:hi], self.scores[:, lo:hi], ACT.Exp, bias=self.bias[:, t % 2:t % 2 + 1],
                accum_out=self.sums[:, t % 2, n:n + 1]))
            for c in range(a, b):
                q.release(("scores", c), done)
                q.release(("p written", c), done)
        q.release(("bias", t % 2), done)
        inv = self.inv[:, slot, t:t + 1]
        q.wait("dve", done)
        q.acquire("dve", ("inv", slot, t))
        if len(parts) == 2:
            q.op("dve", lambda e, i: e.tensor_tensor(inv, self.sums[:, t % 2, 0:1], self.sums[:, t % 2, 1:2], ALU.add))
            done = q.chain("dve", lambda e, i: e.reciprocal(inv, inv))
        else:
            done = q.op("dve", lambda e, i: e.reciprocal(inv, self.sums[:, t % 2, 0:1]))
        q.release(("sums", t % 2), done)
        q.release(("inv", slot, t), done)

    def turn(self, t, b):
        q, n = self.q, min(4, t + 1 - 4 * b)
        bank, self.batch = self.batch % 2, self.batch + 1
        buf = (t // 2) % 2
        q.acquire("pe", ("p written", b))
        q.acquire("pe", ("turned", bank))
        for j in range(n):
            done = q.op("pe", lambda e, i, j=j: e.transpose(
                self.turned[:, bank, j * P:(j + 1) * P], self.p[:, (4 * b + j) * P:(4 * b + j + 1) * P], self.core.ident[:]),
                tick=j == n - 1)
        q.release(("p", b), done)
        where = (slice(None), slice(4 * b, 4 * b + n), slice((t % 2) * P, (t % 2 + 1) * P))
        value = self.turned[:, bank, 0:n * P].rearrange("p (a b) -> p a b", b=P)
        for e in ("act", "dve"):
            q.acquire(e, ("pt", buf, b, t % 2))
        s = split(q, "act", "dve", self.pt_hi[buf][where], self.pt_lo[buf][where], value, done)
        q.release(("turned", bank), s)
        q.release(("pt written", buf, b, t % 2), s)


def values(core, att, g, w_hi, w_lo, v_hi, v_lo, ready):
    q = core.q
    q.wait("pe", *ready)
    q.acquire("pe", "misc")
    for n in range(2):
        t = 2 * g + n
        done = products(q, att.misc[:, n * H:(n + 1) * H], [core.xt_hi[:, k, t * P:(t + 1) * P] for k in range(HK)],
                        [core.xt_lo[:, k, t * P:(t + 1) * P] for k in range(HK)], [(w_hi[:, k, :], w_lo[:, k, :]) for k in range(HK)])
    for e in ("act", "dve"):
        q.acquire(e, ("v", g))
    s = split(q, "act", "dve", v_hi[:, 2 * g:2 * g + 2, :], v_lo[:, 2 * g:2 * g + 2, :],
              att.misc[:].rearrange("p (a b) -> p a b", a=2), done)
    q.release("misc", s)
    q.release(("v written", g), s)


def attention0_phase(core):
    q, nc, src = core.q, core.nc, core.src
    with ExitStack() as stack:
        att = Attention(core, stack)
        sb = att.sb
        raw = {n: sb("raw_" + n, [P, HK, w]) for n, w in (("ws", P), ("wa", P), ("wo0", H))}
        w_hi = {n: sb("hi_" + n, [P, HK, r.shape[2]], F32R) for n, r in raw.items()}
        w_lo = {n: sb("lo_" + n, [P, HK, r.shape[2]], F32R) for n, r in raw.items()}
        bo = sb("bo", [P, H])
        s4, a4 = sb("s4", [P, T], F32R), sb("a4", [P, T], F32R)
        v_hi, v_lo = sb("v_hi", [P, NT, H], F32R), sb("v_lo", [P, NT, H], F32R)
        q.begin()
        ready = {}
        for n, (name, scale) in enumerate((("ws", float(R0) ** -0.5), ("wa", None), ("wo0", None))):
            t = load(core, n, raw[name][:], src[name])
            ready[name] = split(q, "act", "dve", w_hi[name][:], w_lo[name][:], raw[name][:], t, scale)
        t_bo = load(core, 3, bo[:], src["bo"].partition_broadcast(P))
        for c in range(NCH):
            where = slice(c * CH, (c + 1) * CH)
            rights = [(core.xt_hi[:, k, where], core.xt_lo[:, k, where]) for k in range(HK)]
            for name, out, low in (("ws", s4, ((64, 128),)), ("wa", a4, ((32, 64), (96, 128)))):
                bank = att.turned[:, 0 if name == "ws" else 1, :]
                q.wait("pe", ready[name])
                q.acquire("pe", ("turned", name))
                done = products(q, bank, [w_hi[name][:, k, :] for k in range(HK)], [w_lo[name][:, k, :] for k in range(HK)], rights)
                q.wait("act", done)
                done = q.op("act", lambda e, i, out=out, bank=bank, where=where: e.activation(out[:, where], bank, ACT.Copy))
                q.wait("dve", done)
                for a, b in low:
                    done = q.op("dve", lambda e, i, a=a, b=b, out=out, bank=bank, where=where: e.tensor_tensor(
                        out[a:b, where], bank[a:b, :], as_f32(out[a:b, where]), ALU.subtract))
                q.release(("turned", name), done)
        stacked = done
        q.wait("pe", stacked)
        for n in range(2):
            q.release(("turned", n), stacked)

        def scores(t, c):
            att.qk(t, c, lambda n: [(s4[:, t * P:(t + 1) * P], a4[:, c * CH:c * CH + n])], ())

        def pv(t, j):
            buf = (t // 2) % 2
            q.acquire("pe", ("pt written", buf, j // 4, t % 2))
            q.acquire("pe", ("v written", j // 2))
            if j == 0:
                q.acquire("pe", "y")
            cols_ = slice((t % 2) * P, (t % 2 + 1) * P)
            done = products(q, att.y[:, 0:H], [att.pt_hi[buf][:, j, cols_]], [att.pt_lo[buf][:, j, cols_]],
                            [(v_hi[:, j, :], v_lo[:, j, :])], first=j == 0, last=j == t)
            q.release(("pt", buf, j // 4, t % 2), done)
            if j == t:
                q.wait("dve", done)
                q.acquire("dve", ("inv", 0, t))
                done = q.op("dve", lambda e, i: e.scalar_tensor_tensor(
                    core.x[:, t, :], att.y[:, 0:H], att.inv[:, 0, t:t + 1], core.x[:, t, :], ALU.mult, ALU.add))
                q.release("y", done)
                q.chain("dve", lambda e, i: e.tensor_tensor(core.x[:, t, :], core.x[:, t, :], bo[:], ALU.add))

        q.wait("dve", t_bo)
        scores(0, 0)
        att.exps(0, 0)
        for t in range(NT + 1):
            if t < NT and t % 2 == 0:
                values(core, att, t // 2, w_hi["wo0"], w_lo["wo0"], v_hi, v_lo, [ready["wo0"]])
            work = [(t - 1, j) for j in range(t)]
            last_b = (t + 1) // 4 if t + 1 < NT else t // 4
            for b in range(last_b + 1 if t < NT else 0):
                if b <= t // 4:
                    att.turn(t, b)
                if t + 1 < NT and b <= (t + 1) // 4:
                    scores(t + 1, b)
                for _ in range(2):
                    if work:
                        pv(*work.pop(0))
            if t + 1 < NT:
                att.exps(t + 1, 0)
            for w in work:
                pv(*w)
        q.emit()


def attention1_phase(core):
    q, nc, src = core.q, core.nc, core.src
    with ExitStack() as stack:
        att = Attention(core, stack)
        sb = att.sb
        rope = sb("rope", [P, T])
        raw_qk, raw_wv, raw_wo = sb("raw_qk", [P, HK, 2, P]), sb("raw_wv", [P, HK, H]), sb("raw_wo", [P, H])
        qk_hi, qk_lo = (sb(n, [P, HK, 2, P], F32R) for n in ("qk_hi", "qk_lo"))
        wv_hi, wv_lo = (sb(n, [P, HK, H], F32R) for n in ("wv_hi", "wv_lo"))
        wo_hi, wo_lo = (sb(n, [P, H], F32R) for n in ("wo_hi", "wo_lo"))
        k_hi, k_lo = (sb(n, [P, T], F32R) for n in ("k_hi", "k_lo"))
        q_hi, q_lo = (sb(n, [P, 2, 2 * P], F32R) for n in ("q_hi", "q_lo"))
        v_hi, v_lo = (sb(n, [P, NT, 2 * DH], F32R) for n in ("v_hi", "v_lo"))
        y_hi, y_lo = (sb(n, [P, 2 * P], F32R) for n in ("y_hi", "y_lo"))
        straight, crossed, rot = sb("straight", [64, 2, 2 * P]), sb("crossed", [64, 2, 2 * P]), sb("rot", [P, 2, 2 * P])
        G = NT // 2

        def weights(name, n, raw, w_hi, w_lo, pick, scale=None):
            q.acquire("sp", name + " raw")
            t = q.op("sp", lambda e, i: e.dma_start(raw[:], pick(i)), flow=core.loads[n])
            for e in ("act", "dve"):
                q.acquire(e, name)
            s = split(q, "act", "dve", w_hi[:], w_lo[:], raw[:], t, scale)
            q.release(name + " raw", s)
            q.release(name + " split", s)

        def weights_of(slot, ahead):
            head = lambda i: src["qk"][bass.ds(2 * i + slot + 2 * ahead, 1)].rearrange("a p k j d -> p (a k) j d")
            weights("qk", 0, raw_qk, qk_hi, qk_lo, head)
            if slot == 0:
                weights("wv", 1, raw_wv, wv_hi, wv_lo,
                        lambda i: src["wv"][bass.ds(i + ahead, 1)].rearrange("a p k d -> p (a k) d"))

        def project(g, serial):
            cur = serial % 2
            q.acquire("pe", "qk split")
            q.acquire("pe", "misc")
            where = slice(2 * P * g, 2 * P * (g + 1))
            rights = [(core.xt_hi[:, k, where], core.xt_lo[:, k, where]) for k in range(HK)]
            both = att.misc[:].rearrange("p (a b) -> p a b", a=2)
            for j in range(2):
                done = products(q, both[:, j, :], [qk_hi[:, k, j, :] for k in range(HK)], [qk_lo[:, k, j, :] for k in range(HK)], rights)
            q.release("qk", done)
            q.wait("dve", done)
            q.acquire("dve", "crossed")
            wide = lambda rows: rope[rows, where].unsqueeze(1).broadcast_to([rows.stop - rows.start, 2, 2 * P])
            q.op("dve", lambda e, i: e.tensor_tensor(crossed[0:32], both[32:64], wide(slice(96, 128)), ALU.mult))
            t_cross = q.op("dve", lambda e, i: e.tensor_tensor(crossed[32:64], both[0:32], wide(slice(64, 96)), ALU.mult))
            q.wait("act", t_cross)
            q.acquire("act", "rot")
            q.acquire("act", "rot q")
            t_rot = q.op("act", lambda e, i: e.activation(rot[:], both, ACT.Copy))
            q.release("misc", t_rot)
            q.wait("pool", t_rot, t_cross)
            q.wait("pool", q.last("pool")) if q.own["pool"].per.get(q.section) else q.acquire("pool", "pool idle")
            q.op("pool", lambda e, i: e.tensor_tensor(straight[:], rot[0:64], wide(slice(0, 64)), ALU.mult))
            t_add = q.chain("pool", lambda e, i: e.tensor_tensor(rot[0:64], straight[:], crossed[:], ALU.add))
            q.release("crossed", t_add)
            q.wait("act", t_add)
            q.acquire("act", ("q", cur))
            q.acquire("act", ("k", g))
            q.op("act", lambda e, i: e.activation(q_hi[:, cur, :], rot[:, 0, :], ACT.Copy, scale=float(DH) ** -0.5))
            t_hi = q.op("act", lambda e, i: e.activation(k_hi[:, where], rot[:, 1, :], ACT.Copy))
            q.wait("dve", t_hi)
            q.wait("pool", t_hi, t_add)
            q.acquire("dve", ("q", cur))
            q.acquire("pool", ("k", g))
            t_q = q.op("dve", lambda e, i: e.scalar_tensor_tensor(
                q_lo[:, cur, :], rot[:, 0, :], float(DH) ** -0.5, as_f32(q_hi[:, cur, :]), ALU.mult, ALU.subtract))
            t_k = q.op("pool", lambda e, i: e.tensor_tensor(k_lo[:, where], rot[:, 1, :], as_f32(k_hi[:, where]), ALU.subtract))
            q.release("pool idle", t_k)
            q.release("rot q", t_q)
            q.release("rot", t_k)
            q.release(("q written", cur), t_q)
            q.release(("k written", g), t_k)

        def scores(t, c, serial):
            cur, g = serial % 2, t // 2
            q.acquire("pe", ("q written", cur))
            q.acquire("pe", ("k written", g))
            left = slice((t % 2) * P, (t % 2 + 1) * P)
            def pairs(n):
                right = slice(c * CH, c * CH + n)
                a, b = q_hi[:, cur, left], q_lo[:, cur, left]
                return [(a, k_hi[:, right]), (a, k_lo[:, right]), (b, k_hi[:, right])]
            att.qk(t, c, pairs, ())
            done = q.last("pe")
            q.release(("q", cur), done)
            for g in range(2 * c, min(2 * c + 2, t // 2 + 1)):
                q.release(("k", g), done)

        def clear(g):
            buf = g % 2
            q.acquire("dve", ("pt", buf, (2 * g + 1) // 4, 0))
            for pt in (att.pt_hi, att.pt_lo):
                t = q.op("dve", lambda e, i, pt=pt: e.memset(as_f32(pt[buf][:, 2 * g + 1, 0:P]), 0.0))
            q.release(("cleared", buf), t)

        def pv(g, j, slot):
            buf, v = g % 2, slice(slot * DH, (slot + 1) * DH)
            for half in range(2):
                if half or j <= 2 * g:
                    q.acquire("pe", ("pt written", buf, j // 4, half))
            if j == 2 * g + 1:
                q.acquire("pe", ("cleared", buf))
            q.acquire("pe", ("v written", j // 2))
            if j == 0:
                q.acquire("pe", "y")
            done = products(q, att.y[:, 0:2 * P], [v_hi[:, j, v]], [v_lo[:, j, v]],
                            [(att.pt_hi[buf][:, j, :], att.pt_lo[buf][:, j, :])], first=j == 0, last=j == 2 * g + 1)
            for half in range(2):
                q.release(("pt", buf, j // 4, half), done)
            q.release(("v", j // 2), done)
            if j == 2 * g + 1:
                for e in ("act", "dve"):
                    q.acquire(e, "y halves")
                s = split(q, "act", "dve", y_hi[:], y_lo[:], att.y[:, 0:2 * P], done)
                q.release("y", s)
                q.release("y written", s)

        def out(g, slot):
            q.acquire("pe", "y written")
            q.acquire("pe", "wo split")
            q.acquire("pe", "misc")
            for n in range(2):
                done = products(q, att.misc[:, n * H:(n + 1) * H], [y_hi[:, n * P:(n + 1) * P]], [y_lo[:, n * P:(n + 1) * P]],
                                [(wo_hi[:], wo_lo[:])])
            q.release("y halves", done)
            q.release("wo", done)
            q.wait("dve", done)
            for n in range(2):
                t = 2 * g + n
                q.acquire("dve", ("x", t))
                q.acquire("dve", ("inv", slot, t))
                done = q.op("dve", lambda e, i, n=n, t=t: e.scalar_tensor_tensor(
                    core.x[:, t, :], att.misc[:, n * H:(n + 1) * H], att.inv[:, slot, t:t + 1], core.x[:, t, :], ALU.mult, ALU.add))
                q.release(("x", t), done)
                q.release(("inv", slot, t), done)
            q.release("misc", done)

        serial = 0

        def head(slot):
            nonlocal serial
            late = None
            for t in range(NT):
                g = t // 2
                if t == 2:
                    weights("wo", 2, raw_wo, wo_hi, wo_lo,
                            lambda i: src["wo1"][bass.ds(2 * i + slot, 1)].rearrange("a d n -> d (a n)"), 1.0 / 3.0)
                if t == NT - 3:
                    weights_of(1 - slot, slot)
                if t % 2 == 0 and g + 1 < G:
                    project(g + 1, serial + 1)
                    if slot == 0:
                        values(core, att, g + 1, wv_hi, wv_lo, v_hi, v_lo, [])
                        if g + 1 == G - 1:
                            q.release("wv", q.last("pe"))
                if t % 2 == 1:
                    serial += 1
                if t == NT - 1:
                    project(0, serial)
                if t % 2 == 0:
                    clear(g)
                js = range(2 * g) if g else ()
                mid = len(js) // 2
                work = list(js[:mid] if t % 2 == 0 else js[mid:])
                more = (t + 1) if t + 1 < NT else 0
                ahead = max(0, len(work) - 3)
                steps = max(t // 4, more // 4) + 1
                for b in range(steps):
                    if b <= t // 4:
                        att.turn(t, b)
                    if b == 0 and late is not None:
                        out(*late)
                        late = None
                    if b <= more // 4:
                        scores(more, b, serial if t % 2 else serial)
                    for _ in range(-(-ahead // steps)):
                        if len(work) > 3:
                            pv(g - 1, work.pop(0), slot)
                att.exps(more, slot if more else 1 - slot)
                for j in work:
                    pv(g - 1, j, slot)
                if t % 2 == 1 and g:
                    late = (g - 1, slot)
            if late is not None:
                out(*late)
            for j in range(NT):
                pv(G - 1, j, slot)
            out(G - 1, slot)
            if slot == 1:
                q.acquire("pe", "wv split")
                values(core, att, 0, wv_hi, wv_lo, v_hi, v_lo, [])

        q.begin()
        t = load(core, 3, rope[:], src["rope"])
        q.wait("dve", t)
        q.wait("pool", t)
        weights_of(0, 0)
        q.acquire("pe", "wv split")
        project(0, 0)
        values(core, att, 0, wv_hi, wv_lo, v_hi, v_lo, [])
        scores(0, 0, 0)
        att.exps(0, 0)
        q.meet()
        first_batch = att.batch
        q.begin(NH // 2)
        for slot in range(2):
            head(slot)
        assert serial % 2 == 0 and att.batch % 2 == first_batch % 2
        q.emit()


class Routes:

    def __init__(self, core, stack):
        sb, _ = core.rooms(stack)
        self.rows = sb("rows", [P, NE], I32)
        self.weight = sb("weight", [P, NE])
        self.tokens = sb("tokens", [P, NE, H])
        self.zero = sb("zero", [P, 4, H])


def router_phase(core, routes):
    q, nc, src = core.q, core.nc, core.src
    with ExitStack() as stack:
        sb, psum = core.rooms(stack)
        ps, ps_rank, ps_slot = psum("logits", [P, NT, NE]), psum("rank", [P, NT, NE]), psum("slot", [P, NE, 8])
        raw, w_hi, w_lo = sb("raw", [P, HK, NE]), sb("w_hi", [P, HK, NE], F32R), sb("w_lo", [P, HK, NE], F32R)
        below, ones, slots = sb("below", [P, P], BF16), sb("ones", [P, P], BF16), sb("slots", [P, P], BF16)
        row_id, tile_id = sb("row_id", [P, 1]), sb("tile_id", [P, NT])
        score, sel, eq, a, b = (sb(n, [P, NT, NE]) for n in ("score", "sel", "eq", "a", "b"))
        rank = sb("rank_all", [P, NT, NE])
        best = sb("best", [P, NT, 8])
        m1, m2 = sb("m1", [P, NT]), sb("m2", [P, NT])
        sel_b, before_b = sb("sel_b", [P, NT, NE], BF16), sb("before_b", [P, NT, NE], BF16)
        info = sb("info", [P, NT, NE, 6], BF16)
        hot = sb("hot", [P, 2, NT, P], BF16)
        got = sb("got", [P, NE, 8])
        s1, s2 = sb("s1", [P, NE]), sb("s2", [P, NE])
        wide = lambda ap: ap.unsqueeze(2).broadcast_to([P, NT, NE])
        q.begin()
        zeroed = q.op("pool", lambda e, i: e.memset(routes.zero[:], 0.0))
        q.chain("pool", lambda e, i: e.memset(ones[:], 1.0))
        ready_pool = q.last("pool")
        t_raw = load(core, 0, raw[:], src["gate0"])
        consts = [load(core, n, out[:], src[name]) for n, out, name in (
            (1, below, "below_b"), (2, slots, "slots_b"), (3, row_id, "row_id"), (4, tile_id, "tile_id"))]
        q.wait("sp", zeroed)
        stores = [load(core, 8 + c, core.y_rows[c * CH:(c + 1) * CH, :].rearrange("(t p) h -> p t h", p=P), routes.zero[:])
                  for c in range(NCH)]
        stores.append(load(core, 12, core.y_rows[T:T + CAP, :], routes.zero[:, 0, :]))
        stores.append(load(core, 13, core.xn_rows[T:T + CAP, :], routes.zero[:, 0, :]))
        ready = split(q, "act", "dve", w_hi[:], w_lo[:], raw[:], t_raw)
        q.wait("pe", ready)
        for t in range(NT):
            where = slice(t * P, (t + 1) * P)
            done = products(q, ps[:, t, :], [core.xt_hi[:, k, where] for k in range(HK)], [core.xt_lo[:, k, where] for k in range(HK)],
                            [(w_hi[:, k, :], w_lo[:, k, :]) for k in range(HK)])
        V = lambda fn: q.chain("dve", fn)
        q.wait("dve", done, *consts)
        V(lambda e, i: e.tensor_reduce(m1[:], ps[:], AX.X, ALU.max))
        t_sub = V(lambda e, i: e.tensor_tensor(score[:], ps[:], wide(m1[:]), ALU.subtract))
        q.wait("act", t_sub)
        t_exp = q.op("act", lambda e, i: e.activation(score[:], score[:], ACT.Exp))
        q.wait("dve", t_exp)
        V(lambda e, i: e.tensor_reduce(m1[:], score[:], AX.X, ALU.add))
        V(lambda e, i: e.reciprocal(m1[:], m1[:]))
        t_score = V(lambda e, i: e.tensor_tensor(score[:], score[:], wide(m1[:]), ALU.mult))
        q.wait("dve", t_score)
        for t in range(NT):
            q.op("dve", lambda e, i, t=t: e.max(best[:, t, :], score[:, t, :]))
        V(lambda e, i: e.tensor_reduce(m2[:], best[:, :, 0:TOPK], AX.X, ALU.add))
        V(lambda e, i: e.tensor_tensor(sel[:], score[:], wide(best[:, :, TOPK - 1]), ALU.is_gt))
        V(lambda e, i: e.tensor_tensor(eq[:], score[:], wide(best[:, :, TOPK - 1]), ALU.is_equal))
        V(lambda e, i: e.tensor_reduce(m1[:], sel[:], AX.X, ALU.add))
        cur, other = eq, a
        for step in (1, 2, 4, 8):
            V(lambda e, i, cur=cur, other=other, step=step: e.tensor_tensor(
                other[:, :, step:], cur[:, :, step:], cur[:, :, :NE - step], ALU.add))
            V(lambda e, i, cur=cur, other=other, step=step: e.tensor_copy(other[:, :, :step], cur[:, :, :step]))
            cur, other = other, (b if other is a else a)
        V(lambda e, i: e.tensor_tensor(cur[:], cur[:], wide(m1[:]), ALU.add))
        V(lambda e, i: e.tensor_scalar(cur[:], cur[:], TOPK + 0.5, None, ALU.is_lt))
        V(lambda e, i: e.tensor_tensor(cur[:], cur[:], eq[:], ALU.mult))
        V(lambda e, i: e.tensor_tensor(sel[:], sel[:], cur[:], ALU.add))
        V(lambda e, i: e.tensor_scalar(m2[:], m2[:], 1e-20, None, ALU.add))
        V(lambda e, i: e.reciprocal(m2[:], m2[:]))
        V(lambda e, i: e.tensor_tensor(score[:], score[:], wide(m2[:]), ALU.mult))
        V(lambda e, i: e.tensor_scalar(score[:], score[:], 0.5, None, ALU.mult))
        for n in range(3, 6):
            V(lambda e, i, n=n: e.tensor_copy(info[:, :, :, n], score[:]))
            if n < 5:
                V(lambda e, i, n=n: e.tensor_tensor(score[:], score[:], info[:, :, :, n], ALU.subtract))
        V(lambda e, i: e.tensor_scalar(info[:, :, :, 0], sel[:], 0.0, row_id[:], ALU.mult, ALU.add))
        V(lambda e, i: e.tensor_copy(info[:, :, :, 1], wide(tile_id[:])))
        V(lambda e, i: e.memset(info[:, :, :, 2], 1.0))
        V(lambda e, i: e.tensor_copy(sel_b[:], sel[:]))
        V(lambda e, i: e.memset(before_b[:, 0, :], 0.0))
        for t in range(1, NT):
            V(lambda e, i, t=t: e.tensor_tensor(before_b[:, t, :], before_b[:, t - 1, :], sel_b[:, t - 1, :], ALU.add))
        q.wait("pe", q.last("dve"), ready_pool)
        q.op("pe", lambda e, i: e.matmul(ps_rank[:], below[:], sel_b[:], start=True, stop=False), tick=False)
        t_rank = q.op("pe", lambda e, i: e.matmul(ps_rank[:], ones[:], before_b[:], start=False, stop=True))
        V(lambda e, i: e.tensor_scalar(rank[:], sel[:], -4.0 * T, 4.0 * T, ALU.mult, ALU.add))
        q.wait("dve", t_rank)
        V(lambda e, i: e.tensor_tensor(rank[:], rank[:], ps_rank[:], ALU.add))
        q.meet()

        q.begin(NE // 2)
        for n in range(2):
            q.acquire("dve", ("hot", n))
            for t in range(NT):
                rank_of = lambda i, t=t, n=n: rank[:, t, bass.ds(2 * i + n, 1)]
                done = q.op("dve", lambda e, i, t=t, n=n, rank_of=rank_of: e.tensor_scalar(
                    hot[:, n, t, :], slots[:], rank_of(i), None, ALU.is_equal))
            q.wait("pe", done)
            for t in range(NT):
                done = q.op("pe", lambda e, i, t=t, n=n: e.matmul(
                    ps_slot[:, bass.ds(2 * i + n, 1), 0:6].rearrange("p a b -> p (a b)"), hot[:, n, t, :],
                    info[:, t, bass.ds(2 * i + n, 1), :].rearrange("p a b -> p (a b)"),
                    start=t == 0, stop=t == NT - 1), tick=t == NT - 1)
            q.release(("hot", n), done)

        q.begin()
        q.wait("dve", done)
        V(lambda e, i: e.tensor_copy(got[:, :, 0:6], ps_slot[:, :, 0:6]))
        V(lambda e, i: e.tensor_scalar(s1[:], got[:, :, 1], float(P), float(T), ALU.mult, ALU.add))
        V(lambda e, i: e.tensor_tensor(s1[:], s1[:], got[:, :, 0], ALU.add))
        V(lambda e, i: e.tensor_scalar(s2[:], got[:, :, 2], -1.0, 1.0, ALU.mult, ALU.add))
        V(lambda e, i: e.tensor_scalar(s2[:], s2[:], row_id[:], None, ALU.mult))
        V(lambda e, i: e.tensor_tensor(routes.rows[:], s1[:], s2[:], ALU.add))
        V(lambda e, i: e.tensor_tensor(s1[:], got[:, :, 3], got[:, :, 4], ALU.add))
        V(lambda e, i: e.tensor_tensor(routes.weight[:], s1[:], got[:, :, 5], ALU.add))
        q.wait("sp", *stores)
        q.emit()


def fetch_tokens(core, routes):
    q = core.q
    done = [q.op("pool", lambda e, i, n=n: e.indirect_dma_start(
        routes.tokens[:, n, :], None, core.xn_rows, bass.IndirectOffsetOnAxis(ap=routes.rows[:, n:n + 1], axis=0)),
        flow=core.gather_out[n]) for n in range(NE)]
    return done


def experts_phase(core, routes):
    q, nc, src = core.q, core.nc, core.src
    IK = I0P // P
    with ExitStack() as stack:
        sb, psum = core.rooms(stack)
        turned = psum("turned", [P, 2, BANK])
        gu = psum("gu", [P, 2, BANK])
        turned_h = psum("turned_h", [P, 2, BANK])
        down = psum("down", [P, 2, BANK])
        raw_up, raw_dn = sb("raw_up", [P, 2, HK, 2 * I0]), sb("raw_dn", [P, 2, IK, H])
        up_hi, up_lo = (sb(n, [P, 2, HK, 2 * I0], F32R) for n in ("up_hi", "up_lo"))
        dn_hi, dn_lo = (sb(n, [P, 2, IK, H], F32R) for n in ("dn_hi", "dn_lo"))
        x_hi, x_lo = (sb(n, [P, 2, HK, P], F32R) for n in ("x_hi", "x_lo"))
        h_hi, h_lo = (sb(n, [P, 2, IK, P], F32R) for n in ("h_hi", "h_lo"))
        gate, h = sb("gate", [P, 2, I0]), sb("h", [P, 2, I0P])
        rows = sb("rows_out", [P, NE, H])
        q.begin()
        q.op("dve", lambda e, i: e.memset(h[:], 0.0))

        def up(s, e_of):
            q.acquire("sp", ("raw", s))
            q.acquire("sp", ("raw2", s))
            t_up = q.op("sp", lambda e, i: e.dma_start(raw_up[:, s], src["expert_up"][bass.ds(e_of(i), 1)].rearrange("a p k n -> p (a k) n")),
                        flow=core.loads[2 * s])
            t_dn = q.op("sp", lambda e, i: e.dma_start(raw_dn[:, s], src["expert_down"][bass.ds(e_of(i), 1)].rearrange("a p k n -> p (a k) n")),
                        flow=core.loads[2 * s + 1])
            q.acquire("act", ("w", s))
            q.acquire("dve", ("w", s))
            q.acquire("pool", ("w", s))
            t_w = split(q, "act", "pool", up_hi[:, s], up_lo[:, s], raw_up[:, s], t_up)
            t_w2 = split(q, "act", "dve", dn_hi[:, s], dn_lo[:, s], raw_dn[:, s], t_dn)
            q.acquire("pe", ("turned", s))
            token = lambda i, k: routes.tokens[:, bass.ds(e_of(i), 1), k * P:(k + 1) * P].rearrange("p a b -> p (a b)")
            stage = x_raw[:, s]
            q.acquire("dve", ("x_raw", s))
            done = q.op("dve", lambda e, i: e.tensor_copy(stage, routes.tokens[:, bass.ds(e_of(i), 1), :].rearrange("p a b -> p (a b)")))
            q.wait("pe", done)
            for k in range(HK):
                done = q.op("pe", lambda e, i, k=k: e.transpose(turned[:, s, k * P:(k + 1) * P], stage[:, k * P:(k + 1) * P], core.ident[:]),
                            tick=k == HK - 1)
            q.release(("x_raw", s), done)
            q.acquire("act", ("x", s))
            q.acquire("dve", ("x", s))
            t_x = split(q, "act", "dve", x_hi[:, s], x_lo[:, s], turned[:, s, 0:HK * P].rearrange("p (a b) -> p a b", a=HK), done)
            q.release(("turned", s), t_x)
            q.wait("pe", t_x, t_w, t_w2)
            q.acquire("pe", ("gu", s))
            done = products(q, gu[:, s, 0:2 * I0], [x_hi[:, s, k] for k in range(HK)], [x_lo[:, s, k] for k in range(HK)],
                            [(up_hi[:, s, k], up_lo[:, s, k]) for k in range(HK)])
            q.release(("x", s), done)
            q.wait("act", done)
            q.acquire("act", ("gate", s))
            t_g = q.op("act", lambda e, i: e.activation(gate[:, s], gu[:, s, 0:I0], ACT.Silu))
            q.wait("dve", t_g)
            q.acquire("dve", ("h", s))
            t_h = q.op("dve", lambda e, i: e.tensor_tensor(h[:, s, 0:I0], gu[:, s, I0:2 * I0], gate[:, s], ALU.mult))
            q.release(("gate", s), t_h)
            q.release(("gu", s), t_h)
            q.release(("h written", s), t_h)
            q.release(("raw", s), t_w)
            q.release(("raw2", s), t_w2)

        def dn(s, e_of):
            q.acquire("pe", ("h written", s))
            q.acquire("pe", ("turned_h", s))
            for k in range(IK):
                done = q.op("pe", lambda e, i, k=k: e.transpose(turned_h[:, s, k * P:(k + 1) * P], h[:, s, k * P:(k + 1) * P], core.ident[:]),
                            tick=k == IK - 1)
            q.release(("h", s), done)
            q.acquire("act", ("ht", s))
            q.acquire("dve", ("ht", s))
            t_h = split(q, "act", "dve", h_hi[:, s], h_lo[:, s], turned_h[:, s, 0:IK * P].rearrange("p (a b) -> p a b", a=IK), done)
            q.release(("turned_h", s), t_h)
            q.wait("pe", t_h)
            q.acquire("pe", ("down", s))
            done = products(q, down[:, s, 0:H], [h_hi[:, s, k] for k in range(IK)], [h_lo[:, s, k] for k in range(IK)],
                            [(dn_hi[:, s, k], dn_lo[:, s, k]) for k in range(IK)])
            q.release(("ht", s), done)
            q.release(("w", s), done)
            q.wait("dve", done)
            t_o = q.op("dve", lambda e, i: e.tensor_scalar(
                rows[:, bass.ds(e_of(i), 1), :].rearrange("p a b -> p (a b)"), down[:, s, 0:H],
                routes.weight[:, bass.ds(e_of(i), 1)], None, ALU.mult))
            q.release(("down", s), t_o)
            return t_o

        x_raw = sb("x_raw", [P, 2, H])
        q.wait("dve", *routes.fetched)
        up(0, lambda i: 0)
        q.meet()
        q.begin(NE // 2 - 1)
        up(1, lambda i: 2 * i + 1)
        outs = [dn(0, lambda i: 2 * i)]
        up(0, lambda i: 2 * i + 2)
        outs.append(dn(1, lambda i: 2 * i + 1))
        q.begin()
        up(1, lambda i: NE - 1)
        late = [dn(0, lambda i: NE - 2), dn(1, lambda i: NE - 1)]
        for n in range(NE):
            if n < NE - 2:
                q.wait_turn("pool", outs[n % 2], n // 2)
            else:
                q.wait("pool", late[n - (NE - 2)])
            done = q.op("pool", lambda e, i, n=n: e.indirect_dma_start(
                core.y_rows, bass.IndirectOffsetOnAxis(ap=routes.rows[:, n:n + 1], axis=0), rows[:, n, :], None, compute_op=ALU.add),
                flow=core.add_out[n % 2])
            q.wait("pool", done)
        q.emit()


def ffn0_block(core):
    with ExitStack() as stack:
        routes = Routes(core, stack)
        router_phase(core, routes)

        def beside(_):
            routes.fetched = fetch_tokens(core, routes)

        ffn_phase(core, core.src["shared_up"], core.src["shared_down"], IS, extra=beside)
        experts_phase(core, routes)


def program(nc, src, out):
    with ExitStack() as stack:
        q = Queues(nc, stack)
        core = Core(nc, stack, q, src)
        ffn1 = lambda: ffn_phase(core, src["up1"], src["down1"], I1, (src["gs1"], src["us1"], src["ds1"]))
        start_phase(core)
        layernorm_phase(core, keep_rows=True)
        ffn0_block(core)
        layernorm_phase(core, add_y=True)
        attention0_phase(core)
        layernorm_phase(core, keep_rows=True)
        ffn0_block(core)
        layernorm_phase(core, add_y=True)
        ffn1()
        layernorm_phase(core)
        attention1_phase(core)
        layernorm_phase(core)
        ffn1()
        q.begin()
        q.wait("sp", load(core, 0, out.rearrange("(t p) h -> p t h", p=P), core.x[:]))
        q.emit()



def _tables():
    fraction = np.linspace(0.0, 1.0, DH // 4, dtype=np.float32)
    af = np.power(np.float32(1.0 / 1024.0), fraction).astype(np.float32)
    theta = (np.arange(T, dtype=np.float32)[None, :] * af[:, None]).astype(np.float32)
    cos, sin = np.cos(theta).astype(np.float32), np.sin(theta).astype(np.float32)
    bf = mybir.dt.np(BF16)
    r = np.arange(P)
    return {
        "rope": np.concatenate([cos, cos, -sin, sin]),
        "ident": np.eye(P, dtype=np.float32),
        "ident_b": np.eye(P, dtype=bf),
        "mask_b": np.where(r[None, :] > r[:, None], NEG, 0.0).astype(bf),
        "below_b": (r[:, None] < r[None, :]).astype(bf),
        "slots_b": np.broadcast_to(r[None, :], (P, P)).astype(bf),
        "row_id": r[:, None].astype(np.float32),
        "tile_id": np.broadcast_to(np.arange(NT)[None, :] - NT, (P, NT)).astype(np.float32),
    }


def _wide(w):
    return w.reshape(-1, P, w.shape[-1]).transpose(1, 0, 2)


def _pad(w, rows, width):
    out = np.zeros((*w.shape[:-2], rows, width), w.dtype)
    out[..., :w.shape[-2], :w.shape[-1]] = w
    return out


def _layouts(i):
    a = {k: np.asarray(v) for k, v in i.items()}
    out = {"x": a["L0_attn_x"][0]}
    out["gate0"] = _wide(a["L0_ffn_gate_w"].T)
    up = np.concatenate([a["L0_ffn_w_gate"], a["L0_ffn_w_up"]], axis=-1)
    out["expert_up"] = up.reshape(NE, HK, P, 2 * I0).transpose(0, 2, 1, 3)
    out["expert_down"] = _pad(a["L0_ffn_w_down"], I0P, H).reshape(NE, I0P // P, P, H).transpose(0, 2, 1, 3)
    g, u = _pad(a["L0_ffn_sw_gate"], H, ISM * P), _pad(a["L0_ffn_sw_up"], H, ISM * P)
    out["shared_up"] = _wide(np.stack([g.reshape(H, ISM, P), u.reshape(H, ISM, P)], axis=2).reshape(H, -1))
    out["shared_down"] = _wide(_pad(a["L0_ffn_sw_down"], ISM * P, H))
    out["ws"], out["wa"] = (_wide(np.tile(a[n], (1, P // R0))) for n in ("L0_attn_Ws", "L0_attn_Wa"))
    out["wo0"] = _wide(a["L0_attn_Wo"].T)
    out["bo"] = a["L0_attn_bo"][None, :]
    turn = np.concatenate([np.arange(0, 32), np.arange(64, 96), np.arange(32, 64), np.arange(96, 128)])
    qk = np.stack([a[n].reshape(NH, DH, H)[:, turn, :] for n in ("L1_attn_Wq", "L1_attn_Wk")], axis=1)
    out["qk"] = qk.reshape(NH, 2, DH, HK, P).transpose(0, 4, 3, 1, 2)
    out["qk"] = np.concatenate([out["qk"], np.zeros_like(out["qk"][:2])])
    out["wv"] = a["L1_attn_Wv"].reshape(NH // 2, 2 * DH, HK, P).transpose(0, 3, 2, 1)
    out["wv"] = np.concatenate([out["wv"], np.zeros_like(out["wv"][:1])])
    out["wo1"] = a["L1_attn_Wo"].reshape(H, NH, DH).transpose(1, 2, 0)
    full = (I1 // P) * P
    g, u = a["L1_ffn_gate_w"].T, a["L1_ffn_up_w"].T
    both = np.stack([g[:, :full].reshape(H, -1, P), u[:, :full].reshape(H, -1, P)], axis=2).reshape(H, -1)
    out["up1"] = _wide(np.concatenate([both, g[:, full:], u[:, full:]], axis=1))
    out["down1"] = _wide(_pad(a["L1_ffn_down_w"].T, I1M * P, H))
    gs, us = (_pad(a[n].reshape(1, I1), 1, I1M * P).reshape(I1M, P).T for n in ("L1_ffn_gate_s", "L1_ffn_up_s"))
    us = us.copy()
    us[P // 2:, -1] = us[:P // 2, -1]
    out["gs1"], out["us1"], out["ds1"] = gs, us, a["L1_ffn_down_s"][None, :]
    return out


def kernel(**inputs):
    from concourse import bacc
    from concourse.bass_utils import run_bass_kernel_spmd

    nc = bacc.Bacc("TRN2", target_bir_lowering=False, num_devices=1)
    arrays = {n: np.ascontiguousarray(a) for n, a in {**_layouts(inputs), **_tables()}.items()}
    src = {n: nc.dram_tensor(n, a.shape, mybir.dt.from_np(a.dtype), kind="ExternalInput").ap() for n, a in arrays.items()}
    out = nc.dram_tensor("out", (T, H), F32, kind="ExternalOutput").ap()
    program(nc, src, out)
    r = run_bass_kernel_spmd(nc, [arrays], core_ids=[0])
    return r.results[0]["out"].reshape(1, T, H)
```

```python
from contextlib import ExitStack

import numpy as np

import concourse.bass as bass
from concourse import mybir
from concourse.alu_op_type import AluOpType as ALU

F32 = mybir.dt.float32
F32R = mybir.dt.float32r
BF16 = mybir.dt.bfloat16
I32 = mybir.dt.int32
U32 = mybir.dt.uint32
ACT = mybir.ActivationFunctionType
AX = mybir.AxisListType

P = 128
H = 256
HK = H // P
T = 2048
NT = T // P
CH = 512
NCH = T // CH
BANK = 512
EPS = 1e-5

NE, TOPK, CAP = 16, 4, 128
I0 = 176
I0P = 256
IS = 352
ISM = 3
TRASH = T

R0 = 32
NH, DH = 16, 128
I1 = 704
I1M = 6
CREDIT = 1024
NEG = -1e30


class Flow:

    def __init__(self, sem, step):
        self.sem, self.step, self.before, self.per = sem, step, {}, {}
        self.total = 0


class Tick:

    def __init__(self, section, flow, k):
        self.section, self.flow, self.k = section, flow, k


class Section:

    def __init__(self, times):
        self.times, self.items, self.named = times, {}, {}


class Queues:

    ENGINES = ("pe", "act", "dve", "pool", "sp")

    def __init__(self, nc, stack):
        self.nc, self.stack = nc, stack
        self.own = {e: self.flow(f"done_{e}", 1) for e in self.ENGINES}
        self.waited = self.flow("waited", 1)
        self.sections, self.section = [], None

    def flow(self, name, step):
        return Flow(self.stack.enter_context(self.nc.semaphore(name)), step)

    def credit(self, flow):
        flow.total += CREDIT
        return Flow(flow.sem, CREDIT)

    def begin(self, times=1):
        self.section = Section(times)
        self.sections.append(self.section)
        self.seen = {}

    def op(self, engine, fn, flow=None, tick=True, name=None):
        if not tick:
            self.section.items.setdefault(engine, []).append((fn, None))
            return None
        flow = flow or self.own[engine]
        k = flow.per.get(self.section, 0) + flow.step
        flow.per[self.section] = k
        self.section.items.setdefault(engine, []).append((fn, flow))
        t = Tick(self.section, flow, k)
        if name is not None:
            self.section.named[name] = t
        return t

    def last(self, engine):
        flow = self.own[engine]
        return Tick(self.section, flow, flow.per.get(self.section, 0))

    def wait(self, engine, *ticks):
        for t in ticks:
            if t is None:
                continue
            key = (engine, t.flow)
            old = self.seen.get(key)
            if old is not None and old[0] is t.section and old[1] >= t.k:
                continue
            self.seen[key] = (t.section, t.k)
            self.section.items.setdefault(engine, []).append((t, None))

    def wait_before(self, engine, name):
        self.section.items.setdefault(engine, []).append((name, -1))

    def release(self, name, tick):
        self.section.named[name] = tick

    def acquire(self, engine, name):
        if name in self.section.named:
            self.wait(engine, self.section.named[name])
        elif self.section.times > 1:
            self.wait_before(engine, name)
        elif len(self.sections) > 1 and name in self.sections[-2].named:
            self.wait(engine, self.sections[-2].named[name])

    def meet(self):
        for e in self.ENGINES:
            self.wait(e, *(self.last(other) for other in ("pe", "act", "dve", "pool") if self.own[other].per.get(self.section)))

    def wait_turn(self, engine, tick, turn):
        self.section.items.setdefault(engine, []).append((tick, turn))

    def chain(self, engine, fn, **kw):
        self.wait(engine, self.last(engine))
        return self.op(engine, fn, **kw)

    def emit(self):
        nc = self.nc
        for s in self.sections:
            for f in {t for e in s.items.values() for _, t in e if isinstance(t, Flow)}:
                f.before[s] = f.total
                f.total += s.times * f.per[s]

        def strongest(s, items):
            kept, row = [], {}
            for what, extra in items:
                if callable(what):
                    kept += [*(item for _, item in row.values()), (what, extra)]
                    row = {}
                    continue
                t = s.named[what] if extra == -1 else what
                f, own = t.flow, t.section is s
                turn = -1 if extra == -1 else extra if extra is not None else 0 if own else t.section.times - 1
                reach = own and s.times > 1, f.before[t.section] + turn * f.per[t.section] + t.k
                if t.flow not in row or reach > row[t.flow][0]:
                    row[t.flow] = reach, (what, extra)
            return kept + [item for _, item in row.values()]

        def run(engine, name):
            for s in self.sections:
                items = s.items.get(name)
                if not items:
                    continue

                def body(i):
                    for what, extra in strongest(s, items):
                        if isinstance(what, Tick):
                            f = what.flow
                            turn = extra if extra is not None else i if what.section is s else what.section.times - 1
                            engine.wait_ge(f.sem, turn * f.per[what.section] + f.before[what.section] + what.k)
                        elif extra == -1:
                            t = s.named[what]
                            f = t.flow
                            engine.wait_ge(f.sem, i * f.per[s] + f.before[s] + t.k - f.per[s])
                        else:
                            ins = what(engine, i)
                            if extra is not None:
                                ins.then_inc(extra.sem, extra.step)
                        if not callable(what) and name == "sp" and s.times > 1:
                            engine.sem_inc(self.waited.sem, 1)

                if s.times == 1:
                    body(0)
                else:
                    with engine.Fori(0, s.times) as i:
                        body(i)

        with nc.Block() as block:
            block.tensor(lambda eng: run(eng, "pe"))
            block.scalar(lambda eng: run(eng, "act"))
            block.vector(lambda eng: run(eng, "dve"))
            block.gpsimd(lambda eng: run(eng, "pool"))
            block.sync(lambda eng: run(eng, "sp"))
        self.sections = []


def cols(ap, start, n):
    return ap[:, bass.ds(start, n)]


def as_f32(ap):
    return ap.bitcast(F32)


class Core:

    def __init__(self, nc, stack, q, src):
        self.nc, self.q, self.src, self.phase = nc, q, src, 0
        sb = lambda name, shape, dt: stack.enter_context(nc.sbuf_tensor("sb_" + name, shape, dt))
        self.x = sb("x", [P, NT, H], F32)
        self.xt_hi = sb("xt_hi", [P, HK, T], F32R)
        self.xt_lo = sb("xt_lo", [P, HK, T], F32R)
        self.ident = sb("ident", [P, P], F32)
        self.ident_b = sb("ident_b", [P, P], BF16)
        self.mask_b = sb("mask_b", [P, P], BF16)
        self.loads = [q.flow(f"load_{n}", 16) for n in range(24)]
        self.gather_out = [q.flow(f"gather_{n}", 16) for n in range(NE)]
        self.add_out = [q.flow(f"add_{n}", 16) for n in range(2)]
        self.xn_rows = nc.dram_tensor("xn_rows", (T + CAP, H), F32).ap()
        self.y_rows = nc.dram_tensor("y_rows", (T + CAP, H), F32).ap()


    def rooms(self, stack):
        self.phase += 1
        tag = f"phase{self.phase}_"
        return (lambda name, shape, dt=F32: stack.enter_context(self.nc.sbuf_tensor(tag + name, shape, dt)),
                lambda name, shape, dt=F32: stack.enter_context(self.nc.psum_tensor(tag + name, shape, dt)))


def load(core, n, out, src):
    return core.q.op("sp", lambda e, i: e.dma_start(out, src), flow=core.loads[n])


def split(q, hi_engine, lo_engine, hi, lo, value, ready, scale=None):
    q.wait(hi_engine, ready)
    if hi_engine == "act":
        t = q.op("act", lambda e, i: e.activation(hi, value, ACT.Copy, scale=1.0 if scale is None else scale))
    elif scale is None:
        t = q.op(hi_engine, lambda e, i: e.tensor_copy(hi, value))
    else:
        t = q.op(hi_engine, lambda e, i: e.tensor_scalar(hi, value, scale, None, ALU.mult))
    q.wait(lo_engine, ready, t)
    if scale is None:
        return q.op(lo_engine, lambda e, i: e.tensor_tensor(lo, value, as_f32(hi), ALU.subtract))
    return q.op(lo_engine, lambda e, i: e.scalar_tensor_tensor(lo, value, scale, as_f32(hi), ALU.mult, ALU.subtract))


def products(q, out, left_hi, left_lo, rights, first=True, last=True):
    n = len(rights)
    for c, (r_hi, r_lo) in enumerate(rights):
        for p, (a, b) in enumerate(((left_hi[c], r_hi), (left_hi[c], r_lo), (left_lo[c], r_hi))):
            s, e = first and c == 0 and p == 0, last and c == n - 1 and p == 2
            t = q.op("pe", (lambda a, b, s, e: lambda eng, i: eng.matmul(
                out(i) if callable(out) else out, a, b(i) if callable(b) else b, start=s, stop=e))(a, b, s, e),
                tick=c == n - 1 and p == 2)
    return t


def start_phase(core):
    q, c, src = core.q, core, core.src
    q.begin()
    done = [load(core, 0, c.x[:], src["x"].rearrange("(t p) h -> p t h", p=P)),
            load(core, 1, c.ident[:], src["ident"]),
            load(core, 2, c.ident_b[:], src["ident_b"]),
            load(core, 3, c.mask_b[:], src["mask_b"])]
    q.wait("sp", *done)
    for engine, flow in q.own.items():
        q.op(engine, lambda e, i: e.nop(), flow=q.credit(flow))
    q.emit()


def layernorm_phase(core, add_y=False, keep_rows=False):
    q, nc = core.q, core.nc
    with ExitStack() as stack:
        sb, psum = core.rooms(stack)
        ps = psum("ps", [P, 4, BANK])
        xn = sb("ln_xn", [P, NT, H])
        stats = sb("ln_stats", [P, NT, 6])
        mv = sb("ln_mv", [P, NT, 2])
        var, root, rstd, tmp = (sb(f"ln_{n}", [P, NT]) for n in ("var", "root", "rstd", "tmp"))
        q.begin()
        if add_y:
            yb = sb("ln_y", [P, NT, H])
            rows = core.y_rows[0:T, :].rearrange("(t p) h -> p t h", p=P)
            for c in range(4):
                here = yb[:, 4 * c:4 * c + 4, :], core.x[:, 4 * c:4 * c + 4, :]
                t = load(core, c, here[0], rows[:, 4 * c:4 * c + 4, :])
                q.wait("dve", t)
                t = q.op("dve", lambda e, i, h=here: e.tensor_tensor(h[1], h[1], h[0], ALU.add))
            q.wait("dve", t)
        for t in range(NT):
            last = q.op("dve", lambda e, i, t=t: e.bn_stats(stats[:, t, :], core.x[:, t, :]))
        q.wait("dve", last)
        for t in range(NT):
            q.op("dve", lambda e, i, t=t: e.bn_aggr(mv[:, t, :], stats[:, t, :]))
        ready = q.chain("dve", lambda e, i: e.tensor_scalar(var[:], mv[:, :, 1], EPS, None, ALU.add))
        q.wait("act", ready)
        ready = q.op("act", lambda e, i: e.activation(root[:], var[:], ACT.Sqrt))
        q.wait("dve", ready)
        q.op("dve", lambda e, i: e.reciprocal(rstd[:], root[:]))
        q.chain("dve", lambda e, i: e.tensor_tensor(tmp[:], rstd[:], rstd[:], ALU.mult))
        q.chain("dve", lambda e, i: e.tensor_tensor(tmp[:], tmp[:], var[:], ALU.mult))
        q.chain("dve", lambda e, i: e.tensor_scalar(tmp[:], tmp[:], -0.5, 1.5, ALU.mult, ALU.add))
        q.chain("dve", lambda e, i: e.tensor_tensor(rstd[:], rstd[:], tmp[:], ALU.mult))
        q.wait("dve", q.last("dve"))
        normed = [q.op("dve", lambda e, i, t=t: e.tensor_scalar(
            xn[:, t, :], core.x[:, t, :], mv[:, t, 0:1], rstd[:, t:t + 1], ALU.subtract, ALU.mult)) for t in range(NT)]
        freed = []
        for c in range(NCH):
            for k in range(HK):
                b = (HK * c + k) % 4
                if len(freed) >= 4:
                    q.wait("pe", freed[-4])
                q.wait("pe", normed[4 * c + 3])
                for j in range(4):
                    done = q.op("pe", lambda e, i, c=c, k=k, b=b, j=j: e.transpose(
                        ps[:, b, j * P:(j + 1) * P], xn[:, 4 * c + j, k * P:(k + 1) * P], core.ident[:]), tick=j == 3)
                where = slice(c * CH, (c + 1) * CH)
                freed.append(split(q, "act", "dve", core.xt_hi[:, k, where], core.xt_lo[:, k, where], ps[:, b, :], done))
        if keep_rows:
            for c in range(4):
                q.wait("sp", normed[4 * c + 3])
                t = load(core, 4 + c, core.xn_rows[0:T, :].rearrange("(t p) h -> p t h", p=P)[:, 4 * c:4 * c + 4, :],
                         xn[:, 4 * c:4 * c + 4, :])
                q.wait("sp", t)
        q.emit()


def ffn_phase(core, up_src, down_src, width, scales=None, extra=None):
    q, nc, merged = core.q, core.nc, scales is not None
    pairs = width // P if merged else -(-width // P)
    pieces = pairs + merged
    n_up = (2 * pairs + merged) * P
    with ExitStack() as stack:
        sb, psum = core.rooms(stack)
        ps = psum("ps", [P, 8, BANK])
        up_hi, up_lo = (sb(n, [P, HK, n_up], F32R) for n in ("up_hi", "up_lo"))
        dn_hi, dn_lo = (sb(n, [P, pieces, H], F32R) for n in ("dn_hi", "dn_lo"))
        raw_up, raw_dn = sb("raw_up", [P, HK, n_up]), sb("raw_dn", [P, pieces, H])
        h_hi, h_lo = (sb(n, [P, pieces, CH], F32R) for n in ("h_hi", "h_lo"))
        gate, act = sb("gate", [P, 2, CH]), sb("act", [P, 2, CH])
        q.begin()
        if extra:
            extra(stack)
        ready = []
        for k in range(HK):
            t = load(core, k, raw_up[:, k, :], up_src[:, k, :])
            ready.append(split(q, "act", "dve", up_hi[:, k, :], up_lo[:, k, :], raw_up[:, k, :], t))
        t = load(core, 2, raw_dn[:], down_src)
        ready.append(split(q, "act", "pool", dn_hi[:], dn_lo[:], raw_dn[:], t))
        if merged:
            gs, us, ds = sb("gs", [P, pieces]), sb("us", [P, pieces]), sb("ds", [P, H])
            s_t = [load(core, 3, gs[:], scales[0]), load(core, 4, us[:], scales[1]),
                   load(core, 5, ds[:], scales[2].partition_broadcast(P))]
            q.wait("dve", *s_t)
            q.wait("act", *s_t)
            ready.append(q.op("dve", lambda e, i: e.tensor_scalar(ds[:], ds[:], 0.5, None, ALU.mult)))
            ready.append(q.chain("pool", lambda e, i: e.memset(as_f32(h_hi[64:P, pieces - 1, :]), 0.0)))
            ready.append(q.op("pool", lambda e, i: e.memset(as_f32(h_lo[64:P, pieces - 1, :]), 0.0)))
            tmp = sb("tmp", [P, 2, H])

        q.wait("pe", *ready)
        q.wait("dve", *ready)
        q.begin(NCH)
        xt = lambda src, k: (lambda i: src[:, k, bass.ds(i * CH, CH)])
        rights = [(xt(core.xt_hi, k), xt(core.xt_lo, k)) for k in range(HK)]
        split_h = []
        acted = []
        for m in range(pieces):
            half = merged and m == pieces - 1
            rows = slice(0, 64) if half else slice(0, P)
            banks = (m % 2, 2 + m % 2)
            if m >= 2:
                q.wait("pe", acted[m - 2])
            else:
                q.wait_before("pe", ("act", pieces - 1))
            for n, bank in enumerate(banks[:1] if half else banks):
                at = (2 * m + n) * P
                done = products(q, ps[:, bank, :], [up_hi[:, k, at:at + P] for k in range(HK)],
                                [up_lo[:, k, at:at + P] for k in range(HK)], rights)
            g = ps[rows, banks[0], :]
            u = ps[64:P, banks[0], :] if half else ps[:, banks[1], :]
            q.wait("act", done)
            if m >= 2:
                q.wait("act", acted[m - 2])
            else:
                q.wait_before("act", ("act", pieces - 1))
            g_t = q.op("act", lambda e, i, g=g, m=m, rows=rows: e.activation(
                gate[rows, m % 2, :], g, ACT.Silu, scale=gs[rows, m:m + 1] if merged else 1.0))
            q.wait("dve", g_t)
            if m >= 2:
                q.wait("dve", split_h[m - 2])
            else:
                q.wait_before("dve", ("split", pieces - 1))
            urow = slice(64, P) if half else slice(0, P)
            acted.append(q.op("dve", lambda e, i, u=u, m=m, rows=rows, urow=urow: e.scalar_tensor_tensor(
                act[rows, m % 2, :], u, us[urow, m:m + 1] if merged else 1.0, gate[rows, m % 2, :], ALU.mult, ALU.mult),
                name=("act", m)))
            q.wait("pool", q.last("pool")) if m else q.wait_before("pool", ("split", pieces - 1))
            q.wait_before("act", ("down", pieces - 1))
            q.wait_before("pool", ("down", pieces - 1))
            s = split(q, "act", "pool", h_hi[rows, m, :], h_lo[rows, m, :], act[rows, m % 2, :], acted[-1])
            q.section.named[("split", m)] = s
            split_h.append(s)
        q.wait_before("pe", "added")
        for m in range(pieces):
            q.wait("pe", split_h[m])
            for j in range(4):
                t = products(q, ps[:, 4 + j, 0:H], [h_hi[:, m, j * P:(j + 1) * P]], [h_lo[:, m, j * P:(j + 1) * P]],
                             [(dn_hi[:, m, :], dn_lo[:, m, :])], first=m == 0, last=m == pieces - 1)
            q.section.named[("down", m)] = t
        for j in range(4):
            q.wait("dve", t)
            row = lambda i, j=j: core.x[:, bass.ds(i * 4 + j, 1), :].rearrange("p a h -> p (a h)")
            if merged:
                q.wait("dve", q.last("dve"))
                q.op("dve", lambda e, i, j=j: e.tensor_tensor(tmp[:, j % 2, :], ps[:, 4 + j, 0:H], ds[:], ALU.mult))
                q.chain("dve", lambda e, i, j=j, row=row: e.tensor_tensor(row(i), row(i), tmp[:, j % 2, :], ALU.add), name="added")
            else:
                q.op("dve", lambda e, i, j=j, row=row: e.scalar_tensor_tensor(
                    row(i), ps[:, 4 + j, 0:H], 0.5, row(i), ALU.mult, ALU.add), name="added")
        q.emit()


COVER = 33
LAG = 1

SUMS = (4, 6, 6, 2, 0, 4, 2, 4, 3, 5, 4, 6, 6, 6, 6, 8)


class Attention:

    def __init__(self, core, stack):
        self.core, self.q = core, core.q
        sb, psum = core.rooms(stack)
        self.sb = sb
        self.scores = psum("scores", [P, 4 * BANK])
        self.ring = psum("ring", [P, 3, BANK])
        self.y = psum("y", [P, BANK])
        self.p = sb("p", [P, T])
        self.pt_hi, self.pt_lo = ([sb(f"pt_{n}{b}", [P, NT - 2 * (b == 0), 2 * P], F32R) for b in range(2)] for n in ("hi", "lo"))
        self.peaks, self.bias = sb("peaks", [P, 2, 4]), sb("bias", [P, 2])
        self.sums, self.total = sb("sums", [P, 2, 4]), sb("total", [P, 2])
        self.inv = sb("inv", [P, 2, NT])
        self.rung = 0

    def bank(self):
        n, self.rung = self.rung % 3, self.rung + 1
        self.q.acquire("pe", ("ring", n))
        return self.ring[:, n, :], ("ring", n)

    def qk(self, t, c, pairs, ready):
        q = self.q
        diag = c == t // 4
        n = max(256, (t % 4 + 1) * P) if diag else BANK
        out = self.scores[:, c * BANK:c * BANK + n]
        q.wait("pe", *ready)
        q.acquire("pe", ("scores", c))
        products_ = pairs(n)
        for k, (a, b) in enumerate(products_):
            done = q.op("pe", lambda e, i, a=a, b=b, k=k: e.matmul(
                out, a, b, start=k == 0, stop=k == len(products_) - 1),
                tick=k == len(products_) - 1)
        if diag:
            at = t * P
            done = q.op("pe", lambda e, i: e.matmul(self.scores[:, at:at + P], self.core.ident_b[:], self.core.mask_b[:],
                                                    start=False, stop=True, skip_group_check=True))
        width = (t % 4 + 1) * P if diag else BANK
        q.wait("dve", done)
        q.op("dve", lambda e, i: e.tensor_reduce(self.peaks[:, t % 2, c:c + 1],
                                                 self.scores[:, c * BANK:c * BANK + width], AX.X, ALU.max))

    def peak(self, t):
        q, chunks = self.q, t // 4 + 1
        q.wait("dve", q.last("dve"))
        q.acquire("dve", ("bias", t % 2))
        done = q.op("dve", lambda e, i: e.tensor_reduce(self.bias[:, t % 2:t % 2 + 1], self.peaks[:, t % 2, 0:chunks],
                                                          AX.X, ALU.max, negate=True))
        q.release(("bias written", t % 2), done)

    def exps(self, t):
        q, chunks = self.q, t // 4 + 1
        q.acquire("act", ("bias written", t % 2))
        q.acquire("act", ("sums", t % 2))
        parts = [(a, min(b, chunks)) for a, b in ((0, 1), (1, 2), (2, 4)) if a < chunks]
        for n, (a, b) in enumerate(parts):
            lo, hi = a * BANK, min(b * BANK, (t + 1) * P)
            for c in range(a, b):
                q.acquire("act", ("p", c))
            done = q.op("act", lambda e, i, n=n, lo=lo, hi=hi: e.activation(
                self.p[:, lo:hi], self.scores[:, lo:hi], ACT.Exp, bias=self.bias[:, t % 2:t % 2 + 1],
                accum_out=self.sums[:, t % 2, n:n + 1]))
            for c in range(a, b):
                q.release(("scores", c), done)
                q.release(("p written", c), done)
        q.release(("bias", t % 2), done)
        q.release(("sums written", t % 2), done)

    def invert(self, t, slot):
        q, n = self.q, min(3, t // 4 + 1)
        inv = self.inv[:, slot, t:t + 1]
        q.acquire("dve", ("sums written", t % 2))
        q.acquire("dve", ("inv", slot, t))
        if n > 1:
            q.op("dve", lambda e, i: e.tensor_reduce(inv, self.sums[:, t % 2, 0:n], AX.X, ALU.add))
            done = q.chain("dve", lambda e, i: e.reciprocal(inv, inv))
        else:
            done = q.op("dve", lambda e, i: e.reciprocal(inv, self.sums[:, t % 2, 0:1]))
        q.release(("sums", t % 2), done)
        q.release(("inv written", slot, t), done)

    def turn(self, t, b):
        q, n = self.q, min(4, t + 1 - 4 * b)
        buf = (t // 2) % 2
        q.acquire("pe", ("p written", b))
        bank, free = self.bank()
        for j in range(n):
            done = q.op("pe", lambda e, i, j=j: e.transpose(
                bank[:, j * P:(j + 1) * P], self.p[:, (4 * b + j) * P:(4 * b + j + 1) * P], self.core.ident[:]),
                tick=j == n - 1)
        q.release(("p", b), done)
        where = (slice(None), slice(4 * b, 4 * b + n), slice((t % 2) * P, (t % 2 + 1) * P))
        value = bank[:, 0:n * P].rearrange("p (a b) -> p a b", b=P)
        for e in ("act", "dve"):
            q.acquire(e, ("pt", buf, b, t % 2))
        s = split(q, "act", "dve", self.pt_hi[buf][where], self.pt_lo[buf][where], value, done)
        q.release(free, s)
        q.release(("pt written", buf, b, t % 2), s)


def values(core, att, g, w_hi, w_lo, v_hi, v_lo, ready):
    q = core.q
    q.wait("pe", *ready)
    bank, free = att.bank()
    for n in range(2):
        t = 2 * g + n
        done = products(q, bank[:, n * H:(n + 1) * H], [core.xt_hi[:, k, t * P:(t + 1) * P] for k in range(HK)],
                        [core.xt_lo[:, k, t * P:(t + 1) * P] for k in range(HK)], [(w_hi[:, k, :], w_lo[:, k, :]) for k in range(HK)])
    for e in ("act", "dve"):
        q.acquire(e, ("v", g))
    s = split(q, "act", "dve", v_hi[:, 2 * g:2 * g + 2, :], v_lo[:, 2 * g:2 * g + 2, :],
              bank.rearrange("p (a b) -> p a b", a=2), done)
    q.release(free, s)
    q.release(("v written", g), s)


def attention0_phase(core):
    q, nc, src = core.q, core.nc, core.src
    with ExitStack() as stack:
        att = Attention(core, stack)
        sb = att.sb
        raw = {n: sb("raw_" + n, [P, HK, w]) for n, w in (("ws", P), ("wa", P), ("wo0", H))}
        w_hi = {n: sb("hi_" + n, [P, HK, r.shape[2]], F32R) for n, r in raw.items()}
        w_lo = {n: sb("lo_" + n, [P, HK, r.shape[2]], F32R) for n, r in raw.items()}
        bo = sb("bo", [P, H])
        s4, a4 = sb("s4", [P, T], F32R), sb("a4", [P, T], F32R)
        v_hi, v_lo = sb("v_hi", [P, NT, H], F32R), sb("v_lo", [P, NT, H], F32R)
        q.begin()
        ready = {}
        for n, (name, scale) in enumerate((("ws", float(R0) ** -0.5), ("wa", None), ("wo0", None))):
            t = load(core, n, raw[name][:], src[name])
            ready[name] = split(q, "act", "dve", w_hi[name][:], w_lo[name][:], raw[name][:], t, scale)
        t_bo = load(core, 3, bo[:], src["bo"].partition_broadcast(P))
        for c in range(NCH):
            where = slice(c * CH, (c + 1) * CH)
            rights = [(core.xt_hi[:, k, where], core.xt_lo[:, k, where]) for k in range(HK)]
            for name, out, low in (("ws", s4, ((64, 128),)), ("wa", a4, ((32, 64), (96, 128)))):
                q.wait("pe", ready[name])
                bank, free = att.bank()
                done = products(q, bank, [w_hi[name][:, k, :] for k in range(HK)], [w_lo[name][:, k, :] for k in range(HK)], rights)
                q.wait("act", done)
                done = q.op("act", lambda e, i, out=out, bank=bank, where=where: e.activation(out[:, where], bank, ACT.Copy))
                q.wait("dve", done)
                for a, b in low:
                    done = q.op("dve", lambda e, i, a=a, b=b, out=out, bank=bank, where=where: e.tensor_tensor(
                        out[a:b, where], bank[a:b, :], as_f32(out[a:b, where]), ALU.subtract))
                q.release(free, done)
        q.wait("pe", done)

        def scores(t, c):
            att.qk(t, c, lambda n: [(s4[:, t * P:(t + 1) * P], a4[:, c * CH:c * CH + n])], ())

        def pv(t, j):
            buf = (t // 2) % 2
            q.acquire("pe", ("pt written", buf, j // 4, t % 2))
            q.acquire("pe", ("v written", j // 2))
            if j == 0:
                q.acquire("pe", "y")
            cols_ = slice((t % 2) * P, (t % 2 + 1) * P)
            done = products(q, att.y[:, 0:H], [att.pt_hi[buf][:, j, cols_]], [att.pt_lo[buf][:, j, cols_]],
                            [(v_hi[:, j, :], v_lo[:, j, :])], first=j == 0, last=j == t)
            q.release(("pt", buf, j // 4, t % 2), done)
            if j == t:
                q.wait("dve", done)
                q.acquire("dve", ("inv written", 0, t))
                done = q.op("dve", lambda e, i: e.scalar_tensor_tensor(
                    core.x[:, t, :], att.y[:, 0:H], att.inv[:, 0, t:t + 1], core.x[:, t, :], ALU.mult, ALU.add))
                q.release("y", done)
                q.chain("dve", lambda e, i: e.tensor_tensor(core.x[:, t, :], core.x[:, t, :], bo[:], ALU.add))

        q.wait("dve", t_bo)
        scores(0, 0)
        att.peak(0)
        att.exps(0)
        for t in range(NT + 1):
            if t < NT and t % 2 == 0:
                values(core, att, t // 2, w_hi["wo0"], w_lo["wo0"], v_hi, v_lo, [ready["wo0"]])
            work = [(t - 1, j) for j in range(t)]
            last_b = (t + 1) // 4 if t + 1 < NT else t // 4
            for b in range(last_b + 1 if t < NT else 0):
                if b <= t // 4:
                    att.turn(t, b)
                if t + 1 < NT and b <= (t + 1) // 4:
                    scores(t + 1, b)
                for _ in range(2):
                    if work:
                        pv(*work.pop(0))
            if t + 1 < NT:
                att.peak(t + 1)
                att.exps(t + 1)
            if t < NT:
                att.invert(t, 0)
            for w in work:
                pv(*w)
        q.emit()


def attention1_phase(core):
    q, nc, src = core.q, core.nc, core.src
    with ExitStack() as stack:
        att = Attention(core, stack)
        sb = att.sb
        rope = sb("rope", [P, T])
        raw_qk, raw_wv, raw_wo = sb("raw_qk", [P, HK, 2, P]), sb("raw_wv", [P, HK, H]), sb("raw_wo", [P, H])
        qk_hi, qk_lo = (sb(n, [P, HK, 2, P], F32R) for n in ("qk_hi", "qk_lo"))
        wv_hi, wv_lo = (sb(n, [P, HK, H], F32R) for n in ("wv_hi", "wv_lo"))
        wo_hi, wo_lo = (sb(n, [P, H], F32R) for n in ("wo_hi", "wo_lo"))
        k_hi, k_lo = (sb(n, [P, T], F32R) for n in ("k_hi", "k_lo"))
        q_hi, q_lo = (sb(n, [P, 2, 2 * P], F32R) for n in ("q_hi", "q_lo"))
        v_hi, v_lo = (sb(n, [P, NT, 2 * DH], F32R) for n in ("v_hi", "v_lo"))
        y_hi, y_lo = (sb(n, [P, 2 * P], F32R) for n in ("y_hi", "y_lo"))
        part = sb("part", [P, 2, H])
        straight, crossed, rot = sb("straight", [64, 2, 2 * P]), sb("crossed", [64, 2, 2 * P]), sb("rot", [P, 2, 2 * P])
        G = NT // 2

        def weights(name, n, raw, w_hi, w_lo, pick, scale=None):
            q.acquire("sp", name + " raw")
            t = q.op("sp", lambda e, i: e.dma_start(raw[:], pick(i)), flow=core.loads[n])
            for e in ("act", "dve"):
                q.acquire(e, name)
            s = split(q, "act", "dve", w_hi[:], w_lo[:], raw[:], t, scale)
            q.release(name + " raw", s)
            q.release(name + " split", s)

        def weights_of(slot, ahead):
            head = lambda i: src["qk"][bass.ds(2 * i + slot + 2 * ahead, 1)].rearrange("a p k j d -> p (a k) j d")
            weights("qk", 0, raw_qk, qk_hi, qk_lo, head)
            if slot == 0:
                weights("wv", 1, raw_wv, wv_hi, wv_lo,
                        lambda i: src["wv"][bass.ds(i + ahead, 1)].rearrange("a p k d -> p (a k) d"))

        def pool(fn):
            q.wait("pool", q.last("pool")) if q.own["pool"].per.get(q.section) else q.acquire("pool", "pool idle")
            t = q.op("pool", fn)
            q.release("pool idle", t)
            return t

        def project(g):
            q.acquire("pe", "qk split")
            bank, free = att.bank()
            where = slice(2 * P * g, 2 * P * (g + 1))
            rights = [(core.xt_hi[:, k, where], core.xt_lo[:, k, where]) for k in range(HK)]
            both = bank.rearrange("p (a b) -> p a b", a=2)
            for j in range(2):
                done = products(q, both[:, j, :], [qk_hi[:, k, j, :] for k in range(HK)], [qk_lo[:, k, j, :] for k in range(HK)], rights)
            q.release("qk", done)
            q.wait("dve", done)
            q.acquire("dve", "crossed")
            wide = lambda rows: rope[rows, where].unsqueeze(1).broadcast_to([rows.stop - rows.start, 2, 2 * P])
            q.op("dve", lambda e, i: e.tensor_tensor(crossed[0:32], both[32:64], wide(slice(96, 128)), ALU.mult))
            t_cross = q.op("dve", lambda e, i: e.tensor_tensor(crossed[32:64], both[0:32], wide(slice(64, 96)), ALU.mult))
            q.wait("act", t_cross)
            q.acquire("act", "rot")
            q.acquire("act", "rot q")
            t_rot = q.op("act", lambda e, i: e.activation(rot[:], both, ACT.Copy))
            q.release(free, t_rot)
            q.wait("pool", t_rot, t_cross)
            pool(lambda e, i: e.tensor_tensor(straight[:], rot[0:64], wide(slice(0, 64)), ALU.mult))
            t_add = pool(lambda e, i: e.tensor_tensor(rot[0:64], straight[:], crossed[:], ALU.add))
            q.release("crossed", t_add)
            q.release("turned by rope", t_add)

        def finish(g, serial):
            cur, where = serial % 2, slice(2 * P * g, 2 * P * (g + 1))
            q.acquire("act", "turned by rope")
            q.acquire("act", ("q", cur))
            q.acquire("act", ("k", g))
            q.op("act", lambda e, i: e.activation(q_hi[:, cur, :], rot[:, 0, :], ACT.Copy, scale=float(DH) ** -0.5))
            t_hi = q.op("act", lambda e, i: e.activation(k_hi[:, where], rot[:, 1, :], ACT.Copy))
            q.wait("dve", t_hi)
            q.wait("pool", t_hi)
            q.acquire("dve", ("q", cur))
            q.acquire("pool", ("k", g))
            t_q = q.op("dve", lambda e, i: e.scalar_tensor_tensor(
                q_lo[:, cur, :], rot[:, 0, :], float(DH) ** -0.5, as_f32(q_hi[:, cur, :]), ALU.mult, ALU.subtract))
            t_k = pool(lambda e, i: e.tensor_tensor(k_lo[:, where], rot[:, 1, :], as_f32(k_hi[:, where]), ALU.subtract))
            q.release("rot q", t_q)
            q.release("rot", t_k)
            q.release(("q written", cur), t_q)
            q.release(("k written", g), t_k)

        def scores(t, c, serial):
            cur, g = serial % 2, t // 2
            q.acquire("pe", ("q written", cur))
            q.acquire("pe", ("k written", g))
            left = slice((t % 2) * P, (t % 2 + 1) * P)
            def pairs(n):
                right = slice(c * CH, c * CH + n)
                a, b = q_hi[:, cur, left], q_lo[:, cur, left]
                return [(a, k_hi[:, right]), (a, k_lo[:, right]), (b, k_hi[:, right])]
            att.qk(t, c, pairs, ())
            done = q.last("pe")
            q.release(("q", cur), done)
            for g in range(2 * c, min(2 * c + 2, t // 2 + 1)):
                q.release(("k", g), done)

        def clear(g):
            buf = g % 2
            q.acquire("act", ("pt", buf, (2 * g + 1) // 4, 0))
            for pt in (att.pt_hi, att.pt_lo):
                t = q.op("act", lambda e, i, pt=pt: e.activation(pt[buf][:, 2 * g + 1, 0:P], core.ident[:], ACT.Copy, scale=0.0))
            q.release(("cleared", buf), t)

        def pv(g, j, slot):
            buf, v = g % 2, slice(slot * DH, (slot + 1) * DH)
            for half in range(2):
                if half or j <= 2 * g:
                    q.acquire("pe", ("pt written", buf, j // 4, half))
            if j == 2 * g + 1:
                q.acquire("pe", ("cleared", buf))
            q.acquire("pe", ("v written", j // 2))
            if j == 0:
                q.acquire("pe", "y")
            done = products(q, att.y[:, 0:2 * P], [v_hi[:, j, v]], [v_lo[:, j, v]],
                            [(att.pt_hi[buf][:, j, :], att.pt_lo[buf][:, j, :])], first=j == 0, last=j == 2 * g + 1)
            for half in range(2):
                q.release(("pt", buf, j // 4, half), done)
            q.release(("v", j // 2), done)
            if j == 2 * g + 1:
                for e in ("act", "dve"):
                    q.acquire(e, "y halves")
                s = split(q, "act", "dve", y_hi[:], y_lo[:], att.y[:, 0:2 * P], done)
                q.release("y", s)
                q.release("y written", s)

        def out(g, slot):
            q.acquire("pe", "y written")
            q.acquire("pe", "wo split")
            bank, free = att.bank()
            for n in range(2):
                done = products(q, bank[:, n * H:(n + 1) * H], [y_hi[:, n * P:(n + 1) * P]], [y_lo[:, n * P:(n + 1) * P]],
                                [(wo_hi[:], wo_lo[:])])
            q.release("y halves", done)
            q.release("wo", done)
            q.wait("act", done)
            q.acquire("act", "part")
            for n in range(2):
                t = 2 * g + n
                q.acquire("act", ("inv written", slot, t))
                done = q.op("act", lambda e, i, n=n, t=t: e.activation(
                    part[:, n, :], bank[:, n * H:(n + 1) * H], ACT.Copy, scale=att.inv[:, slot, t:t + 1]))
                q.release(("inv", slot, t), done)
            q.release(free, done)
            q.wait("pool", done)
            rows = core.x[:, 2 * g:2 * g + 2, :]
            done = pool(lambda e, i: e.tensor_tensor(rows, rows, part[:], ALU.add))
            q.release("part", done)

        serial = 0
        pending = [(G - 1, j, 1) for j in range(NT)]

        def head(slot):
            nonlocal serial
            for t in range(NT):
                g = t // 2
                if t == NT - 3:
                    weights_of(1 - slot, slot)
                if t % 2 == 0:
                    clear(g)
                more = (t + 1) % NT
                steps = max(t // 4 + (LAG if more else 0), more // 4) + 1
                fill, after = [], []
                if t == 3:
                    fill.append((12, lambda: out(G - 1, 1 - slot)))
                    fill.append((0, lambda: weights("wo", 2, raw_wo, wo_hi, wo_lo, lambda i: src["wo1"][
                        bass.ds(2 * i + slot, 1)].rearrange("a d n -> d (a n)"), 1.0 / 3.0)))
                elif t % 2 == 0 and t != 2:
                    fill.append((12, (lambda: out(g - 2, slot)) if g else (lambda: out(G - 2, 1 - slot))))
                for _ in range(SUMS[t]):
                    fill.append((3, lambda p=pending.pop(0): pv(*p)))
                if t % 2 == 1:
                    pending.extend((g, j, slot) for j in range(2 * g + 2))
                if t % 2 == 0 and g + 2 < G:
                    after.append((24, lambda: project(g + 2)))
                if t >= NT - 2:
                    after.append((24, lambda: project(t - (NT - 2))))
                ahead = len(after)
                if t % 2 == 1 and slot == 0:
                    if g == 0:
                        q.acquire("pe", "wv split")
                    def value():
                        values(core, att, g, wv_hi, wv_lo, v_hi, v_lo, [])
                        if g == G - 1:
                            q.release("wv", q.last("pe"))
                    after.append((24, value))
                early = max(0, sum(w for w, _ in fill + after) - COVER)
                given = 0
                for b in range(steps):
                    if more:
                        if b <= more // 4:
                            scores(more, b, serial + t % 2)
                        if b == more // 4:
                            att.peak(more)
                        if 0 <= b - LAG <= t // 4:
                            att.turn(t, b - LAG)
                    else:
                        att.turn(t, b)
                        if b == steps - 2:
                            finish(0, serial + 1)
                        if b == steps - 1:
                            scores(0, 0, serial + 1)
                            att.peak(0)
                    if t % 2 == 0 and g + 1 < G and b == 0:
                        finish(g + 1, serial + 1)
                    while fill and given + fill[0][0] / 2 < early * (b + 1) / steps:
                        given += fill[0][0]
                        fill.pop(0)[1]()
                att.exps(more)
                att.invert(t, slot)
                for _, what in after[:ahead] + fill + after[ahead:]:
                    what()
                if t % 2 == 1:
                    serial += 1

        q.begin()
        t = load(core, 3, rope[:], src["rope"])
        q.wait("dve", t)
        q.wait("pool", t)
        weights_of(0, 0)
        pool(lambda e, i: e.memset(as_f32(att.pt_hi[1][:]), 0.0))
        pool(lambda e, i: e.memset(as_f32(att.pt_lo[1][:]), 0.0))
        for b in (v_hi, v_lo):
            q.op("dve", lambda e, i, b=b: e.memset(as_f32(b[:]), 0.0))
        for b in (as_f32(wo_hi[:]), as_f32(wo_lo[:]), as_f32(y_hi[:]), as_f32(y_lo[:]), att.inv[:]):
            pool(lambda e, i, b=b: e.memset(b, 0.0))
        project(0)
        finish(0, 0)
        project(1)
        scores(0, 0, 0)
        att.peak(0)
        att.exps(0)
        q.meet()
        first = att.rung
        q.begin(NH // 2)
        for slot in range(2):
            head(slot)
        assert serial % 2 == 0 and (att.rung - first) % 3 == 0
        q.begin()
        out(G - 2, 1)
        for p in pending:
            pv(*p)
        out(G - 1, 1)
        q.emit()


class Routes:

    def __init__(self, core, stack):
        sb, _ = core.rooms(stack)
        self.rows = sb("rows", [P, NE], I32)
        self.weight = sb("weight", [P, NE])
        self.tokens = sb("tokens", [P, NE, H])
        self.zero = sb("zero", [P, 4, H])


def router_phase(core, routes):
    q, nc, src = core.q, core.nc, core.src
    with ExitStack() as stack:
        sb, psum = core.rooms(stack)
        ps, ps_rank, ps_slot = psum("logits", [P, NT, NE]), psum("rank", [P, NT, NE]), psum("slot", [P, NE, 8])
        raw, w_hi, w_lo = sb("raw", [P, HK, NE]), sb("w_hi", [P, HK, NE], F32R), sb("w_lo", [P, HK, NE], F32R)
        below, ones, slots = sb("below", [P, P], BF16), sb("ones", [P, P], BF16), sb("slots", [P, P], BF16)
        row_id, tile_id = sb("row_id", [P, 1]), sb("tile_id", [P, NT])
        score, sel, eq, a, b = (sb(n, [P, NT, NE]) for n in ("score", "sel", "eq", "a", "b"))
        rank = sb("rank_all", [P, NT, NE])
        best = sb("best", [P, NT, 8])
        m1, m2 = sb("m1", [P, NT]), sb("m2", [P, NT])
        sel_b, before_b = sb("sel_b", [P, NT, NE], BF16), sb("before_b", [P, NT, NE], BF16)
        info = sb("info", [P, NT, NE, 6], BF16)
        hot = sb("hot", [P, 2, NT, P], BF16)
        got = sb("got", [P, NE, 8])
        s1, s2 = sb("s1", [P, NE]), sb("s2", [P, NE])
        wide = lambda ap: ap.unsqueeze(2).broadcast_to([P, NT, NE])
        q.begin()
        zeroed = q.op("pool", lambda e, i: e.memset(routes.zero[:], 0.0))
        q.chain("pool", lambda e, i: e.memset(ones[:], 1.0))
        ready_pool = q.last("pool")
        t_raw = load(core, 0, raw[:], src["gate0"])
        consts = [load(core, n, out[:], src[name]) for n, out, name in (
            (1, below, "below_b"), (2, slots, "slots_b"), (3, row_id, "row_id"), (4, tile_id, "tile_id"))]
        q.wait("sp", zeroed)
        stores = [load(core, 8 + c, core.y_rows[c * CH:(c + 1) * CH, :].rearrange("(t p) h -> p t h", p=P), routes.zero[:])
                  for c in range(NCH)]
        stores.append(load(core, 12, core.y_rows[T:T + CAP, :], routes.zero[:, 0, :]))
        stores.append(load(core, 13, core.xn_rows[T:T + CAP, :], routes.zero[:, 0, :]))
        ready = split(q, "act", "dve", w_hi[:], w_lo[:], raw[:], t_raw)
        q.wait("pe", ready)
        for t in range(NT):
            where = slice(t * P, (t + 1) * P)
            done = products(q, ps[:, t, :], [core.xt_hi[:, k, where] for k in range(HK)], [core.xt_lo[:, k, where] for k in range(HK)],
                            [(w_hi[:, k, :], w_lo[:, k, :]) for k in range(HK)])
        V = lambda fn: q.chain("dve", fn)
        q.wait("dve", done, *consts)
        V(lambda e, i: e.tensor_reduce(m1[:], ps[:], AX.X, ALU.max))
        t_sub = V(lambda e, i: e.tensor_tensor(score[:], ps[:], wide(m1[:]), ALU.subtract))
        q.wait("act", t_sub)
        t_exp = q.op("act", lambda e, i: e.activation(score[:], score[:], ACT.Exp))
        q.wait("dve", t_exp)
        V(lambda e, i: e.tensor_reduce(m1[:], score[:], AX.X, ALU.add))
        V(lambda e, i: e.reciprocal(m1[:], m1[:]))
        t_score = V(lambda e, i: e.tensor_tensor(score[:], score[:], wide(m1[:]), ALU.mult))
        q.wait("dve", t_score)
        for t in range(NT):
            q.op("dve", lambda e, i, t=t: e.max(best[:, t, :], score[:, t, :]))
        V(lambda e, i: e.tensor_reduce(m2[:], best[:, :, 0:TOPK], AX.X, ALU.add))
        V(lambda e, i: e.tensor_tensor(sel[:], score[:], wide(best[:, :, TOPK - 1]), ALU.is_gt))
        V(lambda e, i: e.tensor_tensor(eq[:], score[:], wide(best[:, :, TOPK - 1]), ALU.is_equal))
        V(lambda e, i: e.tensor_reduce(m1[:], sel[:], AX.X, ALU.add))
        cur, other = eq, a
        for step in (1, 2, 4, 8):
            V(lambda e, i, cur=cur, other=other, step=step: e.tensor_tensor(
                other[:, :, step:], cur[:, :, step:], cur[:, :, :NE - step], ALU.add))
            V(lambda e, i, cur=cur, other=other, step=step: e.tensor_copy(other[:, :, :step], cur[:, :, :step]))
            cur, other = other, (b if other is a else a)
        V(lambda e, i: e.tensor_tensor(cur[:], cur[:], wide(m1[:]), ALU.add))
        V(lambda e, i: e.tensor_scalar(cur[:], cur[:], TOPK + 0.5, None, ALU.is_lt))
        V(lambda e, i: e.tensor_tensor(cur[:], cur[:], eq[:], ALU.mult))
        V(lambda e, i: e.tensor_tensor(sel[:], sel[:], cur[:], ALU.add))
        V(lambda e, i: e.tensor_scalar(m2[:], m2[:], 1e-20, None, ALU.add))
        V(lambda e, i: e.reciprocal(m2[:], m2[:]))
        V(lambda e, i: e.tensor_tensor(score[:], score[:], wide(m2[:]), ALU.mult))
        V(lambda e, i: e.tensor_scalar(score[:], score[:], 0.5, None, ALU.mult))
        for n in range(3, 6):
            V(lambda e, i, n=n: e.tensor_copy(info[:, :, :, n], score[:]))
            if n < 5:
                V(lambda e, i, n=n: e.tensor_tensor(score[:], score[:], info[:, :, :, n], ALU.subtract))
        V(lambda e, i: e.tensor_scalar(info[:, :, :, 0], sel[:], 0.0, row_id[:], ALU.mult, ALU.add))
        V(lambda e, i: e.tensor_copy(info[:, :, :, 1], wide(tile_id[:])))
        V(lambda e, i: e.memset(info[:, :, :, 2], 1.0))
        V(lambda e, i: e.tensor_copy(sel_b[:], sel[:]))
        V(lambda e, i: e.memset(before_b[:, 0, :], 0.0))
        for t in range(1, NT):
            V(lambda e, i, t=t: e.tensor_tensor(before_b[:, t, :], before_b[:, t - 1, :], sel_b[:, t - 1, :], ALU.add))
        q.wait("pe", q.last("dve"), ready_pool)
        q.op("pe", lambda e, i: e.matmul(ps_rank[:], below[:], sel_b[:], start=True, stop=False), tick=False)
        t_rank = q.op("pe", lambda e, i: e.matmul(ps_rank[:], ones[:], before_b[:], start=False, stop=True))
        V(lambda e, i: e.tensor_scalar(rank[:], sel[:], -4.0 * T, 4.0 * T, ALU.mult, ALU.add))
        q.wait("dve", t_rank)
        V(lambda e, i: e.tensor_tensor(rank[:], rank[:], ps_rank[:], ALU.add))
        q.meet()

        q.begin(NE // 2)
        for n in range(2):
            q.acquire("dve", ("hot", n))
            for t in range(NT):
                rank_of = lambda i, t=t, n=n: rank[:, t, bass.ds(2 * i + n, 1)]
                done = q.op("dve", lambda e, i, t=t, n=n, rank_of=rank_of: e.tensor_scalar(
                    hot[:, n, t, :], slots[:], rank_of(i), None, ALU.is_equal))
            q.wait("pe", done)
            for t in range(NT):
                done = q.op("pe", lambda e, i, t=t, n=n: e.matmul(
                    ps_slot[:, bass.ds(2 * i + n, 1), 0:6].rearrange("p a b -> p (a b)"), hot[:, n, t, :],
                    info[:, t, bass.ds(2 * i + n, 1), :].rearrange("p a b -> p (a b)"),
                    start=t == 0, stop=t == NT - 1), tick=t == NT - 1)
            q.release(("hot", n), done)

        q.begin()
        q.wait("dve", done)
        V(lambda e, i: e.tensor_copy(got[:, :, 0:6], ps_slot[:, :, 0:6]))
        V(lambda e, i: e.tensor_scalar(s1[:], got[:, :, 1], float(P), float(T), ALU.mult, ALU.add))
        V(lambda e, i: e.tensor_tensor(s1[:], s1[:], got[:, :, 0], ALU.add))
        V(lambda e, i: e.tensor_scalar(s2[:], got[:, :, 2], -1.0, 1.0, ALU.mult, ALU.add))
        V(lambda e, i: e.tensor_scalar(s2[:], s2[:], row_id[:], None, ALU.mult))
        V(lambda e, i: e.tensor_tensor(routes.rows[:], s1[:], s2[:], ALU.add))
        V(lambda e, i: e.tensor_tensor(s1[:], got[:, :, 3], got[:, :, 4], ALU.add))
        V(lambda e, i: e.tensor_tensor(routes.weight[:], s1[:], got[:, :, 5], ALU.add))
        q.wait("sp", *stores)
        q.emit()


def fetch_tokens(core, routes):
    q = core.q
    done = [q.op("pool", lambda e, i, n=n: e.indirect_dma_start(
        routes.tokens[:, n, :], None, core.xn_rows, bass.IndirectOffsetOnAxis(ap=routes.rows[:, n:n + 1], axis=0)),
        flow=core.gather_out[n]) for n in range(NE)]
    return done


def experts_phase(core, routes):
    q, nc, src = core.q, core.nc, core.src
    IK = I0P // P
    with ExitStack() as stack:
        sb, psum = core.rooms(stack)
        turned = psum("turned", [P, 2, BANK])
        gu = psum("gu", [P, 2, BANK])
        turned_h = psum("turned_h", [P, 2, BANK])
        down = psum("down", [P, 2, BANK])
        raw_up, raw_dn = sb("raw_up", [P, 2, HK, 2 * I0]), sb("raw_dn", [P, 2, IK, H])
        up_hi, up_lo = (sb(n, [P, 2, HK, 2 * I0], F32R) for n in ("up_hi", "up_lo"))
        dn_hi, dn_lo = (sb(n, [P, 2, IK, H], F32R) for n in ("dn_hi", "dn_lo"))
        x_hi, x_lo = (sb(n, [P, 2, HK, P], F32R) for n in ("x_hi", "x_lo"))
        h_hi, h_lo = (sb(n, [P, 2, IK, P], F32R) for n in ("h_hi", "h_lo"))
        gate, h = sb("gate", [P, 2, I0]), sb("h", [P, 2, I0P])
        rows = sb("rows_out", [P, NE, H])
        q.begin()
        q.op("dve", lambda e, i: e.memset(h[:], 0.0))

        def up(s, e_of):
            q.acquire("sp", ("raw", s))
            q.acquire("sp", ("raw2", s))
            t_up = q.op("sp", lambda e, i: e.dma_start(raw_up[:, s], src["expert_up"][bass.ds(e_of(i), 1)].rearrange("a p k n -> p (a k) n")),
                        flow=core.loads[2 * s])
            t_dn = q.op("sp", lambda e, i: e.dma_start(raw_dn[:, s], src["expert_down"][bass.ds(e_of(i), 1)].rearrange("a p k n -> p (a k) n")),
                        flow=core.loads[2 * s + 1])
            q.acquire("act", ("w", s))
            q.acquire("dve", ("w", s))
            q.acquire("pool", ("w", s))
            t_w = split(q, "act", "pool", up_hi[:, s], up_lo[:, s], raw_up[:, s], t_up)
            t_w2 = split(q, "act", "dve", dn_hi[:, s], dn_lo[:, s], raw_dn[:, s], t_dn)
            q.acquire("pe", ("turned", s))
            token = lambda i, k: routes.tokens[:, bass.ds(e_of(i), 1), k * P:(k + 1) * P].rearrange("p a b -> p (a b)")
            stage = x_raw[:, s]
            q.acquire("dve", ("x_raw", s))
            done = q.op("dve", lambda e, i: e.tensor_copy(stage, routes.tokens[:, bass.ds(e_of(i), 1), :].rearrange("p a b -> p (a b)")))
            q.wait("pe", done)
            for k in range(HK):
                done = q.op("pe", lambda e, i, k=k: e.transpose(turned[:, s, k * P:(k + 1) * P], stage[:, k * P:(k + 1) * P], core.ident[:]),
                            tick=k == HK - 1)
            q.release(("x_raw", s), done)
            q.acquire("act", ("x", s))
            q.acquire("dve", ("x", s))
            t_x = split(q, "act", "dve", x_hi[:, s], x_lo[:, s], turned[:, s, 0:HK * P].rearrange("p (a b) -> p a b", a=HK), done)
            q.release(("turned", s), t_x)
            q.wait("pe", t_x, t_w, t_w2)
            q.acquire("pe", ("gu", s))
            done = products(q, gu[:, s, 0:2 * I0], [x_hi[:, s, k] for k in range(HK)], [x_lo[:, s, k] for k in range(HK)],
                            [(up_hi[:, s, k], up_lo[:, s, k]) for k in range(HK)])
            q.release(("x", s), done)
            q.wait("act", done)
            q.acquire("act", ("gate", s))
            t_g = q.op("act", lambda e, i: e.activation(gate[:, s], gu[:, s, 0:I0], ACT.Silu))
            q.wait("dve", t_g)
            q.acquire("dve", ("h", s))
            t_h = q.op("dve", lambda e, i: e.tensor_tensor(h[:, s, 0:I0], gu[:, s, I0:2 * I0], gate[:, s], ALU.mult))
            q.release(("gate", s), t_h)
            q.release(("gu", s), t_h)
            q.release(("h written", s), t_h)
            q.release(("raw", s), t_w)
            q.release(("raw2", s), t_w2)

        def dn(s, e_of):
            q.acquire("pe", ("h written", s))
            q.acquire("pe", ("turned_h", s))
            for k in range(IK):
                done = q.op("pe", lambda e, i, k=k: e.transpose(turned_h[:, s, k * P:(k + 1) * P], h[:, s, k * P:(k + 1) * P], core.ident[:]),
                            tick=k == IK - 1)
            q.release(("h", s), done)
            q.acquire("act", ("ht", s))
            q.acquire("dve", ("ht", s))
            t_h = split(q, "act", "dve", h_hi[:, s], h_lo[:, s], turned_h[:, s, 0:IK * P].rearrange("p (a b) -> p a b", a=IK), done)
            q.release(("turned_h", s), t_h)
            q.wait("pe", t_h)
            q.acquire("pe", ("down", s))
            done = products(q, down[:, s, 0:H], [h_hi[:, s, k] for k in range(IK)], [h_lo[:, s, k] for k in range(IK)],
                            [(dn_hi[:, s, k], dn_lo[:, s, k]) for k in range(IK)])
            q.release(("ht", s), done)
            q.release(("w", s), done)
            q.wait("dve", done)
            t_o = q.op("dve", lambda e, i: e.tensor_scalar(
                rows[:, bass.ds(e_of(i), 1), :].rearrange("p a b -> p (a b)"), down[:, s, 0:H],
                routes.weight[:, bass.ds(e_of(i), 1)], None, ALU.mult))
            q.release(("down", s), t_o)
            return t_o

        x_raw = sb("x_raw", [P, 2, H])
        q.wait("dve", *routes.fetched)
        up(0, lambda i: 0)
        q.meet()
        q.begin(NE // 2 - 1)
        up(1, lambda i: 2 * i + 1)
        outs = [dn(0, lambda i: 2 * i)]
        up(0, lambda i: 2 * i + 2)
        outs.append(dn(1, lambda i: 2 * i + 1))
        q.begin()
        up(1, lambda i: NE - 1)
        late = [dn(0, lambda i: NE - 2), dn(1, lambda i: NE - 1)]
        for n in range(NE):
            if n < NE - 2:
                q.wait_turn("pool", outs[n % 2], n // 2)
            else:
                q.wait("pool", late[n - (NE - 2)])
            done = q.op("pool", lambda e, i, n=n: e.indirect_dma_start(
                core.y_rows, bass.IndirectOffsetOnAxis(ap=routes.rows[:, n:n + 1], axis=0), rows[:, n, :], None, compute_op=ALU.add),
                flow=core.add_out[n % 2])
            q.wait("pool", done)
        q.emit()


def ffn0_block(core):
    with ExitStack() as stack:
        routes = Routes(core, stack)
        router_phase(core, routes)

        def beside(_):
            routes.fetched = fetch_tokens(core, routes)

        ffn_phase(core, core.src["shared_up"], core.src["shared_down"], IS, extra=beside)
        experts_phase(core, routes)


def program(nc, src, out):
    with ExitStack() as stack:
        q = Queues(nc, stack)
        core = Core(nc, stack, q, src)
        ffn1 = lambda: ffn_phase(core, src["up1"], src["down1"], I1, (src["gs1"], src["us1"], src["ds1"]))
        start_phase(core)
        layernorm_phase(core, keep_rows=True)
        ffn0_block(core)
        layernorm_phase(core, add_y=True)
        attention0_phase(core)
        layernorm_phase(core, keep_rows=True)
        ffn0_block(core)
        layernorm_phase(core, add_y=True)
        ffn1()
        layernorm_phase(core)
        attention1_phase(core)
        layernorm_phase(core)
        ffn1()
        q.begin()
        q.wait("sp", load(core, 0, out.rearrange("(t p) h -> p t h", p=P), core.x[:]))
        q.emit()



def _tables():
    fraction = np.linspace(0.0, 1.0, DH // 4, dtype=np.float32)
    af = np.power(np.float32(1.0 / 1024.0), fraction).astype(np.float32)
    theta = (np.arange(T, dtype=np.float32)[None, :] * af[:, None]).astype(np.float32)
    cos, sin = np.cos(theta).astype(np.float32), np.sin(theta).astype(np.float32)
    bf = mybir.dt.np(BF16)
    r = np.arange(P)
    return {
        "rope": np.concatenate([cos, cos, -sin, sin]),
        "ident": np.eye(P, dtype=np.float32),
        "ident_b": np.eye(P, dtype=bf),
        "mask_b": np.where(r[None, :] > r[:, None], NEG, 0.0).astype(bf),
        "below_b": (r[:, None] < r[None, :]).astype(bf),
        "slots_b": np.broadcast_to(r[None, :], (P, P)).astype(bf),
        "row_id": r[:, None].astype(np.float32),
        "tile_id": np.broadcast_to(np.arange(NT)[None, :] - NT, (P, NT)).astype(np.float32),
    }


def _wide(w):
    return w.reshape(-1, P, w.shape[-1]).transpose(1, 0, 2)


def _pad(w, rows, width):
    out = np.zeros((*w.shape[:-2], rows, width), w.dtype)
    out[..., :w.shape[-2], :w.shape[-1]] = w
    return out


def _layouts(i):
    a = {k: np.asarray(v) for k, v in i.items()}
    out = {"x": a["L0_attn_x"][0]}
    out["gate0"] = _wide(a["L0_ffn_gate_w"].T)
    up = np.concatenate([a["L0_ffn_w_gate"], a["L0_ffn_w_up"]], axis=-1)
    out["expert_up"] = up.reshape(NE, HK, P, 2 * I0).transpose(0, 2, 1, 3)
    out["expert_down"] = _pad(a["L0_ffn_w_down"], I0P, H).reshape(NE, I0P // P, P, H).transpose(0, 2, 1, 3)
    g, u = _pad(a["L0_ffn_sw_gate"], H, ISM * P), _pad(a["L0_ffn_sw_up"], H, ISM * P)
    out["shared_up"] = _wide(np.stack([g.reshape(H, ISM, P), u.reshape(H, ISM, P)], axis=2).reshape(H, -1))
    out["shared_down"] = _wide(_pad(a["L0_ffn_sw_down"], ISM * P, H))
    out["ws"], out["wa"] = (_wide(np.tile(a[n], (1, P // R0))) for n in ("L0_attn_Ws", "L0_attn_Wa"))
    out["wo0"] = _wide(a["L0_attn_Wo"].T)
    out["bo"] = a["L0_attn_bo"][None, :]
    turn = np.concatenate([np.arange(0, 32), np.arange(64, 96), np.arange(32, 64), np.arange(96, 128)])
    qk = np.stack([a[n].reshape(NH, DH, H)[:, turn, :] for n in ("L1_attn_Wq", "L1_attn_Wk")], axis=1)
    out["qk"] = qk.reshape(NH, 2, DH, HK, P).transpose(0, 4, 3, 1, 2)
    out["qk"] = np.concatenate([out["qk"], np.zeros_like(out["qk"][:2])])
    out["wv"] = a["L1_attn_Wv"].reshape(NH // 2, 2 * DH, HK, P).transpose(0, 3, 2, 1)
    out["wv"] = np.concatenate([out["wv"], np.zeros_like(out["wv"][:1])])
    out["wo1"] = a["L1_attn_Wo"].reshape(H, NH, DH).transpose(1, 2, 0)
    full = (I1 // P) * P
    g, u = a["L1_ffn_gate_w"].T, a["L1_ffn_up_w"].T
    both = np.stack([g[:, :full].reshape(H, -1, P), u[:, :full].reshape(H, -1, P)], axis=2).reshape(H, -1)
    out["up1"] = _wide(np.concatenate([both, g[:, full:], u[:, full:]], axis=1))
    out["down1"] = _wide(_pad(a["L1_ffn_down_w"].T, I1M * P, H))
    gs, us = (_pad(a[n].reshape(1, I1), 1, I1M * P).reshape(I1M, P).T for n in ("L1_ffn_gate_s", "L1_ffn_up_s"))
    us = us.copy()
    us[P // 2:, -1] = us[:P // 2, -1]
    out["gs1"], out["us1"], out["ds1"] = gs, us, a["L1_ffn_down_s"][None, :]
    return out


def kernel(**inputs):
    from concourse import bacc
    from concourse.bass_utils import run_bass_kernel_spmd

    nc = bacc.Bacc("TRN2", target_bir_lowering=False, num_devices=1)
    arrays = {n: np.ascontiguousarray(a) for n, a in {**_layouts(inputs), **_tables()}.items()}
    src = {n: nc.dram_tensor(n, a.shape, mybir.dt.from_np(a.dtype), kind="ExternalInput").ap() for n, a in arrays.items()}
    out = nc.dram_tensor("out", (T, H), F32, kind="ExternalOutput").ap()
    program(nc, src, out)
    r = run_bass_kernel_spmd(nc, [arrays], core_ids=[0])
    return r.results[0]["out"].reshape(1, T, H)
```

```python
from contextlib import ExitStack

import numpy as np

import concourse.bass as bass
from concourse import mybir
from concourse.alu_op_type import AluOpType as ALU

F32 = mybir.dt.float32
F32R = mybir.dt.float32r
BF16 = mybir.dt.bfloat16
I32 = mybir.dt.int32
U32 = mybir.dt.uint32
ACT = mybir.ActivationFunctionType
AX = mybir.AxisListType

P = 128
H = 256
HK = H // P
T = 2048
NT = T // P
CH = 512
NCH = T // CH
BANK = 512
EPS = 1e-5

NE, TOPK, CAP = 16, 4, 128
I0 = 176
I0P = 256
IS = 352
ISM = 3
TRASH = T

R0 = 32
NH, DH = 16, 128
I1 = 704
I1M = 6
CREDIT = 1024
NEG = -1e30


class Flow:

    def __init__(self, sem, step):
        self.sem, self.step, self.before, self.per = sem, step, {}, {}
        self.total = 0


class Tick:

    def __init__(self, section, flow, k):
        self.section, self.flow, self.k = section, flow, k


class Section:

    def __init__(self, times):
        self.times, self.items, self.named = times, {}, {}


class Queues:

    ENGINES = ("pe", "act", "dve", "pool", "sp")

    def __init__(self, nc, stack):
        self.nc, self.stack = nc, stack
        self.own = {e: self.flow(f"done_{e}", 1) for e in self.ENGINES}
        self.waited = self.flow("waited", 1)
        self.sections, self.section = [], None

    def flow(self, name, step):
        return Flow(self.stack.enter_context(self.nc.semaphore(name)), step)

    def credit(self, flow):
        flow.total += CREDIT
        return Flow(flow.sem, CREDIT)

    def begin(self, times=1):
        self.section = Section(times)
        self.sections.append(self.section)
        self.seen = {}

    def op(self, engine, fn, flow=None, tick=True, name=None):
        if not tick:
            self.section.items.setdefault(engine, []).append((fn, None))
            return None
        flow = flow or self.own[engine]
        k = flow.per.get(self.section, 0) + flow.step
        flow.per[self.section] = k
        self.section.items.setdefault(engine, []).append((fn, flow))
        t = Tick(self.section, flow, k)
        if name is not None:
            self.section.named[name] = t
        return t

    def last(self, engine):
        flow = self.own[engine]
        return Tick(self.section, flow, flow.per.get(self.section, 0))

    def wait(self, engine, *ticks):
        for t in ticks:
            if t is None:
                continue
            key = (engine, t.flow)
            old = self.seen.get(key)
            if old is not None and old[0] is t.section and old[1] >= t.k:
                continue
            self.seen[key] = (t.section, t.k)
            self.section.items.setdefault(engine, []).append((t, None))

    def wait_before(self, engine, name):
        self.section.items.setdefault(engine, []).append((name, -1))

    def release(self, name, tick):
        self.section.named[name] = tick

    def acquire(self, engine, name):
        if name in self.section.named:
            self.wait(engine, self.section.named[name])
        elif self.section.times > 1:
            self.wait_before(engine, name)
        elif len(self.sections) > 1 and name in self.sections[-2].named:
            self.wait(engine, self.sections[-2].named[name])

    def meet(self):
        for e in self.ENGINES:
            self.wait(e, *(self.last(other) for other in ("pe", "act", "dve", "pool") if self.own[other].per.get(self.section)))

    def chain(self, engine, fn, **kw):
        self.wait(engine, self.last(engine))
        return self.op(engine, fn, **kw)

    def emit(self):
        nc = self.nc
        for s in self.sections:
            for f in {t for e in s.items.values() for _, t in e if isinstance(t, Flow)}:
                f.before[s] = f.total
                f.total += s.times * f.per[s]

        def strongest(s, items):
            kept, row = [], {}
            for what, extra in items:
                if callable(what):
                    kept += [*(item for _, item in row.values()), (what, extra)]
                    row = {}
                    continue
                t = s.named[what] if extra == -1 else what
                f, own = t.flow, t.section is s
                turn = -1 if extra == -1 else extra if extra is not None else 0 if own else t.section.times - 1
                reach = own and s.times > 1, f.before[t.section] + turn * f.per[t.section] + t.k
                if t.flow not in row or reach > row[t.flow][0]:
                    row[t.flow] = reach, (what, extra)
            return kept + [item for _, item in row.values()]

        def run(engine, name):
            for s in self.sections:
                items = s.items.get(name)
                if not items:
                    continue

                def body(i):
                    for what, extra in strongest(s, items):
                        if isinstance(what, Tick):
                            f = what.flow
                            turn = extra if extra is not None else i if what.section is s else what.section.times - 1
                            engine.wait_ge(f.sem, turn * f.per[what.section] + f.before[what.section] + what.k)
                        elif extra == -1:
                            t = s.named[what]
                            f = t.flow
                            engine.wait_ge(f.sem, i * f.per[s] + f.before[s] + t.k - f.per[s])
                        else:
                            ins = what(engine, i)
                            if extra is not None:
                                ins.then_inc(extra.sem, extra.step)
                        if not callable(what) and name in ("sp", "pool") and s.times > 1:
                            engine.sem_inc(self.waited.sem, 1)

                if s.times == 1:
                    body(0)
                else:
                    with engine.Fori(0, s.times) as i:
                        body(i)

        with nc.Block() as block:
            block.tensor(lambda eng: run(eng, "pe"))
            block.scalar(lambda eng: run(eng, "act"))
            block.vector(lambda eng: run(eng, "dve"))
            block.gpsimd(lambda eng: run(eng, "pool"))
            block.sync(lambda eng: run(eng, "sp"))
        self.sections = []


def cols(ap, start, n):
    return ap[:, bass.ds(start, n)]


def as_f32(ap):
    return ap.bitcast(F32)


class Core:

    def __init__(self, nc, stack, q, src):
        self.nc, self.q, self.src, self.phase = nc, q, src, 0
        sb = lambda name, shape, dt: stack.enter_context(nc.sbuf_tensor("sb_" + name, shape, dt))
        self.x = sb("x", [P, NT, H], F32)
        self.xt_hi = sb("xt_hi", [P, HK, T], F32R)
        self.xt_lo = sb("xt_lo", [P, HK, T], F32R)
        self.ident = sb("ident", [P, P], F32)
        self.ident_b = sb("ident_b", [P, P], BF16)
        self.mask_b = sb("mask_b", [P, P], BF16)
        self.arriving = []
        self.stores = []
        self.loads = [q.flow(f"load_{n}", 16) for n in range(28)]
        self.gather_out = [q.flow(f"gather_{n}", 16) for n in range(NE)]
        self.add_out = [q.flow(f"add_{n}", 16) for n in range(2)]
        self.xn_rows = nc.dram_tensor("xn_rows", (T + CAP, H), F32).ap()
        self.y_rows = nc.dram_tensor("y_rows", (T + CAP, H), F32).ap()


    def rooms(self, stack):
        self.phase += 1
        tag = f"phase{self.phase}_"
        return (lambda name, shape, dt=F32: stack.enter_context(self.nc.sbuf_tensor(tag + name, shape, dt)),
                lambda name, shape, dt=F32: stack.enter_context(self.nc.psum_tensor(tag + name, shape, dt)))


def load(core, n, out, src):
    return core.q.op("sp", lambda e, i: e.dma_start(out, src), flow=core.loads[n])


def split(q, hi_engine, lo_engine, hi, lo, value, ready, scale=None):
    q.wait(hi_engine, ready)
    if hi_engine == "act":
        t = q.op("act", lambda e, i: e.activation(hi, value, ACT.Copy, scale=1.0 if scale is None else scale))
    elif scale is None:
        t = q.op(hi_engine, lambda e, i: e.tensor_copy(hi, value))
    else:
        t = q.op(hi_engine, lambda e, i: e.tensor_scalar(hi, value, scale, None, ALU.mult))
    q.wait(lo_engine, ready, t)
    if scale is None:
        return q.op(lo_engine, lambda e, i: e.tensor_tensor(lo, value, as_f32(hi), ALU.subtract))
    return q.op(lo_engine, lambda e, i: e.scalar_tensor_tensor(lo, value, scale, as_f32(hi), ALU.mult, ALU.subtract))


def products(q, out, left_hi, left_lo, rights, first=True, last=True):
    n = len(rights)
    for c, (r_hi, r_lo) in enumerate(rights):
        for p, (a, b) in enumerate(((left_hi[c], r_hi), (left_hi[c], r_lo), (left_lo[c], r_hi))):
            s, e = first and c == 0 and p == 0, last and c == n - 1 and p == 2
            t = q.op("pe", (lambda a, b, s, e: lambda eng, i: eng.matmul(
                out(i) if callable(out) else out, a, b(i) if callable(b) else b, start=s, stop=e))(a, b, s, e),
                tick=c == n - 1 and p == 2)
    return t


def start_phase(core):
    q, c, src = core.q, core, core.src
    q.begin()
    for engine, flow in q.own.items():
        q.op(engine, lambda e, i: e.nop(), flow=q.credit(flow))
    rows = src["x"].rearrange("(t p) h -> p t h", p=P)
    core.arriving = [load(core, 24 + n, c.x[:, 4 * n:4 * n + 4, :], rows[:, 4 * n:4 * n + 4, :]) for n in range(4)]
    constants = [load(core, 5 + n, out[:], src[name]) for n, (out, name) in enumerate((
        (c.ident, "ident"), (c.ident_b, "ident_b"), (c.mask_b, "mask_b")))]
    q.wait("pe", constants[0])
    core.stores = constants


def normalise(core, sb, banks, xn=None, add_y=False, keep_rows=False, between=lambda: None):
    q = core.q
    xn = sb("ln_xn", [P, NT, H])[:] if xn is None else xn
    room = xn.shape[1]
    stats, mv = sb("ln_stats", [P, NT, 6]), sb("ln_mv", [P, NT, 2])
    var, root, rstd, tmp = (sb(f"ln_{n}", [P, NT]) for n in ("var", "root", "rstd", "tmp"))
    halves = (slice(0, NT // 2), slice(NT // 2, NT))
    freed, added = [], {}
    if add_y:
        rows = core.y_rows[0:T, :].rearrange("(t p) h -> p t h", p=P)
        loads = [load(core, 20 + c, xn[:, 4 * c:4 * c + 4, :], rows[:, 4 * c:4 * c + 4, :]) for c in range(4)]

    def measure(half):
        tiles = range(NT)[half]
        if core.arriving:
            q.wait("dve", *core.arriving[tiles.start // 4:tiles.stop // 4])
        if add_y:
            for c in range(tiles.start // 4, tiles.stop // 4):
                here = xn[:, 4 * c:4 * c + 4, :], core.x[:, 4 * c:4 * c + 4, :]
                engine = ("dve", "pool")[c % 2]
                q.wait(engine, loads[c], q.last(engine) if engine == "pool" else None)
                added[c] = q.op(engine, lambda e, i, h=here: e.tensor_tensor(h[1], h[1], h[0], ALU.add))
        for t in tiles:
            q.wait("dve", added.get(t // 4))
            q.op("dve", lambda e, i, t=t: e.bn_stats(stats[:, t, :], core.x[:, t, :]))
        q.wait("dve", q.last("dve"))
        for t in tiles:
            q.op("dve", lambda e, i, t=t: e.bn_aggr(mv[:, t, :], stats[:, t, :]))
        ready = q.chain("dve", lambda e, i: e.tensor_scalar(var[:, half], mv[:, half, 1], EPS, None, ALU.add))
        q.wait("act", ready)
        return q.op("act", lambda e, i: e.activation(root[:, half], var[:, half], ACT.Sqrt))

    def scale(half, rooted):
        q.wait("dve", rooted)
        q.op("dve", lambda e, i: e.reciprocal(rstd[:, half], root[:, half]))
        q.chain("dve", lambda e, i: e.tensor_tensor(tmp[:, half], rstd[:, half], rstd[:, half], ALU.mult))
        q.chain("dve", lambda e, i: e.tensor_tensor(tmp[:, half], tmp[:, half], var[:, half], ALU.mult))
        q.chain("dve", lambda e, i: e.tensor_scalar(tmp[:, half], tmp[:, half], -0.5, 1.5, ALU.mult, ALU.add))
        inverse = q.chain("dve", lambda e, i: e.tensor_tensor(rstd[:, half], rstd[:, half], tmp[:, half], ALU.mult))
        normed = {}
        for t in range(NT)[half]:
            q.wait("dve", inverse, freed[-1] if freed and room < NT else None)
            normed[t] = q.op("dve", lambda e, i, t=t: e.tensor_scalar(
                xn[:, t % room, :], core.x[:, t, :], mv[:, t, 0:1], rstd[:, t:t + 1], ALU.subtract, ALU.mult))
        return normed

    def turn(c, normed):
        for k in range(HK):
            bank = banks[(HK * c + k) % 4]
            if len(freed) >= 4:
                q.wait("pe", freed[-4])
            q.wait("pe", normed[4 * c + 3])
            for j in range(4):
                done = q.op("pe", lambda e, i, k=k, bank=bank, j=j: e.transpose(
                    bank[:, j * P:(j + 1) * P], xn[:, (4 * c + j) % room, k * P:(k + 1) * P], core.ident[:]), tick=j == 3)
            where = slice(c * CH, (c + 1) * CH)
            freed.append(split(q, "act", "dve", core.xt_hi[:, k, where], core.xt_lo[:, k, where], bank, done))

    rooted = [measure(half) for half in halves]
    core.arriving = []
    between()
    for n, half in enumerate(halves):
        normed = scale(half, rooted[n])
        for c in range(2 * n, 2 * n + 2):
            turn(c, normed)
            if keep_rows:
                q.wait("sp", normed[4 * c + 3])
                t = load(core, 20 + c, core.xn_rows[0:T, :].rearrange("(t p) h -> p t h", p=P)[:, 4 * c:4 * c + 4, :],
                         xn[:, 4 * c:4 * c + 4, :])
                core.stores.append(t)
    return freed[-1]


def ffn_phase(core, up_src, down_src, width, scales=None, add_y=False, result=None):
    q, nc, merged = core.q, core.nc, scales is not None
    pairs = width // P if merged else -(-width // P)
    pieces = pairs + merged
    n_up = (2 * pairs + merged) * P
    with ExitStack() as stack:
        sb, psum = core.rooms(stack)
        ps = psum("ps", [P, 8, BANK])
        up_hi, up_lo = (sb(n, [P, HK, n_up], F32R) for n in ("up_hi", "up_lo"))
        dn_hi, dn_lo = (sb(n, [P, pieces, H], F32R) for n in ("dn_hi", "dn_lo"))
        raw_up, raw_dn = sb("raw_up", [P, HK, n_up]), sb("raw_dn", [P, pieces, H])
        h_hi, h_lo = (sb(n, [P, pieces, CH], F32R) for n in ("h_hi", "h_lo"))
        gate, act = sb("gate", [P, 2, CH]), sb("act", [P, 2, CH])
        q.begin()
        ready = []
        if merged:
            gs, us, ds, tmp = sb("gs", [P, pieces]), sb("us", [P, pieces]), sb("ds", [P, H]), sb("tmp", [P, 2, H])
            s_t = [load(core, 3, gs[:], scales[0]), load(core, 4, us[:], scales[1]),
                   load(core, 5, ds[:], scales[2].partition_broadcast(P))]
        up_t = [load(core, k, raw_up[:, k, :], up_src[:, k, :]) for k in range(HK)]
        dn_t = load(core, 2, raw_dn[:], down_src)

        def prepare():
            for k in range(HK):
                ready.append(split(q, "act", "pool", up_hi[:, k, :], up_lo[:, k, :], raw_up[:, k, :], up_t[k]))
            ready.append(split(q, "act", "pool", dn_hi[:], dn_lo[:], raw_dn[:], dn_t))
            if merged:
                q.wait("dve", *s_t)
                q.wait("act", *s_t)
                ready.append(q.op("dve", lambda e, i: e.tensor_scalar(ds[:], ds[:], 0.5, None, ALU.mult)))
                ready.append(q.chain("pool", lambda e, i: e.memset(as_f32(h_hi[64:P, pieces - 1, :]), 0.0)))
                ready.append(q.op("pool", lambda e, i: e.memset(as_f32(h_lo[64:P, pieces - 1, :]), 0.0)))

        ready.append(normalise(core, sb, [ps[:, 4 + n, :] for n in range(4)], add_y=add_y, between=prepare))
        q.wait("pe", *ready)
        q.wait("dve", *ready)
        q.begin(NCH)
        xt = lambda src, k: (lambda i: src[:, k, bass.ds(i * CH, CH)])
        rights = [(xt(core.xt_hi, k), xt(core.xt_lo, k)) for k in range(HK)]
        split_h = []
        acted = []
        for m in range(pieces):
            half = merged and m == pieces - 1
            rows = slice(0, 64) if half else slice(0, P)
            banks = (m % 2, 2 + m % 2)
            if m >= 2:
                q.wait("pe", acted[m - 2])
            else:
                q.wait_before("pe", ("act", pieces - 1))
            for n, bank in enumerate(banks[:1] if half else banks):
                at = (2 * m + n) * P
                done = products(q, ps[:, bank, :], [up_hi[:, k, at:at + P] for k in range(HK)],
                                [up_lo[:, k, at:at + P] for k in range(HK)], rights)
            g = ps[rows, banks[0], :]
            u = ps[64:P, banks[0], :] if half else ps[:, banks[1], :]
            q.wait("act", done)
            if m >= 2:
                q.wait("act", acted[m - 2])
            else:
                q.wait_before("act", ("act", pieces - 1))
            g_t = q.op("act", lambda e, i, g=g, m=m, rows=rows: e.activation(
                gate[rows, m % 2, :], g, ACT.Silu, scale=gs[rows, m:m + 1] if merged else 1.0))
            q.wait("dve", g_t)
            if m >= 2:
                q.wait("dve", split_h[m - 2])
            else:
                q.wait_before("dve", ("split", pieces - 1))
            urow = slice(64, P) if half else slice(0, P)
            acted.append(q.op("dve", lambda e, i, u=u, m=m, rows=rows, urow=urow: e.scalar_tensor_tensor(
                act[rows, m % 2, :], u, us[urow, m:m + 1] if merged else 1.0, gate[rows, m % 2, :], ALU.mult, ALU.mult),
                name=("act", m)))
            q.wait("pool", q.last("pool")) if m else q.wait_before("pool", ("split", pieces - 1))
            q.wait_before("act", ("down", pieces - 1))
            q.wait_before("pool", ("down", pieces - 1))
            s = split(q, "act", "pool", h_hi[rows, m, :], h_lo[rows, m, :], act[rows, m % 2, :], acted[-1])
            q.section.named[("split", m)] = s
            split_h.append(s)
        q.wait_before("pe", "added")
        for m in range(pieces):
            q.wait("pe", split_h[m])
            for j in range(4):
                t = products(q, ps[:, 4 + j, 0:H], [h_hi[:, m, j * P:(j + 1) * P]], [h_lo[:, m, j * P:(j + 1) * P]],
                             [(dn_hi[:, m, :], dn_lo[:, m, :])], first=m == 0, last=m == pieces - 1)
            q.section.named[("down", m)] = t
        for j in range(4):
            q.wait("dve", t)
            row = lambda i, j=j: core.x[:, bass.ds(i * 4 + j, 1), :].rearrange("p a h -> p (a h)")
            if merged:
                q.wait("dve", q.last("dve"))
                q.op("dve", lambda e, i, j=j: e.tensor_tensor(tmp[:, j % 2, :], ps[:, 4 + j, 0:H], ds[:], ALU.mult))
                q.chain("dve", lambda e, i, j=j, row=row: e.tensor_tensor(row(i), row(i), tmp[:, j % 2, :], ALU.add), name="added")
            else:
                q.op("dve", lambda e, i, j=j, row=row: e.scalar_tensor_tensor(
                    row(i), ps[:, 4 + j, 0:H], 0.5, row(i), ALU.mult, ALU.add), name="added")
        if result is not None:
            q.wait("sp", q.section.named["added"])
            q.op("sp", lambda e, i: e.dma_start(
                result.rearrange("(c t p) h -> c p t h", p=P, t=4)[bass.ds(i, 1)].rearrange("a p t h -> p (a t) h"),
                core.x[:, bass.ds(i * 4, 4), :]), flow=core.loads[6])
            stored = Tick(q.section, core.loads[6], 16)
            q.begin()
            q.wait("sp", stored)
        q.emit()


KEEP = 3
COVER = 29
LAG = 1

SUMS = (4, 6, 6, 2, 0, 4, 2, 4, 3, 5, 4, 6, 6, 6, 6, 8)


class Attention:

    def __init__(self, core, stack):
        self.core, self.q = core, core.q
        sb, psum = core.rooms(stack)
        self.sb = sb
        self.scores = psum("scores", [P, 4 * BANK])
        self.ring = psum("ring", [P, 3, BANK])
        self.y = psum("y", [P, BANK])
        self.p = sb("p", [P, T])
        self.pt_hi, self.pt_lo = ([sb(f"pt_{n}{b}", [P, NT - 2 * (b == 0), 2 * P], F32R) for b in range(2)] for n in ("hi", "lo"))
        self.peaks, self.bias = sb("peaks", [P, 2, 4]), sb("bias", [P, 2])
        self.sums = sb("sums", [P, 2, 4])
        self.inv = sb("inv", [P, 2, NT])
        self.rung = 0
        self.chunk, self.places = 0, {}

    def bank(self):
        n, self.rung = self.rung % 3, self.rung + 1
        self.q.acquire("pe", ("ring", n))
        return self.ring[:, n, :], ("ring", n)

    def qk(self, t, c, pairs, ready):
        q = self.q
        diag = c == t // 4
        n = max(256, (t % 4 + 1) * P) if diag else BANK
        bank, self.chunk = self.chunk % 4, self.chunk + 1
        self.places[t] = (self.places[t] if c else []) + [bank]
        out = self.scores[:, bank * BANK:bank * BANK + n]
        q.wait("pe", *ready)
        q.acquire("pe", ("scores", bank))
        products_ = pairs(n)
        for k, (a, b) in enumerate(products_):
            done = q.op("pe", lambda e, i, a=a, b=b, k=k: e.matmul(
                out, a, b, start=k == 0, stop=k == len(products_) - 1),
                tick=k == len(products_) - 1)
        if diag:
            at = bank * BANK + t % 4 * P
            done = q.op("pe", lambda e, i: e.matmul(self.scores[:, at:at + P], self.core.ident_b[:], self.core.mask_b[:],
                                                    start=False, stop=True, skip_group_check=True))
        width = (t % 4 + 1) * P if diag else BANK
        q.wait("dve", done)
        q.op("dve", lambda e, i: e.tensor_reduce(self.peaks[:, t % 2, c:c + 1],
                                                 self.scores[:, bank * BANK:bank * BANK + width], AX.X, ALU.max))

    def peak(self, t):
        q, chunks = self.q, t // 4 + 1
        q.wait("dve", q.last("dve"))
        q.acquire("dve", ("bias", t % 2))
        done = q.op("dve", lambda e, i: e.tensor_reduce(self.bias[:, t % 2:t % 2 + 1], self.peaks[:, t % 2, 0:chunks],
                                                          AX.X, ALU.max, negate=True))
        q.release(("bias written", t % 2), done)

    def exps(self, t):
        q, chunks = self.q, t // 4 + 1
        q.acquire("act", ("bias written", t % 2))
        q.acquire("act", ("sums", t % 2))
        for c, bank in enumerate(self.places[t]):
            width = min(BANK, (t + 1) * P - c * BANK)
            q.acquire("act", ("p", bank))
            done = q.op("act", lambda e, i, c=c, bank=bank, width=width: e.activation(
                self.p[:, bank * BANK:bank * BANK + width], self.scores[:, bank * BANK:bank * BANK + width], ACT.Exp,
                bias=self.bias[:, t % 2:t % 2 + 1], accum_out=self.sums[:, t % 2, c:c + 1]))
            q.release(("scores", bank), done)
            q.release(("p written", bank), done)
        q.release(("bias", t % 2), done)
        q.release(("sums written", t % 2), done)

    def invert(self, t, slot):
        q, n = self.q, t // 4 + 1
        inv = self.inv[:, slot, t:t + 1]
        q.acquire("dve", ("sums written", t % 2))
        q.acquire("dve", ("inv", slot, t))
        if n > 1:
            q.op("dve", lambda e, i: e.tensor_reduce(inv, self.sums[:, t % 2, 0:n], AX.X, ALU.add))
            done = q.chain("dve", lambda e, i: e.reciprocal(inv, inv))
        else:
            done = q.op("dve", lambda e, i: e.reciprocal(inv, self.sums[:, t % 2, 0:1]))
        q.release(("sums", t % 2), done)
        q.release(("inv written", slot, t), done)

    def turn(self, t, b):
        q, n = self.q, min(4, t + 1 - 4 * b)
        buf = (t // 2) % 2
        place = self.places[t][b]
        q.acquire("pe", ("p written", place))
        bank, free = self.bank()
        for j in range(n):
            done = q.op("pe", lambda e, i, j=j: e.transpose(
                bank[:, j * P:(j + 1) * P], self.p[:, (4 * place + j) * P:(4 * place + j + 1) * P], self.core.ident[:]),
                tick=j == n - 1)
        q.release(("p", place), done)
        where = (slice(None), slice(4 * b, 4 * b + n), slice((t % 2) * P, (t % 2 + 1) * P))
        value = bank[:, 0:n * P].rearrange("p (a b) -> p a b", b=P)
        for e in ("act", "dve"):
            q.acquire(e, ("pt", buf, b, t % 2))
        s = split(q, "act", "dve", self.pt_hi[buf][where], self.pt_lo[buf][where], value, done)
        q.release(free, s)
        q.release(("pt written", buf, b, t % 2), s)


def values(core, att, g, w_hi, w_lo, v_hi, v_lo, ready):
    q = core.q
    q.wait("pe", *ready)
    bank, free = att.bank()
    for n in range(2):
        t = 2 * g + n
        done = products(q, bank[:, n * H:(n + 1) * H], [core.xt_hi[:, k, t * P:(t + 1) * P] for k in range(HK)],
                        [core.xt_lo[:, k, t * P:(t + 1) * P] for k in range(HK)], [(w_hi[:, k, :], w_lo[:, k, :]) for k in range(HK)])
    for e in ("act", "dve"):
        q.acquire(e, ("v", g))
    s = split(q, "act", "dve", v_hi[:, 2 * g:2 * g + 2, :], v_lo[:, 2 * g:2 * g + 2, :],
              bank.rearrange("p (a b) -> p a b", a=2), done)
    q.release(free, s)
    q.release(("v written", g), s)


def attention0_phase(core, add_y=False):
    q, nc, src = core.q, core.nc, core.src
    with ExitStack() as stack:
        att = Attention(core, stack)
        sb = att.sb
        raw = {n: sb("raw_" + n, [P, HK, w]) for n, w in (("ws", P), ("wa", P), ("wo0", H))}
        w_hi = {n: sb("hi_" + n, [P, HK, r.shape[2]], F32R) for n, r in raw.items()}
        w_lo = {n: sb("lo_" + n, [P, HK, r.shape[2]], F32R) for n, r in raw.items()}
        bo = sb("bo", [P, H])
        s4, a4 = sb("s4", [P, T], F32R), sb("a4", [P, T], F32R)
        v_hi, v_lo = sb("v_hi", [P, NT, H], F32R), sb("v_lo", [P, NT, H], F32R)
        q.begin()
        ready = {}

        def prepare():
            for n, (name, scale) in enumerate((("ws", float(R0) ** -0.5), ("wa", None), ("wo0", None))):
                t = load(core, n, raw[name][:], src[name])
                ready[name] = split(q, "act", "dve", w_hi[name][:], w_lo[name][:], raw[name][:], t, scale)

        q.wait("pe", normalise(core, sb, [att.scores[:, n * BANK:(n + 1) * BANK] for n in range(4)], add_y=add_y, between=prepare))
        t_bo = load(core, 3, bo[:], src["bo"].partition_broadcast(P))

        def project(c):
            where = slice(c * CH, (c + 1) * CH)
            rights = [(core.xt_hi[:, k, where], core.xt_lo[:, k, where]) for k in range(HK)]
            for name, out, low in (("ws", s4, ((64, 128),)), ("wa", a4, ((32, 64), (96, 128)))):
                q.wait("pe", ready[name])
                bank, free = att.bank()
                done = products(q, bank, [w_hi[name][:, k, :] for k in range(HK)], [w_lo[name][:, k, :] for k in range(HK)], rights)
                q.wait("act", done)
                done = q.op("act", lambda e, i, out=out, bank=bank, where=where: e.activation(out[:, where], bank, ACT.Copy))
                q.wait("dve", done)
                for a, b in low:
                    done = q.op("dve", lambda e, i, a=a, b=b, out=out, bank=bank, where=where: e.tensor_tensor(
                        out[a:b, where], bank[a:b, :], as_f32(out[a:b, where]), ALU.subtract))
                q.release(free, done)
                q.release((name, c), done)

        for c in range(NCH):
            project(c)

        def scores(t, c):
            q.acquire("pe", ("ws", t // 4))
            q.acquire("pe", ("wa", c))
            att.qk(t, c, lambda n: [(s4[:, t * P:(t + 1) * P], a4[:, c * CH:c * CH + n])], ())

        def pv(t, j):
            buf = (t // 2) % 2
            q.acquire("pe", ("pt written", buf, j // 4, t % 2))
            q.acquire("pe", ("v written", j // 2))
            if j == 0:
                q.acquire("pe", "y")
            cols_ = slice((t % 2) * P, (t % 2 + 1) * P)
            done = products(q, att.y[:, 0:H], [att.pt_hi[buf][:, j, cols_]], [att.pt_lo[buf][:, j, cols_]],
                            [(v_hi[:, j, :], v_lo[:, j, :])], first=j == 0, last=j == t)
            q.release(("pt", buf, j // 4, t % 2), done)
            if j == t:
                q.wait("dve", done)
                q.acquire("dve", ("inv written", 0, t))
                done = q.op("dve", lambda e, i: e.scalar_tensor_tensor(
                    core.x[:, t, :], att.y[:, 0:H], att.inv[:, 0, t:t + 1], core.x[:, t, :], ALU.mult, ALU.add))
                q.release("y", done)
                q.chain("dve", lambda e, i: e.tensor_tensor(core.x[:, t, :], core.x[:, t, :], bo[:], ALU.add))

        q.wait("dve", t_bo)
        scores(0, 0)
        att.peak(0)
        att.exps(0)
        for t in range(NT + 1):
            if t < NT and t % 2 == 0:
                values(core, att, t // 2, w_hi["wo0"], w_lo["wo0"], v_hi, v_lo, [ready["wo0"]])
            work = [(t - 1, j) for j in range(t)]
            more = t + 1 if t + 1 < NT else None
            lag = LAG if t > 2 else 0
            steps = 0 if t == NT else max(t // 4 + lag, (more or 0) // 4) + 1
            early = max(0, len(work) - COVER // 4)
            for b in range(steps):
                if more and b <= more // 4:
                    scores(more, b)
                    if b == more // 4:
                        att.peak(more)
                if 0 <= b - lag <= t // 4:
                    att.turn(t, b - lag)
                while work and t - len(work) < early * (b + 1) // steps:
                    pv(*work.pop(0))
            if more:
                att.exps(more)
            if t < NT:
                att.invert(t, 0)
            for w in work:
                pv(*w)
        q.emit()


def attention1_phase(core):
    q, nc, src = core.q, core.nc, core.src
    with ExitStack() as stack:
        att = Attention(core, stack)
        sb = att.sb
        rope = sb("rope", [P, T])
        raw_qk, raw_wv, raw_wo = sb("raw_qk", [P, HK, 2, P]), sb("raw_wv", [P, HK, H]), sb("raw_wo", [P, H])
        qk_hi, qk_lo = (sb(n, [P, HK, 2, P], F32R) for n in ("qk_hi", "qk_lo"))
        wv_hi, wv_lo = (sb(n, [P, HK, H], F32R) for n in ("wv_hi", "wv_lo"))
        wo_hi, wo_lo = (sb(n, [P, H], F32R) for n in ("wo_hi", "wo_lo"))
        k_hi, k_lo = (sb(n, [P, T], F32R) for n in ("k_hi", "k_lo"))
        q_hi, q_lo = (sb(n, [P, 2, 2 * P], F32R) for n in ("q_hi", "q_lo"))
        v_hi, v_lo = (sb(n, [P, NT, 2 * DH], F32R) for n in ("v_hi", "v_lo"))
        y_hi, y_lo = (sb(n, [P, 2 * P], F32R) for n in ("y_hi", "y_lo"))
        part = sb("part", [P, 2, H])
        straight, crossed, rot = sb("straight", [64, 2, 2 * P]), sb("crossed", [64, 2, 2 * P]), sb("rot", [P, 2, 2 * P])
        G = NT // 2

        def weights(name, n, raw, w_hi, w_lo, pick, scale=None):
            q.acquire("sp", name + " raw")
            t = q.op("sp", lambda e, i: e.dma_start(raw[:], pick(i)), flow=core.loads[n])
            for e in ("act", "dve"):
                q.acquire(e, name)
            s = split(q, "act", "dve", w_hi[:], w_lo[:], raw[:], t, scale)
            q.release(name + " raw", s)
            q.release(name + " split", s)

        def weights_of(slot, ahead):
            head = lambda i: src["qk"][bass.ds(2 * i + slot + 2 * ahead, 1)].rearrange("a p k j d -> p (a k) j d")
            weights("qk", 0, raw_qk, qk_hi, qk_lo, head)
            if slot == 0:
                weights("wv", 1, raw_wv, wv_hi, wv_lo,
                        lambda i: src["wv"][bass.ds(i + ahead, 1)].rearrange("a p k d -> p (a k) d"))

        def pool(fn):
            q.wait("pool", q.last("pool")) if q.own["pool"].per.get(q.section) else q.acquire("pool", "pool idle")
            t = q.op("pool", fn)
            q.release("pool idle", t)
            return t

        def project(g):
            q.acquire("pe", "qk split")
            bank, free = att.bank()
            where = slice(2 * P * g, 2 * P * (g + 1))
            rights = [(core.xt_hi[:, k, where], core.xt_lo[:, k, where]) for k in range(HK)]
            both = bank.rearrange("p (a b) -> p a b", a=2)
            for j in range(2):
                done = products(q, both[:, j, :], [qk_hi[:, k, j, :] for k in range(HK)], [qk_lo[:, k, j, :] for k in range(HK)], rights)
            q.release("qk", done)
            q.wait("dve", done)
            q.acquire("dve", "crossed")
            wide = lambda rows: rope[rows, where].unsqueeze(1).broadcast_to([rows.stop - rows.start, 2, 2 * P])
            q.op("dve", lambda e, i: e.tensor_tensor(crossed[0:32], both[32:64], wide(slice(96, 128)), ALU.mult))
            t_cross = q.op("dve", lambda e, i: e.tensor_tensor(crossed[32:64], both[0:32], wide(slice(64, 96)), ALU.mult))
            q.wait("act", t_cross)
            q.acquire("act", "rot")
            q.acquire("act", "rot q")
            t_rot = q.op("act", lambda e, i: e.activation(rot[:], both, ACT.Copy))
            q.release(free, t_rot)
            q.wait("pool", t_rot, t_cross)
            pool(lambda e, i: e.tensor_tensor(straight[:], rot[0:64], wide(slice(0, 64)), ALU.mult))
            t_add = pool(lambda e, i: e.tensor_tensor(rot[0:64], straight[:], crossed[:], ALU.add))
            q.release("crossed", t_add)
            q.release("turned by rope", t_add)

        def finish(g, serial):
            cur, where = serial % 2, slice(2 * P * g, 2 * P * (g + 1))
            q.acquire("act", "turned by rope")
            q.acquire("act", ("q", cur))
            q.acquire("act", ("k", g))
            q.op("act", lambda e, i: e.activation(q_hi[:, cur, :], rot[:, 0, :], ACT.Copy, scale=float(DH) ** -0.5))
            t_hi = q.op("act", lambda e, i: e.activation(k_hi[:, where], rot[:, 1, :], ACT.Copy))
            q.wait("dve", t_hi)
            q.wait("pool", t_hi)
            q.acquire("dve", ("q", cur))
            q.acquire("pool", ("k", g))
            t_q = q.op("dve", lambda e, i: e.scalar_tensor_tensor(
                q_lo[:, cur, :], rot[:, 0, :], float(DH) ** -0.5, as_f32(q_hi[:, cur, :]), ALU.mult, ALU.subtract))
            t_k = pool(lambda e, i: e.tensor_tensor(k_lo[:, where], rot[:, 1, :], as_f32(k_hi[:, where]), ALU.subtract))
            q.release("rot q", t_q)
            q.release("rot", t_k)
            q.release(("q written", cur), t_q)
            q.release(("k written", g), t_k)

        def scores(t, c, serial):
            cur, g = serial % 2, t // 2
            q.acquire("pe", ("q written", cur))
            q.acquire("pe", ("k written", g))
            left = slice((t % 2) * P, (t % 2 + 1) * P)
            def pairs(n):
                right = slice(c * CH, c * CH + n)
                a, b = q_hi[:, cur, left], q_lo[:, cur, left]
                return [(a, k_hi[:, right]), (a, k_lo[:, right]), (b, k_hi[:, right])]
            att.qk(t, c, pairs, ())
            done = q.last("pe")
            q.release(("q", cur), done)
            for g in range(2 * c, min(2 * c + 2, t // 2 + 1)):
                q.release(("k", g), done)

        def clear(g):
            buf = g % 2
            q.acquire("act", ("pt", buf, (2 * g + 1) // 4, 0))
            for pt in (att.pt_hi, att.pt_lo):
                t = q.op("act", lambda e, i, pt=pt: e.activation(pt[buf][:, 2 * g + 1, 0:P], core.ident[:], ACT.Copy, scale=0.0))
            q.release(("cleared", buf), t)

        def pv(g, j, slot):
            buf, v = g % 2, slice(slot * DH, (slot + 1) * DH)
            for half in range(2):
                if half or j <= 2 * g:
                    q.acquire("pe", ("pt written", buf, j // 4, half))
            if j == 2 * g + 1:
                q.acquire("pe", ("cleared", buf))
            q.acquire("pe", ("v written", j // 2))
            if j == 0:
                q.acquire("pe", "y")
            done = products(q, att.y[:, 0:2 * P], [v_hi[:, j, v]], [v_lo[:, j, v]],
                            [(att.pt_hi[buf][:, j, :], att.pt_lo[buf][:, j, :])], first=j == 0, last=j == 2 * g + 1)
            for half in range(2):
                q.release(("pt", buf, j // 4, half), done)
            q.release(("v", j // 2), done)
            if j == 2 * g + 1:
                for e in ("act", "dve"):
                    q.acquire(e, "y halves")
                s = split(q, "act", "dve", y_hi[:], y_lo[:], att.y[:, 0:2 * P], done)
                q.release("y", s)
                q.release("y written", s)

        def out(g, slot):
            q.acquire("pe", "y written")
            q.acquire("pe", "wo split")
            bank, free = att.bank()
            for n in range(2):
                done = products(q, bank[:, n * H:(n + 1) * H], [y_hi[:, n * P:(n + 1) * P]], [y_lo[:, n * P:(n + 1) * P]],
                                [(wo_hi[:], wo_lo[:])])
            q.release("y halves", done)
            q.release("wo", done)
            q.wait("act", done)
            q.acquire("act", "part")
            for n in range(2):
                t = 2 * g + n
                q.acquire("act", ("inv written", slot, t))
                done = q.op("act", lambda e, i, n=n, t=t: e.activation(
                    part[:, n, :], bank[:, n * H:(n + 1) * H], ACT.Copy, scale=att.inv[:, slot, t:t + 1]))
                q.release(("inv", slot, t), done)
            q.release(free, done)
            q.wait("pool", done)
            rows = core.x[:, 2 * g:2 * g + 2, :]
            done = pool(lambda e, i: e.tensor_tensor(rows, rows, part[:], ALU.add))
            q.release("part", done)

        serial = 0
        pending = [(G - 1, j, 1) for j in range(NT)]

        def head(slot):
            nonlocal serial
            for t in range(NT):
                g = t // 2
                if t == NT - 3:
                    weights_of(1 - slot, slot)
                if t % 2 == 0:
                    clear(g)
                more = (t + 1) % NT
                lag = LAG if t > 2 and more else 0
                steps = max(t // 4 + lag, more // 4) + 1
                fill, after = [], []
                if t == 3:
                    fill.append((6, lambda: out(G - 1, 1 - slot)))
                    fill.append((0, lambda: weights("wo", 2, raw_wo, wo_hi, wo_lo, lambda i: src["wo1"][
                        bass.ds(2 * i + slot, 1)].rearrange("a d n -> d (a n)"), 1.0 / 3.0)))
                elif t % 2 == 0 and t != 2:
                    fill.append((6, (lambda: out(g - 2, slot)) if g else (lambda: out(G - 2, 1 - slot))))
                for _ in range(SUMS[t]):
                    fill.append((3, lambda p=pending.pop(0): pv(*p)))
                if t % 2 == 1:
                    pending.extend((g, j, slot) for j in range(2 * g + 2))
                if t % 2 == 0 and g + 2 < G:
                    after.append((12, lambda: project(g + 2)))
                if t >= NT - 2:
                    after.append((12, lambda: project(t - (NT - 2))))
                ahead = len(after)
                if t % 2 == 1 and slot == 0:
                    if g == 0:
                        q.acquire("pe", "wv split")
                    def value():
                        values(core, att, g, wv_hi, wv_lo, v_hi, v_lo, [])
                        if g == G - 1:
                            q.release("wv", q.last("pe"))
                    after.append((12, value))
                early = max(0, sum(w for w, _ in fill + after) - COVER) if more else 0
                given = 0
                for b in range(steps):
                    if more:
                        if b <= more // 4:
                            scores(more, b, serial + t % 2)
                        if b == more // 4:
                            att.peak(more)
                        if 0 <= b - lag <= t // 4:
                            att.turn(t, b - lag)
                    else:
                        att.turn(t, b)
                        if b == steps - 1:
                            finish(0, serial + 1)
                    if t % 2 == 0 and g + 1 < G and b == steps - 1:
                        finish(g + 1, serial + 1)
                    while fill and given + fill[0][0] / 2 < early * (b + 1) / steps:
                        given += fill[0][0]
                        fill.pop(0)[1]()
                if not more:
                    for _ in range(KEEP):
                        fill.pop(0)[1]()
                    for _, what in after:
                        what()
                    after = []
                    scores(0, 0, serial + 1)
                    att.peak(0)
                att.exps(more)
                att.invert(t, slot)
                for _, what in after[:ahead] + fill + after[ahead:]:
                    what()
                if t % 2 == 1:
                    serial += 1

        q.begin()
        t = load(core, 3, rope[:], src["rope"])
        def prepare():
            weights_of(0, 0)
            for b in (as_f32(wo_hi[:]), as_f32(wo_lo[:]), as_f32(y_hi[:]), as_f32(y_lo[:]), att.inv[:],
                      as_f32(att.pt_hi[1][:]), as_f32(att.pt_lo[1][:]), as_f32(v_hi[:]), as_f32(v_lo[:])):
                pool(lambda e, i, b=b: e.memset(b, 0.0))

        normed = normalise(core, sb, [att.scores[:, n * BANK:(n + 1) * BANK] for n in range(4)],
                           att.p[:].rearrange("p (t h) -> p t h", h=H), between=prepare)
        q.wait("pe", normed)
        q.wait("dve", t)
        q.wait("pool", t)
        project(0)
        finish(0, 0)
        project(1)
        scores(0, 0, 0)
        att.peak(0)
        att.exps(0)
        q.meet()
        first = att.rung
        q.begin(NH // 2)
        for slot in range(2):
            head(slot)
        assert serial % 2 == 0 and (att.rung - first) % 3 == 0 and (att.chunk - 1) % 4 == 0
        q.begin()
        out(G - 2, 1)
        for p in pending:
            pv(*p)
        out(G - 1, 1)
        q.emit()


class Routes:

    def __init__(self, core, stack):
        sb, _ = core.rooms(stack)
        self.rows = sb("rows", [P, NE])
        self.weight = sb("weight", [P, NE])
        self.zero = sb("zero", [P, 4, H])


def route_and_share(core, routes):
    q, nc, src = core.q, core.nc, core.src
    with ExitStack() as stack:
        sb, psum = core.rooms(stack)
        up_ps, down_ps = psum("up_ps", [P, 3, BANK]), psum("down_ps", [P, 4, BANK])
        route_ps = psum("route_ps", [P, 2, NT, NE])
        logits_ps, rank_ps = route_ps[:, 0], route_ps[:, 1]
        slot_ps = logits_ps
        raw, w_hi, w_lo = sb("raw", [P, HK, NE]), sb("w_hi", [P, HK, NE], F32R), sb("w_lo", [P, HK, NE], F32R)
        below, ones = sb("below", [P, P], BF16), sb("ones", [P, P], BF16)
        slots = sb("slots", [P, P, NT], BF16)
        row_id, tile_id = sb("row_id", [P, 1]), sb("tile_id", [P, NT])
        turned = sb("logits_t", [NE, T])
        score, sel, eq, a, b = (sb(n, [P, NT, NE]) for n in ("score", "sel", "eq", "a", "b"))
        rank, rank_b = sb("rank_all", [P, NT, NE]), sb("rank_b", [P, NE, NT], BF16)
        best = sb("best", [P, NT, 8])
        m1, m2 = sb("m1", [P, NT]), sb("m2", [P, NT])
        sel_b = sb("sel_b", [P, NT + 1, NE], BF16)
        info, info_e = sb("info", [P, NT, NE, 6], BF16), sb("info_e", [P, 4, NT, 6], BF16)
        hot = sb("hot", [P, 4, P, NT], BF16)
        got = sb("got", [P, NE, 8])
        none = sb("none", [P, 4, 6])
        s1, s2 = sb("s1", [P, NE]), sb("s2", [P, NE])
        wide = lambda ap: ap.unsqueeze(2).broadcast_to([P, NT, NE])
        n_up = 2 * ISM * P
        up_hi, up_lo = (sb(n, [P, HK, n_up], F32R) for n in ("up_hi", "up_lo"))
        dn_hi, dn_lo = (sb(n, [P, ISM, H], F32R) for n in ("dn_hi", "dn_lo"))
        raw_up, raw_dn = sb("raw_up", [P, HK, n_up]), sb("raw_dn", [P, ISM, H])
        h_hi, h_lo = (sb(n, [P, ISM, CH], F32R) for n in ("h_hi", "h_lo"))
        gate, up_sb, act, part = (sb(n, [P, 2, CH]) for n in ("gate", "up_sb", "act", "part"))

        q.begin()
        zeroed = q.op("pool", lambda e, i: e.memset(routes.zero[:], 0.0))
        ones_done = q.chain("pool", lambda e, i: e.memset(ones[:], 1.0))
        t_raw = load(core, 0, raw[:], src["gate0"])
        up_loads = [load(core, 14 + k, raw_up[:, k, :], src["shared_up"][:, k, :]) for k in range(HK)]
        down_load = load(core, 16, raw_dn[:], src["shared_down"])
        consts = [load(core, n, out[:], src[name]) for n, out, name in (
            (1, below, "below_b"), (2, slots, "slots_b"), (3, row_id, "row_id"), (4, tile_id, "tile_id"))]
        q.wait("sp", zeroed)
        stores = [load(core, 8 + c, core.y_rows[c * CH:(c + 1) * CH, :].rearrange("(t p) h -> p t h", p=P), routes.zero[:])
                  for c in range(NCH)]
        stores.append(load(core, 12, core.y_rows[T:T + CAP, :], routes.zero[:, 0, :]))
        stores.append(load(core, 13, core.xn_rows[T:T + CAP, :], routes.zero[:, 0, :]))
        ready = split(q, "act", "dve", w_hi[:], w_lo[:], raw[:], t_raw)
        q.wait("pe", ready, normalise(core, sb, [down_ps[:, n, :] for n in range(4)], keep_rows=True))
        for c in range(NCH):
            where = slice(c * CH, (c + 1) * CH)
            done = products(q, down_ps[0:NE, c, :], [w_hi[:, k, :] for k in range(HK)], [w_lo[:, k, :] for k in range(HK)],
                            [(core.xt_hi[:, k, where], core.xt_lo[:, k, where]) for k in range(HK)])
            q.wait("act", done)
            copied = q.op("act", lambda e, i, c=c, where=where: e.activation(turned[:, where], down_ps[0:NE, c, :], ACT.Copy))
        q.wait("pe", copied)
        for t in range(NT):
            logits = q.op("pe", lambda e, i, t=t: e.transpose(
                logits_ps[:, t, :], turned[:, t * P:(t + 1) * P], core.ident[0:NE, 0:NE]), tick=t == NT - 1)
        w_ready = [split(q, "act", "dve", up_hi[:, 0, :], up_lo[:, 0, :], raw_up[:, 0, :], up_loads[0]),
                   split(q, "act", "pool", up_hi[:, 1, :], up_lo[:, 1, :], raw_up[:, 1, :], up_loads[1]),
                   split(q, "act", "pool", dn_hi[:], dn_lo[:], raw_dn[:], down_load)]
        V = lambda fn: q.chain("dve", fn)
        q.wait("dve", logits, *consts)
        V(lambda e, i: e.tensor_reduce(m1[:], logits_ps, AX.X, ALU.max))
        t_sub = V(lambda e, i: e.tensor_tensor(score[:], logits_ps, wide(m1[:]), ALU.subtract))
        q.wait("act", t_sub)
        t_exp = q.op("act", lambda e, i: e.activation(score[:], score[:], ACT.Exp))
        q.wait("dve", t_exp)
        V(lambda e, i: e.tensor_reduce(m1[:], score[:], AX.X, ALU.add))
        V(lambda e, i: e.reciprocal(m1[:], m1[:]))
        t_score = V(lambda e, i: e.tensor_tensor(score[:], score[:], wide(m1[:]), ALU.mult))
        q.wait("dve", t_score)
        for t in range(NT):
            q.op("dve", lambda e, i, t=t: e.max(best[:, t, :], score[:, t, :]))
        V(lambda e, i: e.tensor_tensor(sel[:], score[:], wide(best[:, :, TOPK - 1]), ALU.is_gt))
        q.op("dve", lambda e, i: e.tensor_tensor(eq[:], score[:], wide(best[:, :, TOPK - 1]), ALU.is_equal))
        V(lambda e, i: e.tensor_reduce(m1[:], sel[:], AX.X, ALU.add))
        cur, other = eq, a
        for step in (1, 2, 4, 8):
            V(lambda e, i, cur=cur, other=other, step=step: e.tensor_tensor(
                other[:, :, step:], cur[:, :, step:], cur[:, :, :NE - step], ALU.add))
            q.op("dve", lambda e, i, cur=cur, other=other, step=step: e.tensor_copy(other[:, :, :step], cur[:, :, :step]))
            cur, other = other, (b if other is a else a)
        V(lambda e, i: e.tensor_tensor(cur[:], cur[:], wide(m1[:]), ALU.add))
        V(lambda e, i: e.scalar_tensor_tensor(cur[:], cur[:], TOPK + 0.5, eq[:], ALU.is_lt, ALU.mult))
        V(lambda e, i: e.tensor_tensor(sel[:], sel[:], cur[:], ALU.add))
        V(lambda e, i: e.memset(sel_b[:, 0], 0.0))
        counted = V(lambda e, i: e.tensor_copy(sel_b[:, 1:], sel[:]))
        q.op("dve", lambda e, i: e.tensor_scalar(rank[:], sel[:], -4.0 * T, 4.0 * T, ALU.mult, ALU.add))
        q.op("dve", lambda e, i: e.tensor_reduce(m2[:], best[:, :, 0:TOPK], AX.X, ALU.add))
        V(lambda e, i: e.tensor_scalar(m2[:], m2[:], 1e-20, None, ALU.add))
        V(lambda e, i: e.reciprocal(m2[:], m2[:]))
        V(lambda e, i: e.tensor_tensor(score[:], score[:], wide(m2[:]), ALU.mult))
        V(lambda e, i: e.tensor_scalar(score[:], score[:], 0.5, None, ALU.mult))
        for n in range(3, 6):
            V(lambda e, i, n=n: e.tensor_copy(info[:, :, :, n], score[:]))
            if n < 5:
                V(lambda e, i, n=n: e.tensor_tensor(score[:], score[:], info[:, :, :, n], ALU.subtract))
        q.op("dve", lambda e, i: e.tensor_scalar(info[:, :, :, 0], sel[:], 0.0, row_id[:], ALU.mult, ALU.add))
        q.op("dve", lambda e, i: e.tensor_copy(info[:, :, :, 1], wide(tile_id[:])))
        q.op("dve", lambda e, i: e.memset(info[:, :, :, 2], 1.0))
        info_done = q.op("dve", lambda e, i: e.memset(none[:], 0.0))
        q.wait("pe", *w_ready)

        def pool(fn):
            q.wait("pool", q.last("pool")) if q.own["pool"].per.get(q.section) else q.wait_before("pool", "pool idle")
            t = q.op("pool", fn)
            q.release("pool idle", t)
            return t

        def slots_of(n_of):
            for n in range(4):
                q.acquire("dve", ("hot", n))
                q.op("dve", lambda e, i, n=n: e.tensor_tensor(
                    hot[:, n], slots[:], rank_b[:, bass.ds(n_of(i) + n, 1), :].broadcast_to([P, P, NT]), ALU.is_equal))
                done = q.op("dve", lambda e, i, n=n: e.tensor_copy(
                    info_e[:, n], info[:, :, bass.ds(n_of(i) + n, 1), :].rearrange("p t a b -> p t (a b)")))
                yield
                q.wait("pe", done)
                if n == 0:
                    q.acquire("pe", "slot_ps")
                for t in range(NT):
                    done = q.op("pe", lambda e, i, t=t, n=n: e.matmul(
                        slot_ps[:, n, 0:6], hot[:, n, :, t], info_e[:, n, t, :], start=t == 0, stop=t == NT - 1), tick=t == NT - 1)
                q.release(("hot", n), done)
            yield
            q.wait("dve", done)
            q.release("slot_ps", q.op("dve", lambda e, i: e.tensor_tensor(
                got[:, bass.ds(n_of(i), 4), 0:6], slot_ps[:, 0:4, 0:6], none[:], ALU.add)))

        def ffn_turns(first, times, slot_steps=None):
            q.begin(times)
            beside = slot_steps() if slot_steps else iter(())
            xt = lambda buf, k: (lambda i: buf[:, k, bass.ds((i + first) * CH, CH)])
            rights = [(xt(core.xt_hi, k), xt(core.xt_lo, k)) for k in range(HK)]
            halves = []
            for m in range(ISM):
                helper = "dve" if m == ISM - 1 else "pool"
                for n in range(2):
                    bank = (2 * m + n) % 3
                    q.acquire("pe", ("up", bank))
                    at = (2 * m + n) * P
                    done = products(q, up_ps[:, bank, :], [up_hi[:, k, at:at + P] for k in range(HK)],
                                    [up_lo[:, k, at:at + P] for k in range(HK)], rights)
                    q.wait("act", done)
                    q.acquire("act", ("act", m % 2))
                    out, what = ((gate, ACT.Silu), (up_sb, ACT.Copy))[n]
                    read = q.op("act", lambda e, i, out=out, m=m, bank=bank, what=what: e.activation(out[:, m % 2, :], up_ps[:, bank, :], what))
                    q.release(("up", bank), read)
                next(beside, None)
                if m == ISM - 2:
                    next(beside, None)
                queue = pool if helper == "pool" else lambda fn: q.op("dve", fn)
                q.wait(helper, read)
                if helper == "dve":
                    q.acquire("dve", ("act", m % 2))
                t_act = queue(lambda e, i, m=m: e.tensor_tensor(act[:, m % 2, :], gate[:, m % 2, :], up_sb[:, m % 2, :], ALU.mult))
                q.wait("act", t_act)
                q.acquire("act", ("h", m))
                t_hi = q.op("act", lambda e, i, m=m: e.activation(h_hi[:, m, :], act[:, m % 2, :], ACT.Copy))
                q.wait(helper, t_hi)
                halves.append(queue(lambda e, i, m=m: e.tensor_tensor(h_lo[:, m, :], act[:, m % 2, :], as_f32(h_hi[:, m, :]), ALU.subtract)))
                q.release(("act", m % 2), halves[-1])
            for _ in beside:
                pass
            for m in range(ISM):
                q.wait("pe", halves[m])
                for j in range(4):
                    if m == 0:
                        q.acquire("pe", ("down", j))
                    done = products(q, down_ps[:, j, 0:H], [h_hi[:, m, j * P:(j + 1) * P]], [h_lo[:, m, j * P:(j + 1) * P]],
                                    [(dn_hi[:, m, :], dn_lo[:, m, :])], first=m == 0, last=m == ISM - 1)
                q.release(("h", m), done)
            q.wait("act", done)
            for j in range(4):
                q.acquire("act", ("part", j))
                at = part[:, j // 2, (j % 2) * H:(j % 2 + 1) * H]
                t_part = q.op("act", lambda e, i, j=j, at=at: e.activation(at, down_ps[:, j, 0:H], ACT.Copy, scale=0.5))
                q.release(("down", j), t_part)
                q.wait("pool", t_part)
                row = lambda i, j=j: core.x[:, bass.ds((i + first) * 4 + j, 1), :].rearrange("p a h -> p (a h)")
                q.release(("part", j), pool(lambda e, i, at=at, row=row: e.tensor_tensor(row(i), row(i), at, ALU.add)))

        ffn_turns(0, 1)
        q.begin()
        used = q.sections[-2].named
        for engine in ("pe", "act", "dve", "pool"):
            q.wait(engine, *(used[name] for name in used if name[0] in {
                "pe": ("up", "down"), "act": ("act", "h", "part"), "dve": ("act", "h"), "pool": ("act", "h", "part")}[engine]))
        q.wait("pool", used["pool idle"])
        q.wait("pe", counted, ones_done)
        q.op("pe", lambda e, i: e.matmul(rank_ps, ones[:], sel_b[:, 0:NT], start=True, stop=False), tick=False)
        for t in range(NT - 2):
            q.op("pe", lambda e, i, t=t: e.matmul(
                rank_ps[:, t + 2:], ones[:], sel_b[:, t + 1].unsqueeze(1).broadcast_to([P, NT - 2 - t, NE]),
                start=False, stop=False, skip_group_check=True), tick=False)
        t_rank = q.op("pe", lambda e, i: e.matmul(rank_ps, below[:], sel_b[:, 1:], start=False, stop=True))
        q.wait("dve", t_rank, info_done)
        ranked = V(lambda e, i: e.tensor_tensor(rank_b[:].rearrange("p e t -> p t e"), rank[:], rank_ps, ALU.add))
        q.wait("dve", ranked)
        ffn_turns(1, NCH - 1, lambda: slots_of(lambda i: 4 * i))
        q.begin()
        for _ in slots_of(lambda i: NE - 4):
            pass

        q.wait("dve", q.last("dve"))
        q.op("dve", lambda e, i: e.tensor_scalar(s1[:], got[:, :, 1], float(P), float(T), ALU.mult, ALU.add))
        q.op("dve", lambda e, i: e.tensor_scalar(s2[:], got[:, :, 2], -1.0, 1.0, ALU.mult, ALU.add))
        V(lambda e, i: e.tensor_tensor(s1[:], s1[:], got[:, :, 0], ALU.add))
        q.op("dve", lambda e, i: e.tensor_scalar(s2[:], s2[:], row_id[:], None, ALU.mult))
        V(lambda e, i: e.tensor_tensor(routes.rows[:], s1[:], s2[:], ALU.add))
        V(lambda e, i: e.tensor_tensor(s1[:], got[:, :, 3], got[:, :, 4], ALU.add))
        V(lambda e, i: e.tensor_tensor(routes.weight[:], s1[:], got[:, :, 5], ALU.add))
        q.wait("sp", *stores, *core.stores)
        core.stores = []
        q.emit()


def experts_phase(core, routes):
    q, nc, src = core.q, core.nc, core.src
    IK = I0P // P
    with ExitStack() as stack:
        sb, psum = core.rooms(stack)
        turned = psum("turned", [P, 2, BANK])
        gu = psum("gu", [P, 2, BANK])
        turned_h = psum("turned_h", [P, 2, BANK])
        down_ps = psum("down", [P, 2, BANK])
        raw_up, raw_dn = sb("raw_up", [P, 2, HK, 2 * I0]), sb("raw_dn", [P, 2, IK, H])
        up_hi, up_lo = (sb(n, [P, 2, HK, 2 * I0], F32R) for n in ("up_hi", "up_lo"))
        dn_hi, dn_lo = (sb(n, [P, 2, IK, H], F32R) for n in ("dn_hi", "dn_lo"))
        x_raw = sb("x_raw", [P, 2, H])
        x_hi, x_lo = (sb(n, [P, 2, HK, P], F32R) for n in ("x_hi", "x_lo"))
        h_hi, h_lo = (sb(n, [P, 2, IK, P], F32R) for n in ("h_hi", "h_lo"))
        gate, h = sb("gate", [P, 2, I0]), sb("h", [P, 2, I0P])
        out, in_rows, out_rows = sb("out", [P, 2, H]), sb("in_rows", [P, 2, 1], I32), sb("out_rows", [P, 2, 1], I32)
        none = sb("none", [P, 1])

        def rows_of(dst, n_of):
            return q.op("dve", lambda e, i: e.tensor_tensor(dst, routes.rows[:, bass.ds(n_of(i), 1)], none[:], ALU.add))

        def fetch(s, n_of):
            q.acquire("dve", ("fetched", s))
            t = rows_of(in_rows[:, s], n_of)
            q.wait("pool", t)
            q.acquire("pool", ("x_raw", s))
            q.release(("fetched", s), q.op("pool", lambda e, i: e.indirect_dma_start(
                x_raw[:, s], None, core.xn_rows, bass.IndirectOffsetOnAxis(ap=in_rows[:, s], axis=0)), flow=core.gather_out[s]))

        def weights(s, n_of):
            for k in range(HK):
                q.acquire("sp", ("raw up", s, k))
            t_up = q.op("sp", lambda e, i: e.dma_start(raw_up[:, s], src["expert_up"][bass.ds(n_of(i), 1)].rearrange("a p k n -> p (a k) n")),
                        flow=core.loads[2 * s])
            q.acquire("sp", ("raw down", s))
            t_dn = q.op("sp", lambda e, i: e.dma_start(raw_dn[:, s], src["expert_down"][bass.ds(n_of(i), 1)].rearrange("a p k n -> p (a k) n")),
                        flow=core.loads[2 * s + 1])
            q.release(("down loaded", s), t_dn)
            q.wait("act", t_up)
            q.acquire("act", ("up", s))
            t_hi = q.op("act", lambda e, i: e.activation(up_hi[:, s], raw_up[:, s], ACT.Copy))
            for k, engine in enumerate(("pool", "dve")):
                q.wait(engine, t_hi)
                t = q.op(engine, lambda e, i, k=k: e.tensor_tensor(up_lo[:, s, k], raw_up[:, s, k], as_f32(up_hi[:, s, k]), ALU.subtract))
                q.release(("raw up", s, k), t)
                q.release(("up split", s, k), t)

        def down_weights(s):
            q.acquire("act", ("down loaded", s))
            q.acquire("act", ("dn", s))
            q.acquire("dve", ("dn", s))
            t = split(q, "act", "dve", dn_hi[:, s], dn_lo[:, s], raw_dn[:, s], None)
            q.release(("raw down", s), t)
            q.release(("dn split", s), t)

        def tokens(s):
            q.acquire("pe", ("fetched", s))
            q.acquire("pe", ("turned", s))
            for k in range(HK):
                done = q.op("pe", lambda e, i, k=k: e.transpose(turned[:, s, k * P:(k + 1) * P], x_raw[:, s, k * P:(k + 1) * P], core.ident[:]),
                            tick=k == HK - 1)
            q.release(("x_raw", s), done)
            for e in ("act", "dve"):
                q.acquire(e, ("x", s))
            t = split(q, "act", "dve", x_hi[:, s], x_lo[:, s], turned[:, s, 0:HK * P].rearrange("p (a b) -> p a b", a=HK), done)
            q.release(("turned", s), t)
            q.release(("x split", s), t)

        def up(s):
            q.acquire("pe", ("x split", s))
            for k in range(HK):
                q.acquire("pe", ("up split", s, k))
            q.acquire("pe", ("gu", s))
            done = products(q, gu[:, s, 0:2 * I0], [x_hi[:, s, k] for k in range(HK)], [x_lo[:, s, k] for k in range(HK)],
                            [(up_hi[:, s, k], up_lo[:, s, k]) for k in range(HK)])
            q.release(("x", s), done)
            q.release(("up", s), done)
            q.wait("act", done)
            q.acquire("act", ("gate", s))
            t_g = q.op("act", lambda e, i: e.activation(gate[:, s], gu[:, s, 0:I0], ACT.Silu))
            q.wait("dve", t_g)
            q.acquire("dve", ("h", s))
            t_h = q.op("dve", lambda e, i: e.tensor_tensor(h[:, s, 0:I0], gu[:, s, I0:2 * I0], gate[:, s], ALU.mult))
            for name in ("gate", "gu", "h written"):
                q.release((name, s), t_h)

        def turn(s):
            q.acquire("pe", ("h written", s))
            q.acquire("pe", ("turned_h", s))
            for k in range(IK):
                done = q.op("pe", lambda e, i, k=k: e.transpose(turned_h[:, s, k * P:(k + 1) * P], h[:, s, k * P:(k + 1) * P], core.ident[:]),
                            tick=k == IK - 1)
            q.release(("h", s), done)
            for e in ("act", "dve"):
                q.acquire(e, ("ht", s))
            t = split(q, "act", "dve", h_hi[:, s], h_lo[:, s], turned_h[:, s, 0:IK * P].rearrange("p (a b) -> p a b", a=IK), done)
            q.release(("turned_h", s), t)
            q.release(("ht split", s), t)

        def down(s, n_of):
            q.acquire("pe", ("ht split", s))
            q.acquire("pe", ("dn split", s))
            q.acquire("pe", ("down", s))
            done = products(q, down_ps[:, s, 0:H], [h_hi[:, s, k] for k in range(IK)], [h_lo[:, s, k] for k in range(IK)],
                            [(dn_hi[:, s, k], dn_lo[:, s, k]) for k in range(IK)])
            q.release(("ht", s), done)
            q.release(("dn", s), done)
            q.wait("dve", done)
            q.acquire("dve", ("out", s))
            t_o = q.op("dve", lambda e, i: e.tensor_scalar(out[:, s], down_ps[:, s, 0:H], routes.weight[:, bass.ds(n_of(i), 1)], None, ALU.mult))
            q.release(("down", s), t_o)
            return rows_of(out_rows[:, s], n_of)

        def add(s, t_o):
            q.wait("pool", t_o)
            q.acquire("pool", "added")
            added = q.op("pool", lambda e, i: e.indirect_dma_start(
                core.y_rows, bass.IndirectOffsetOnAxis(ap=out_rows[:, s], axis=0), out[:, s], None, compute_op=ALU.add),
                flow=core.add_out[s])
            q.release(("out", s), added)
            q.release("added", added)

        def step(s, n_of, first=False, weigh=True, fetching=True, more=True):
            if fetching:
                fetch(s, lambda i: n_of(i) + 2)
            up(s)
            if not first:
                t_o = down(1 - s, lambda i: n_of(i) - 1)
            if weigh:
                weights(s, lambda i: n_of(i) + 2)
            if more:
                tokens(1 - s)
            turn(s)
            if not first:
                add(1 - s, t_o)
                if more:
                    down_weights(1 - s)

        q.begin()
        q.op("dve", lambda e, i: e.memset(h[:], 0.0))
        q.op("dve", lambda e, i: e.memset(none[:], 0.0))
        q.wait("dve", q.last("dve"))
        for s in range(2):
            fetch(s, lambda i, s=s: s)
        for s in range(2):
            weights(s, lambda i, s=s: s)
        tokens(0)
        for s in range(2):
            down_weights(s)
        step(0, lambda i: 0, first=True)
        q.meet()
        q.begin((NE - 4) // 2)
        step(1, lambda i: 2 * i + 1)
        step(0, lambda i: 2 * i + 2)
        q.begin()
        step(1, lambda i: NE - 3)
        step(0, lambda i: NE - 2, weigh=False, fetching=False)
        step(1, lambda i: NE - 1, weigh=False, fetching=False, more=False)
        add(1, down(1, lambda i: NE - 1))
        q.acquire("pool", "added")
        q.emit()


def ffn0_block(core):
    with ExitStack() as stack:
        routes = Routes(core, stack)
        route_and_share(core, routes)
        experts_phase(core, routes)


def program(nc, src, out):
    with ExitStack() as stack:
        q = Queues(nc, stack)
        core = Core(nc, stack, q, src)
        ffn1 = lambda **kw: ffn_phase(core, src["up1"], src["down1"], I1, (src["gs1"], src["us1"], src["ds1"]), **kw)
        start_phase(core)
        ffn0_block(core)
        attention0_phase(core, add_y=True)
        ffn0_block(core)
        ffn1(add_y=True)
        attention1_phase(core)
        ffn1(result=out)



def _tables():
    fraction = np.linspace(0.0, 1.0, DH // 4, dtype=np.float32)
    af = np.power(np.float32(1.0 / 1024.0), fraction).astype(np.float32)
    theta = (np.arange(T, dtype=np.float32)[None, :] * af[:, None]).astype(np.float32)
    cos, sin = np.cos(theta).astype(np.float32), np.sin(theta).astype(np.float32)
    bf = mybir.dt.np(BF16)
    r = np.arange(P)
    return {
        "rope": np.concatenate([cos, cos, -sin, sin]),
        "ident": np.eye(P, dtype=np.float32),
        "ident_b": np.eye(P, dtype=bf),
        "mask_b": np.where(r[None, :] > r[:, None], NEG, 0.0).astype(bf),
        "below_b": (r[:, None] < r[None, :]).astype(bf),
        "slots_b": np.broadcast_to(r[None, :, None], (P, P, NT)).astype(bf),
        "row_id": r[:, None].astype(np.float32),
        "tile_id": np.broadcast_to(np.arange(NT)[None, :] - NT, (P, NT)).astype(np.float32),
    }


def _wide(w):
    return w.reshape(-1, P, w.shape[-1]).transpose(1, 0, 2)


def _pad(w, rows, width):
    out = np.zeros((*w.shape[:-2], rows, width), w.dtype)
    out[..., :w.shape[-2], :w.shape[-1]] = w
    return out


def _layouts(i):
    a = {k: np.asarray(v) for k, v in i.items()}
    out = {"x": a["L0_attn_x"][0]}
    out["gate0"] = _wide(a["L0_ffn_gate_w"].T)
    up = np.concatenate([a["L0_ffn_w_gate"], a["L0_ffn_w_up"]], axis=-1)
    out["expert_up"] = up.reshape(NE, HK, P, 2 * I0).transpose(0, 2, 1, 3)
    out["expert_down"] = _pad(a["L0_ffn_w_down"], I0P, H).reshape(NE, I0P // P, P, H).transpose(0, 2, 1, 3)
    g, u = _pad(a["L0_ffn_sw_gate"], H, ISM * P), _pad(a["L0_ffn_sw_up"], H, ISM * P)
    out["shared_up"] = _wide(np.stack([g.reshape(H, ISM, P), u.reshape(H, ISM, P)], axis=2).reshape(H, -1))
    out["shared_down"] = _wide(_pad(a["L0_ffn_sw_down"], ISM * P, H))
    out["ws"], out["wa"] = (_wide(np.tile(a[n], (1, P // R0))) for n in ("L0_attn_Ws", "L0_attn_Wa"))
    out["wo0"] = _wide(a["L0_attn_Wo"].T)
    out["bo"] = a["L0_attn_bo"][None, :]
    turn = np.concatenate([np.arange(0, 32), np.arange(64, 96), np.arange(32, 64), np.arange(96, 128)])
    qk = np.stack([a[n].reshape(NH, DH, H)[:, turn, :] for n in ("L1_attn_Wq", "L1_attn_Wk")], axis=1)
    out["qk"] = qk.reshape(NH, 2, DH, HK, P).transpose(0, 4, 3, 1, 2)
    out["qk"] = np.concatenate([out["qk"], np.zeros_like(out["qk"][:2])])
    out["wv"] = a["L1_attn_Wv"].reshape(NH // 2, 2 * DH, HK, P).transpose(0, 3, 2, 1)
    out["wv"] = np.concatenate([out["wv"], np.zeros_like(out["wv"][:1])])
    out["wo1"] = a["L1_attn_Wo"].reshape(H, NH, DH).transpose(1, 2, 0)
    full = (I1 // P) * P
    g, u = a["L1_ffn_gate_w"].T, a["L1_ffn_up_w"].T
    both = np.stack([g[:, :full].reshape(H, -1, P), u[:, :full].reshape(H, -1, P)], axis=2).reshape(H, -1)
    out["up1"] = _wide(np.concatenate([both, g[:, full:], u[:, full:]], axis=1))
    out["down1"] = _wide(_pad(a["L1_ffn_down_w"].T, I1M * P, H))
    gs, us = (_pad(a[n].reshape(1, I1), 1, I1M * P).reshape(I1M, P).T for n in ("L1_ffn_gate_s", "L1_ffn_up_s"))
    us = us.copy()
    us[P // 2:, -1] = us[:P // 2, -1]
    out["gs1"], out["us1"], out["ds1"] = gs, us, a["L1_ffn_down_s"][None, :]
    return out


def kernel(**inputs):
    from concourse import bacc
    from concourse.bass_utils import run_bass_kernel_spmd

    nc = bacc.Bacc("TRN2", target_bir_lowering=False, num_devices=1)
    arrays = {n: np.ascontiguousarray(a) for n, a in {**_layouts(inputs), **_tables()}.items()}
    src = {n: nc.dram_tensor(n, a.shape, mybir.dt.from_np(a.dtype), kind="ExternalInput").ap() for n, a in arrays.items()}
    out = nc.dram_tensor("out", (T, H), F32, kind="ExternalOutput").ap()
    program(nc, src, out)
    r = run_bass_kernel_spmd(nc, [arrays], core_ids=[0])
    return r.results[0]["out"].reshape(1, T, H)
```
